# Optimizing a Trainium2 kernel written in Bass

```python
import numpy as np
import jax
import jax.numpy as jnp

def _softmax(x, axis=-1):
    return jax.nn.softmax(x, axis=axis)

def _gelu(x):
    return jax.nn.gelu(x, approximate=True)

def _silu(x):
    return jax.nn.silu(x)

def _sigmoid(x):
    return jax.nn.sigmoid(x)

def _layernorm(x, axis=-1, eps=1e-05):
    m = jnp.mean(x, axis=axis, keepdims=True)
    v = jnp.var(x, axis=axis, keepdims=True)
    return (x - m) / jnp.sqrt(v + eps)

def _scatter_add(tgt, idx, src, axis=0):
    return tgt.at[idx].add(src)

def _segment_sum(src, seg, n):
    return jax.ops.segment_sum(src, seg, n)
kernel_name = 'mk_seq_preln_d2_jaxref_r4_e0a9cc'

def setup_inputs(seed: int=0):
    np.random.seed(seed)
    _w = jnp.asarray

    def _L0_attn_setup():
        import jax, jax.numpy as jnp
        import numpy as np
        EMBED_DIM = 256
        NUM_HEADS = 16
        HEAD_DIM = EMBED_DIM // NUM_HEADS
        WINDOW = 128
        SEQ = 512
        BATCH = 2
        key = jax.random.key(seed)
        ks = jax.random.split(key, 5)
        s = 0.02
        x = jax.random.normal(ks[0], (BATCH, SEQ, EMBED_DIM), dtype=jnp.float32)
        Wq = jax.random.normal(ks[1], (EMBED_DIM, EMBED_DIM), dtype=jnp.float32) * s
        Wk = jax.random.normal(ks[2], (EMBED_DIM, EMBED_DIM), dtype=jnp.float32) * s
        Wv = jax.random.normal(ks[3], (EMBED_DIM, EMBED_DIM), dtype=jnp.float32) * s
        Wo = jax.random.normal(ks[4], (EMBED_DIM, EMBED_DIM), dtype=jnp.float32) * s
        return {'x': x, 'Wq': Wq, 'Wk': Wk, 'Wv': Wv, 'Wo': Wo}
    _L0_attn_in = _L0_attn_setup()

    def _L0_ffn_setup():
        import jax, jax.numpy as jnp
        import numpy as np
        B, S, H, I, E, TOP_K = (1, 512, 256, 512, 8, 2)
        key = jax.random.key(seed)
        ks = jax.random.split(key, 6)
        x = jax.random.normal(ks[0], (B, S, H), dtype=jnp.float32)
        Wr = jax.random.normal(ks[1], (H, E), dtype=jnp.float32) * (1.0 / np.sqrt(H))
        br = jnp.zeros((E,), dtype=jnp.float32)
        W1 = jax.random.normal(ks[2], (E, H, I), dtype=jnp.float32) * (1.0 / np.sqrt(H))
        W3 = jax.random.normal(ks[3], (E, H, I), dtype=jnp.float32) * (1.0 / np.sqrt(H))
        W2 = jax.random.normal(ks[4], (E, I, H), dtype=jnp.float32) * (1.0 / np.sqrt(I))
        return {'x': x, 'Wr': Wr, 'br': br, 'W1': W1, 'W3': W3, 'W2': W2}
    _L0_ffn_in = _L0_ffn_setup()

    def _L1_attn_setup():
        import jax, jax.numpy as jnp
        import numpy as np
        HEADS = 16
        THETA = 10000.0

        def _rope(x):
            b, n, d = x.shape
            half = d // 2
            inv_freq = 1.0 / THETA ** (jnp.arange(0, d, 2, dtype=jnp.float32) / d)
            ang = jnp.arange(n, dtype=jnp.float32)[:, None] * inv_freq
            cos, sin = (jnp.cos(ang), jnp.sin(ang))
            xp = x.reshape(b, n, half, 2)
            x1, x2 = (xp[..., 0], xp[..., 1])
            out = jnp.stack([x1 * cos - x2 * sin, x2 * cos + x1 * sin], axis=-1)
            return out.reshape(b, n, d)
        key = jax.random.key(seed)
        ks = jax.random.split(key, 8)
        B, N, C = (8, 512, 256)
        s = C ** (-0.5)
        return {'x': jax.random.normal(ks[0], (B, N, C), jnp.float32), 'Wq': jax.random.normal(ks[1], (C, C), jnp.float32) * s, 'bq': jax.random.normal(ks[2], (C,), jnp.float32) * 0.01, 'Wk': jax.random.normal(ks[3], (C, C), jnp.float32) * s, 'bk': jax.random.normal(ks[4], (C,), jnp.float32) * 0.01, 'Wv': jax.random.normal(ks[5], (C, C), jnp.float32) * s, 'bv': jax.random.normal(ks[6], (C,), jnp.float32) * 0.01, 'gamma': jnp.ones((C,), jnp.float32), 'beta': jnp.zeros((C,), jnp.float32)}
    _L1_attn_in = _L1_attn_setup()

    def _L1_ffn_setup():
        import jax, jax.numpy as jnp
        import numpy as np
        NUM_EXPERTS = 8
        CAPACITY = 160
        key = jax.random.key(seed)
        ks = jax.random.split(key, 5)
        D, E, F = (256, NUM_EXPERTS, 1024)
        inputs = jax.random.normal(ks[0], (2, 512, D), dtype=jnp.float32)
        gate_w = jax.random.normal(ks[1], (D, E), dtype=jnp.float32) * 0.02
        gate_b = jnp.zeros((E,), dtype=jnp.float32)
        w1 = jax.random.normal(ks[2], (E, D, F), dtype=jnp.float32) * 0.02
        b1 = jnp.zeros((E, F), dtype=jnp.float32)
        w2 = jax.random.normal(ks[3], (E, F, D), dtype=jnp.float32) * 0.02
        b2 = jnp.zeros((E, D), dtype=jnp.float32)
        return {'inputs': inputs, 'gate_w': gate_w, 'gate_b': gate_b, 'w1': w1, 'b1': b1, 'w2': w2, 'b2': b2}
    _L1_ffn_in = _L1_ffn_setup()
    _d = {'L0_attn_x': _L0_attn_in['x'], 'L0_attn_Wq': _L0_attn_in['Wq'], 'L0_attn_Wk': _L0_attn_in['Wk'], 'L0_attn_Wv': _L0_attn_in['Wv'], 'L0_attn_Wo': _L0_attn_in['Wo'], 'L0_ffn_Wr': _L0_ffn_in['Wr'], 'L0_ffn_br': _L0_ffn_in['br'], 'L0_ffn_W1': _L0_ffn_in['W1'], 'L0_ffn_W3': _L0_ffn_in['W3'], 'L0_ffn_W2': _L0_ffn_in['W2'], 'L1_attn_Wq': _L1_attn_in['Wq'], 'L1_attn_bq': _L1_attn_in['bq'], 'L1_attn_Wk': _L1_attn_in['Wk'], 'L1_attn_bk': _L1_attn_in['bk'], 'L1_attn_Wv': _L1_attn_in['Wv'], 'L1_attn_bv': _L1_attn_in['bv'], 'L1_attn_gamma': _L1_attn_in['gamma'], 'L1_attn_beta': _L1_attn_in['beta'], 'L1_ffn_gate_w': _L1_ffn_in['gate_w'], 'L1_ffn_gate_b': _L1_ffn_in['gate_b'], 'L1_ffn_w1': _L1_ffn_in['w1'], 'L1_ffn_b1': _L1_ffn_in['b1'], 'L1_ffn_w2': _L1_ffn_in['w2'], 'L1_ffn_b2': _L1_ffn_in['b2']}
    _x0 = _d['L0_attn_x']
    _d['L0_attn_x'] = jax.random.normal(jax.random.fold_in(jax.random.key(seed), 1), (2, 2048, 256), dtype=_x0.dtype)
    del _x0
    return _d

def reference(L0_attn_x, L0_attn_Wq, L0_attn_Wk, L0_attn_Wv, L0_attn_Wo, L0_ffn_Wr, L0_ffn_br, L0_ffn_W1, L0_ffn_W3, L0_ffn_W2, L1_attn_Wq, L1_attn_bq, L1_attn_Wk, L1_attn_bk, L1_attn_Wv, L1_attn_bv, L1_attn_gamma, L1_attn_beta, L1_ffn_gate_w, L1_ffn_gate_b, L1_ffn_w1, L1_ffn_b1, L1_ffn_w2, L1_ffn_b2):

    def _L0_attn_ref(x, Wq, Wk, Wv, Wo):
        import jax, jax.numpy as jnp
        import numpy as np
        EMBED_DIM = 256
        NUM_HEADS = 16
        HEAD_DIM = EMBED_DIM // NUM_HEADS
        WINDOW = 128
        SEQ = 512
        BATCH = 2
        b, s, _ = x.shape
        scale = 1.0 / np.sqrt(HEAD_DIM)
        q = (x @ Wq.T).reshape(b, s, NUM_HEADS, HEAD_DIM)
        k = (x @ Wk.T).reshape(b, s, NUM_HEADS, HEAD_DIM)
        v = (x @ Wv.T).reshape(b, s, NUM_HEADS, HEAD_DIM)
        attn = jnp.einsum('bqhd,bkhd->bhqk', q, k) * scale
        i = jnp.arange(s)[:, None]
        j = jnp.arange(s)[None, :]
        allowed = (j <= i) & (j > i - WINDOW)
        attn = jnp.where(allowed, attn, -jnp.inf)
        attn = jax.nn.softmax(attn.astype(jnp.float32), axis=-1).astype(q.dtype)
        out = jnp.einsum('bhqk,bkhd->bqhd', attn, v).reshape(b, s, EMBED_DIM)
        return out @ Wo.T

    def _L0_ffn_ref(x, Wr, br, W1, W3, W2):
        import jax, jax.numpy as jnp
        import numpy as np
        B, S, H, I, E, TOP_K = (1, 512, 256, 512, 8, 2)
        logits = jnp.einsum('bsh,he->bse', x, Wr) + br
        routing_weights, expert_indices = jax.lax.top_k(logits, TOP_K)
        routing_weights = jax.nn.softmax(routing_weights, axis=-1)
        c = jnp.sum(jax.nn.one_hot(expert_indices, E, dtype=x.dtype) * routing_weights[..., None], axis=-2)
        gate = jnp.einsum('bsh,ehi->besi', x, W1)
        up = jnp.einsum('bsh,ehi->besi', x, W3)
        h = jax.nn.silu(gate) * up
        y = jnp.einsum('besi,eih->besh', h, W2)
        out = jnp.einsum('bse,besh->bsh', c, y)
        return out

    def _L1_attn_ref(x, Wq, bq, Wk, bk, Wv, bv, gamma, beta):
        import jax, jax.numpy as jnp
        import numpy as np
        HEADS = 16
        THETA = 10000.0

        def _rope(x):
            b, n, d = x.shape
            half = d // 2
            inv_freq = 1.0 / THETA ** (jnp.arange(0, d, 2, dtype=jnp.float32) / d)
            ang = jnp.arange(n, dtype=jnp.float32)[:, None] * inv_freq
            cos, sin = (jnp.cos(ang), jnp.sin(ang))
            xp = x.reshape(b, n, half, 2)
            x1, x2 = (xp[..., 0], xp[..., 1])
            out = jnp.stack([x1 * cos - x2 * sin, x2 * cos + x1 * sin], axis=-1)
            return out.reshape(b, n, d)
        b, n, c = x.shape
        h = HEADS
        d = c // h
        gelu = lambda t: jax.nn.gelu(t, approximate=False)
        q = gelu(x @ Wq.T + bq) + 0.21
        k = gelu(x @ Wk.T + bk) + 0.21
        v = x @ Wv.T + bv
        q_r = _rope(q)
        k_r = _rope(k)
        split = lambda t: t.reshape(b, n, h, d).transpose(0, 2, 1, 3)
        qh, kh, vh, qrh, krh = (split(q), split(k), split(v), split(q_r), split(k_r))
        z = 1.0 / (jnp.einsum('bhnd,bhd->bhn', qh, kh.mean(axis=2)) + 1e-06)
        scale = n ** (-0.5)
        kv = jnp.einsum('bhnd,bhne->bhde', krh * scale, vh * scale)
        out = jnp.einsum('bhnd,bhde->bhne', qrh, kv) * z[..., None]
        out = out.transpose(0, 2, 1, 3).reshape(b, n, c)
        res = out + x
        mu = res.mean(-1, keepdims=True)
        var = res.var(-1, keepdims=True)
        return (res - mu) / jnp.sqrt(var + 1e-12) * gamma + beta

    def _L1_ffn_ref(inputs, gate_w, gate_b, w1, b1, w2, b2):
        import jax, jax.numpy as jnp
        import numpy as np
        NUM_EXPERTS = 8
        CAPACITY = 160
        D = inputs.shape[-1]
        tokens = inputs.reshape(-1, D)
        logits = tokens @ gate_w + gate_b
        probs = jax.nn.softmax(logits, axis=-1)
        expert_idx = jnp.argmax(probs, axis=-1)
        mask1 = jax.nn.one_hot(expert_idx, NUM_EXPERTS, dtype=jnp.float32)
        pos = jnp.sum(jnp.cumsum(mask1, axis=0) * mask1, axis=-1) - 1.0
        pos = pos.astype(jnp.int32)
        keep = (pos < CAPACITY).astype(jnp.float32)
        gate_prob = jnp.sum(probs * mask1, axis=-1)
        pos_oh = jax.nn.one_hot(pos, CAPACITY, dtype=jnp.float32)
        sec_mask = mask1[:, :, None] * pos_oh[:, None, :] * keep[:, None, None]
        combine_weights = sec_mask * gate_prob[:, None, None]
        dispatch = jnp.einsum('nec,nd->ecd', sec_mask, tokens)
        h = jax.nn.gelu(jnp.einsum('ecd,edf->ecf', dispatch, w1) + b1[:, None, :])
        expert_out = jnp.einsum('ecf,efd->ecd', h, w2) + b2[:, None, :]
        out = jnp.einsum('nec,ecd->nd', combine_weights, expert_out)
        return out.reshape(inputs.shape)
    x = L0_attn_x
    x = x + _L0_attn_ref(_layernorm(x, axis=-1), L0_attn_Wq, L0_attn_Wk, L0_attn_Wv, L0_attn_Wo)
    x = x + _L0_ffn_ref(_layernorm(x, axis=-1), L0_ffn_Wr, L0_ffn_br, L0_ffn_W1, L0_ffn_W3, L0_ffn_W2)
    x = x + _L1_attn_ref(_layernorm(x, axis=-1), L1_attn_Wq, L1_attn_bq, L1_attn_Wk, L1_attn_bk, L1_attn_Wv, L1_attn_bv, L1_attn_gamma, L1_attn_beta)
    x = x + _L1_ffn_ref(_layernorm(x, axis=-1), L1_ffn_gate_w, L1_ffn_gate_b, L1_ffn_w1, L1_ffn_b1, L1_ffn_w2, L1_ffn_b2)
    return x

_drawn_inputs = setup_inputs


def setup_inputs(seed=0):
    import zlib

    import numpy as np

    out = dict(_drawn_inputs(seed))
    spreads = {'L0_ffn_br': (0.0, 0.1),
     'L1_attn_gamma': (1.0, 0.2),
     'L1_attn_beta': (0.0, 0.1),
     'L1_ffn_gate_b': (0.0, 0.8),
     'L1_ffn_b1': (0.0, 0.8),
     'L1_ffn_b2': (0.0, 0.8)}
    factors = {'L0_attn_Wq': 4.971,
     'L0_attn_Wk': 5.744,
     'L1_attn_Wq': 8.0,
     'L1_attn_bq': 8.0,
     'L1_attn_Wk': 7.463,
     'L1_attn_bk': 8.0,
     'L1_attn_Wv': 5.03,
     'L1_attn_bv': 8.0,
     'L1_ffn_gate_w': 7.62,
     'L1_ffn_w1': 8.0,
     'L1_ffn_w2': 8.0}
    for name, (base, spread) in spreads.items():
        noise = np.random.default_rng([zlib.crc32(name.encode()), seed]).standard_normal(out[name].shape)
        drawn = base * np.exp(spread * noise) if base else spread * noise
        out[name] = jnp.asarray(drawn.astype(out[name].dtype))
    for name, factor in factors.items():
        out[name] = (out[name] * factor).astype(out[name].dtype)
    return out
```

```python
from contextlib import ExitStack

import concourse.bass as bass
from concourse import mybir

F32 = mybir.dt.float32
I32 = mybir.dt.int32
ALU = mybir.AluOpType
ACT = mybir.ActivationFunctionType
AX_X = mybir.AxisListType.X

P = 128
BATCH, SEQ, D = 2, 2048, 256
T = BATCH * SEQ // P
TB = SEQ // P
KD = D // P
HEADS, HD = 16, 16
HB = P // HD
WINDOW = 128
E = 8
F0 = 512
K0 = F0 // P
NT0 = 2 * T + E
F1 = 1024
K1 = F1 // P
CAP = 160
CR = CAP // 2
NS1 = E * CAP
U = 4
BIG = 1e30

C_ID = 0
C_TRI = C_ID + P
C_ONE = C_TRI + P
C_MEAN = C_ONE + P
C_BD = C_MEAN + P
C_HM = C_BD + P
C_W8 = C_HM + HB
C_J = C_W8 + E * T
C_ECAP = C_J + NT0
C_TRASH = C_ECAP + E * T
C_MN = C_TRASH + T
C_MT = C_MN + 2 * P
C_END = C_MT + 2 * 2 * P


def mixed_model_kernel(nc, x, wq, wk, wv, wo, wr, br, w1, w3, w2, aq, av, ab, gamma_beta,
                       gate_w, gate_b, v1, b1, v2, b2, consts, cos, sin, out):
    ctx = ExitStack()
    with ctx:
        def sb(name, shape, dt=F32):
            return ctx.enter_context(nc.sbuf_tensor(name, shape, dt))

        def sem(name):
            return ctx.enter_context(nc.semaphore(name))

        X = sb("X", [P, T, D])
        XN = sb("XN", [P, T, D])
        arena = sb("arena", [P, 3, 2 * T * P])
        cst = sb("cst", [P, C_END])
        prob = arena[:, 2, :].rearrange("p (b h k) -> p b h k", b=2, h=HEADS)
        WORK = 6912
        work = sb("work", [P, WORK])
        xn_flat = XN[:, :, :].rearrange("p t n -> p (t n)")

        def cut(at, n, of=work, size=WORK):
            assert at[0] + n <= size
            at[0] += n
            return of[:, at[0] - n:at[0]]
        a = [0]
        q_pad = cut(a, 2 * HEADS * P, xn_flat, T * D).rearrange("p (b h q) -> p b h q", b=2, h=HEADS)
        v_pad = cut(a, U * HEADS * 32, xn_flat, T * D).rearrange("p (s h c) -> p s h c", s=U, h=HEADS)
        k_t = cut(a, KD * U * P, xn_flat, T * D).rearrange("p (g s n) -> p g s n", g=KD, s=U)
        p_t = cut(a, 2 * 4 * P, xn_flat, T * D).rearrange("p (b n) -> p b n", b=2)
        a = [0]
        xnb = cut(a, 2 * D).rearrange("p (b n) -> p b n", b=2)
        xn_t = cut(a, KD * P).rearrange("p (k n) -> p k n", k=KD)
        b = [a[0]]
        c = [a[0]]
        wqkvo = cut(a, 4 * KD * D).rearrange("p (w k n) -> p w k n", w=4, k=KD)
        q_t = cut(a, KD * P).rearrange("p (k n) -> p k n", k=KD)
        rden_x = cut(a, D).rearrange("p (h c) -> p h c", h=HEADS)
        rden_t = cut(a, D)
        o_t = cut(a, D).rearrange("p (k n) -> p k n", k=KD)
        mask0 = cut(a, 2 * P)
        den = sb("den", [P, 2, HEADS])
        nmax = sb("nmax", [P, 2, HEADS])
        rden = sb("rden", [P, HEADS])[:, :]
        w1s = arena[:, 0, :].rearrange("p (e k n) -> p e k n", e=E, k=KD)
        w3s = arena[:, 1, :].rearrange("p (e k n) -> p e k n", e=E, k=KD)
        w2s = arena[:, 2, :].rearrange("p (e k n) -> p e k n", e=E, k=K0)
        xg = cut(b, 4 * D).rearrange("p (b n) -> p b n", b=4)
        xg_t = cut(b, 2 * D).rearrange("p (b k n) -> p b k n", b=2, k=KD)
        gact = cut(b, 2 * F0).rearrange("p (b n) -> p b n", b=2)
        hid = cut(b, 2 * F0).rearrange("p (b n) -> p b n", b=2)
        hid_t = cut(b, 2 * F0).rearrange("p (b k n) -> p b k n", b=2, k=K0)
        yo = cut(b, 2 * D).rearrange("p (b n) -> p b n", b=2)
        yg = XN[:, 0:8, :]
        zrow = sb("zrow", [P, D])[:, :]
        logit = sb("logit", [P, E, T])[:, :, :]
        oh = sb("oh", [P, 2, E, T])
        b = [2 * D + KD * P]
        rt = cut(b, 4 * E * T).rearrange("p (b e t) -> p b e t", b=4, e=E)
        small = sb("small", [P, 16, T])
        ecol = sb("ecol", [P, 4, E])
        ecol_i = sb("ecol_i", [P, 2, E], I32)
        slot_i = sb("slot_i", [P, 2, T], I32)
        slot2_i = sb("slot2_i", [P, 2, T], I32)
        etile = cut(b, NT0 * E).rearrange("p (j e) -> p j e", j=NT0)
        etile_s = sb("etile_s", [P, NT0])[:, :]
        etile_i = sb("etile_i", [P, NT0], I32)[:, :]
        cw = sb("cw", [P, 2, T])
        st = sb("st", [P, T, 6])
        mean = sb("mean", [P, T])[:, :]
        rstd = sb("rstd", [P, T])[:, :]
        lnw = sb("lnw", [P, 4, T])
        qs = arena[:, 0, :].rearrange("p (t n) -> p t n", t=T)
        qr_t = arena[:, 1, :].rearrange("p (t k n) -> p t k n", t=T, k=KD)
        rope_c = arena[:, 2, 0:TB * P].rearrange("p (t n) -> p t n", t=TB)
        rope_s = arena[:, 2, TB * P:2 * TB * P].rearrange("p (t n) -> p t n", t=TB)
        wqk2 = arena[:, 2, 4096:5120].rearrange("p (k n) -> p k n", k=KD)
        wv2 = arena[:, 2, 5120:5632].rearrange("p (k n) -> p k n", k=KD)
        bqkv = arena[:, 2, 5632:6400]
        gab = arena[:, 2, 6400:6912]
        xc_t = cut(c, 2 * D).rearrange("p (b k n) -> p b k n", b=2, k=KD)
        qkb = cut(c, 2 * D)
        qk = cut(c, 4 * D).rearrange("p (b s n) -> p b s n", b=2, s=2)
        vb = cut(c, 2 * D).rearrange("p (b n) -> p b n", b=2)
        ra = cut(c, 2 * D)
        rb = cut(c, 2 * D)
        qkr = cut(c, 4 * D).rearrange("p (b s n) -> p b s n", b=2, s=2)
        kv_bd = cut(c, KD * P).rearrange("p (k n) -> p k n", k=KD)
        kmean = cut(c, D)
        zt = cut(c, D)
        zd = sb("zd", [P, 2, HEADS])
        qr_st = cut(c, 2 * D).rearrange("p (b k n) -> p b k n", b=2, k=KD)
        v1s = arena[:, 2, 0:4096].rearrange("p (b k n) -> p b k n", b=2, k=KD)
        v2s = arena[:, 2, 4096:8192].rearrange("p (b k n) -> p b k n", b=2, k=K1)
        d = [2 * D + KD * P + 2 * D + 4 * E * T]
        xe = XN[0:CR, 0:4, :].rearrange("p (b r) n -> p b r n", b=2)
        xe_t = cut(d, 2 * KD * CAP).rearrange("p (b k n) -> p b k n", b=2, k=KD)
        he_t = arena[:, 1, 0:2 * K1 * CAP].rearrange("p (b k n) -> p b k n", b=2, k=K1)
        ye_t = arena[:, 1, 4096:4096 + KD * CAP].rearrange("p (k n) -> p k n", k=KD)
        ye = arena[0:CR, 1, 5120:5120 + 4 * D].rearrange("p (b r n) -> p b r n", b=2, r=2)
        b1s = sb("b1s", [P, E, K1])
        b2s = sb("b2s", [P, E, KD])
        wrs = sb("wrs", [P, 2, KD, P])
        rbias = sb("rbias", [P, 2, E])

        ps = ctx.enter_context(nc.psum_tensor("ps", [P, 8, 512], F32))
        rows1 = nc.dram_tensor("slots1", [NT0 * P, D], F32)
        outs1 = nc.dram_tensor("outs1", [NT0 * P, D], F32)
        rows2 = nc.dram_tensor("slots2", [NS1 + T * P, D], F32)
        outs2 = nc.dram_tensor("outs2", [NS1, D], F32)

        ident = cst[:, C_ID:C_ID + P]
        tri = cst[:, C_TRI:C_TRI + P]
        ones = cst[:, C_ONE:C_ONE + P]
        meanm = cst[:, C_MEAN:C_MEAN + P]
        bdm = cst[:, C_BD:C_BD + P]
        hmask = cst[:, C_HM:C_HM + HB]
        w8 = cst[:, C_W8:C_W8 + E * T].rearrange("p (e t) -> p e t", e=E)
        jfirst = cst[:, C_J:C_J + NT0]
        ecap = cst[:, C_ECAP:C_ECAP + E * T].rearrange("p (e t) -> p e t", e=E)
        trash = cst[:, C_TRASH:C_TRASH + T]
        mask_n = cst[:, C_MN:C_MN + 2 * P]
        
        def sems(*names):
            return [sem(n) for n in names]
        (cst_in, x_in, aw_in, rw_in, w13_in, w2_in, zr_set, zr_out, zpad_set) = sems(
            "cst_in", "x_in", "aw_in", "rw_in", "w13_in", "w2_in", "zr_set", "zr_out", "zpad_set")
        ln_st = [sem(f"ln{i}_stats") for i in range(5)]
        ln_fin, ln_std, ln_rstd = sems("ln_fin", "ln_std", "ln_rstd")
        (xn_rdy, xt_done, xnt_rdy, qkv_done, q_evac, k_evac, vpad_rdy, qpad_rdy, s_done, ttr_done,
         p_rdy, pt_done, ptev_a, ptev_d, pv_done, rden_rdy, dt_done, dt_evac, ot_rdy, wo_done,
         x1_rdy, mask_rdy, rden_a) = sems(
            "a_xn_rdy", "a_xt_done", "a_xnt_rdy", "a_qkv_done", "a_q_evac", "a_k_evac",
            "a_vpad_rdy", "a_qpad_rdy", "a_s_done", "a_ttr_done", "a_p_rdy", "a_pt_done",
            "a_ptev_a", "a_ptev_d", "a_pv_done", "a_rden_rdy", "a_dt_done", "a_dt_evac",
            "a_ot_rdy", "a_wo_done", "x1_rdy", "a_mask_rdy", "a_rden")
        (b_xn, b_xt, b_xte, b_lg, b_l, r_oh, r_rank, r_dve, slot_rdy, disp, e_rdy, cw_e,
         xg_in0, xg_in1, xg_in2, xg_in3, xgt, xgte, gu_done, g_act, h_rdy, ht_done, hte, dn_done,
         y_rdy, y_out0, y_out1) = sems(
            "b_xn", "b_xt", "b_xte", "b_lg", "b_l", "r_oh", "r_rank", "r_dve", "slot_rdy", "disp",
            "e_rdy", "cw_e", "xg_in0", "xg_in1", "xg_in2", "xg_in3", "xgt", "xgte",
            "gu_done", "g_act", "h_rdy", "ht_done", "hte", "dn_done", "y_rdy", "y_out0", "y_out1")

        xg_in = [xg_in0, xg_in1, xg_in2, xg_in3]
        y_out = [y_out0, y_out1]
        yg_in = [sem(f"yg_in{i}") for i in range(4)]
        yg_acc = sem("yg_acc")
        (c_in, c_xn, c_xt, c_xte, c_qk, c_v, c_qkb, c_gelu, c_qk21, c_ra, c_rb, c_rope, c_vb,
         c_qrt, c_qrte, c_kvm, c_kve, c_zt, c_zd, c_z, c_o, c_oz, c_res, c_n1, c_n2, c_x3) = sems(
            "c_in", "c_xn", "c_xt", "c_xte", "c_qk", "c_v", "c_qkb", "c_gelu", "c_qk21", "c_ra",
            "c_rb", "c_rope", "c_vb", "c_qrt", "c_qrte", "c_kvm", "c_kve", "c_zt", "c_zd", "c_z",
            "c_o", "c_oz", "c_res", "c_n1", "c_n2", "c_x3")
        (d_xn, d_xt, d_xte, d_lg, d_l, q_oh, q_rank, q_dve, d_slot, d_scat, d_p, d_xt2,
         d_xt2e, d_h, d_g, d_y, d_ye, d_yt, d_yte, d_fin) = sems(
            "d_xn", "d_xt", "d_xte", "d_lg", "d_l", "q_oh", "q_rank", "q_dve", "d_slot", "d_scat",
            "d_p", "d_xt2", "d_xt2e", "d_h", "d_g", "d_y", "d_ye", "d_yt", "d_yte",
            "d_fin")
        (c_qs, c_qst, c_pzt, c_zero, c_xn2) = sems("c_qs", "c_qst", "c_xb", "c_zero", "c_xn2")
        s_seen = sem("a_s_seen")
        l_xn = sems("b_xn_kept", "d_xn_kept")
        dw_in = [sem("dw_in0"), sem("dw_in1")]
        xe_in = [sem("xe_in0"), sem("xe_in1")]
        ye_out = [sem("ye_out0"), sem("ye_out1")]
        dg_in = [sem(f"dg_in{i}") for i in range(8)]
        o_out = sem("o_out")

        block = ctx.enter_context(nc.Block())

        def at(buf, t):
            if isinstance(t, int):
                return buf[:, t]
            return buf[:, bass.ds(t, 1)].rearrange("p a n -> p (a n)")

        def batch_steps(eng, bt, step):
            t0 = bt * TB
            step(t0, 0, True, False)
            with eng.Fori(0, TB // 2 - 1) as i:
                step(i * 2 + (t0 + 1), 1, True, True)
                step(i * 2 + (t0 + 2), 0, True, True)
            step(t0 + TB - 1, 1, True, True)
            step(t0 + TB, 0, False, True)

        def key_slots(u):
            lo, hi = (u - 1, u) if u else (0, U - 1)
            return lo, hi

        def mask_of(u):
            return mask_n if u else mask0

        LOOP = (T - 3) // U * U

        @block.sync
        def _(sp):
            sp.dma_start(X[:, :, :], x.rearrange("(t p) n -> p t n", p=P)).then_inc(x_in, 16)
            for e in range(E):
                sp.dma_start(w1s[:, e], w1[e].rearrange("(k p) n -> p k n", p=P)).then_inc(w13_in, 16)
                sp.dma_start(w3s[:, e], w3[e].rearrange("(k p) n -> p k n", p=P)).then_inc(w13_in, 16)
            sp.wait_ge(zr_set, 1)
            sp.dma_start(rows1.rearrange("(j p) n -> p j n", p=P),
                         zrow.unsqueeze(1).broadcast_to((P, NT0, D))).then_inc(zr_out, 16)
            sp.dma_start(rows2[0:NS1].rearrange("(j p) n -> p j n", p=P),
                         zrow.unsqueeze(1).broadcast_to((P, NS1 // P, D))).then_inc(zr_out, 16)
            sp.wait_ge(x1_rdy, T)
            for e in range(E):
                sp.dma_start(w2s[:, e], w2[e].rearrange("(k p) n -> p k n", p=P)).then_inc(w2_in, 16)
            sp.wait_ge(disp, 16 * 2 * T)

            def slot_in(j, n, b_):
                sp.dma_start(xg[:, b_], rows1[bass.ds(j * P, P), :]).then_inc(xg_in[b_], 16)

            def out_store(j, done, b_):
                sp.wait_ge(y_rdy, done)
                sp.dma_start(outs1[bass.ds(j * P, P), :], yo[:, b_]).then_inc(y_out[b_], 16)
            for j in range(4):
                slot_in(j, 0, j)
            with sp.Fori(0, NT0 // 4 - 1) as i:
                for u in range(4):
                    sp.wait_ge(xgt, i * 4 + (u + 1))
                    slot_in(i * 4 + (u + 4), 0, u)
                    out_store(i * 4 + u, i * 4 + (u + 1), u % 2)
            for j in range(NT0 - 4, NT0):
                out_store(j, j + 1, j % 2)
            sp.wait_ge(dn_done, NT0)
            sp.dma_start(rope_c, cos.rearrange("(t p) n -> p t n", p=P)).then_inc(c_in, 16)
            sp.dma_start(rope_s, sin.rearrange("(t p) n -> p t n", p=P)).then_inc(c_in, 16)
            sp.dma_start(wqk2, aq.rearrange("(k p) n -> p k n", p=P)).then_inc(c_in, 16)
            sp.dma_start(wv2, av.rearrange("(k p) n -> p k n", p=P)).then_inc(c_in, 16)
            sp.dma_start(bqkv, ab.partition_broadcast(P)).then_inc(c_in, 16)
            sp.dma_start(gab, gamma_beta.partition_broadcast(P)).then_inc(c_in, 16)
            sp.wait_ge(c_x3, T)

            def expert_in(e, b_):
                sp.dma_start(v1s[:, b_], v1[bass.ds(e * D, D), :].rearrange("(k p) n -> p k n", p=P)).then_inc(dw_in[b_], 16)
                sp.dma_start(v2s[:, b_], v2[bass.ds(e * F1, F1), :].rearrange("(k p) n -> p k n", p=P)).then_inc(dw_in[b_], 16)

            def rows_in(e, b_):
                sp.dma_start(xe[:, b_], rows2[bass.ds(e * CAP, CAP), :].rearrange("(r p) n -> p r n", p=CR)).then_inc(xe_in[b_], 16)
            expert_in(0, 0)
            expert_in(1, 1)
            sp.wait_ge(d_scat, 16 * T)
            rows_in(0, 0)
            rows_in(1, 1)
            with sp.Fori(0, E // 2) as i:
                for u in range(2):
                    sp.wait_ge(d_yte, i * 2 + (u + 1))
                    sp.dma_start(outs2[bass.ds(i * (2 * CAP) + u * CAP, CAP), :].rearrange("(r p) n -> p r n", p=CR),
                                 ye[:, u]).then_inc(ye_out[u], 16)
                    nxt = (i * 2 + (u + 2)) % E
                    expert_in(nxt, u)
                    rows_in(nxt, u)
            for u in range(2):
                sp.wait_ge(ye_out[u], 16 * (E // 2))
                sp.wait_ge(dw_in[u], 32 * (E // 2 + 1))
                sp.wait_ge(xe_in[u], 16 * (E // 2 + 1))
            sp.wait_ge(zr_out, 32)
            with sp.Fori(0, T) as t:
                sp.wait_ge(d_fin, t + 1)
                sp.dma_start(out[bass.ds(t * P, P), :], X[:, bass.ds(t, 1), :].rearrange("p a n -> p (a n)")).then_inc(o_out, 16)
            sp.wait_ge(o_out, 16 * T)

        @block.scalar
        def _(act):
            act.dma_start(cst[:, :], consts[:, :]).then_inc(cst_in, 16)
            for n, w in enumerate((wq, wk, wv, wo)):
                act.dma_start(wqkvo[:, n], w.rearrange("(k p) n -> p k n", p=P)).then_inc(aw_in, 16)
            act.dma_start(wrs[:, 0], wr.rearrange("(k p) n -> p k n", p=P)).then_inc(rw_in, 16)
            act.dma_start(wrs[:, 1], gate_w.rearrange("(k p) n -> p k n", p=P)).then_inc(rw_in, 16)
            act.dma_start(rbias[:, 0], br.partition_broadcast(P)).then_inc(rw_in, 16)
            act.dma_start(rbias[:, 1], gate_b.partition_broadcast(P)).then_inc(rw_in, 16)
            act.dma_start(b1s[:, :, :], b1).then_inc(rw_in, 16)
            act.dma_start(b2s[:, :, :], b2).then_inc(rw_in, 16)

            def std(n, lo, hi):
                act.wait_ge(ln_fin, 7 * (n + 1))
                nc.scalar.activation(lnw[:, 3, lo:hi], lnw[:, 2, lo:hi], ACT.Sqrt).then_inc(ln_std, 1)
            std(0, 0, T)
            act.wait_ge(zpad_set, 2)

            def project_evac(s1, u):
                act.wait_ge(qkv_done, s1)
                if not isinstance(s1, int) or s1 > 1:
                    act.wait_ge(qpad_rdy, s1 - 1)
                nc.scalar.activation(q_t, ps[:, 1, 0:2 * P], ACT.Copy).then_inc(q_evac, 1)
                nc.scalar.activation(k_t[:, :, u, :], ps[:, 1, 2 * P:4 * P].rearrange("p (g n) -> p g n", g=KD),
                                     ACT.Copy).then_inc(k_evac, 1)

            def xnt_evac(s1):
                act.wait_ge(xt_done, s1)
                if not isinstance(s1, int) or s1 > 1:
                    act.wait_ge(qkv_done, s1 - 1)
                nc.scalar.activation(xn_t, ps[:, 0, 0:D], ACT.Copy).then_inc(xnt_rdy, 1)

            def a_step(s, u, front, scores, back):
                if front:
                    xnt_evac(s + 3)
                for p in range(HEADS // 2):
                    if scores:
                        act.wait_ge(ttr_done, s * 8 + (p + 1))
                        if p == 0:
                            if not isinstance(s, int) or s > 1:
                                act.wait_ge(rden_a, s - 1)
                        for h in (2 * p, 2 * p + 1):
                            e_ = nc.scalar.activation(prob[:, u % 2, h], prob[:, u % 2, h], ACT.Exp,
                                                      bias=nmax[:, u % 2, h:h + 1], scale=-1.0,
                                                      accum_out=den[:, u % 2, h:h + 1])
                        e_.then_inc(p_rdy, 1)
                    if back and p % 2 == 0:
                        act.wait_ge(pt_done, (s - 1) * 8 + (p + 1))
                        nc.scalar.activation(p_t[:, 0], ps[:, 4], ACT.Copy).then_inc(ptev_a, 1)
                if back:
                    act.wait_ge(dt_done, s + 0)
                    if not isinstance(s, int) or s > 1:
                        act.wait_ge(ot_rdy, s - 1)
                    nc.scalar.activation(rden_t, ps[:, 0, 0:D], ACT.Copy).then_inc(dt_evac, 1)
                if front:
                    project_evac(s + 3, (u + 2) % U)
            for t in range(2):
                xnt_evac(t + 1)
                project_evac(t + 1, t)
            a_step(0, 0, True, True, False)
            with act.Fori(0, LOOP // U) as i:
                for u in range(U):
                    a_step(i * U + (u + 1), (u + 1) % U, True, True, True)
            for s in range(LOOP + 1, T + 1):
                a_step(s, s % U, s + 2 < T, s < T, True)

            std(1, 0, T)
            with act.Fori(0, T) as t:
                act.wait_ge(b_xt, t + 1)
                nc.scalar.activation(xn_t, ps[:, 0, 0:D], ACT.Copy).then_inc(b_xte, 1)
                act.wait_ge(b_lg, t + 1)
            act.wait_ge(cw_e, 1)
            nc.scalar.activation(small[:, 5], small[:, 4], ACT.Exp).then_inc(cw_e, 1)

            def m_step(j, u, load, gu, dn):
                if load:
                    act.wait_ge(xgt, j + 2)
                    nc.scalar.activation(xg_t[:, (u + 1) % 2], ps[:, 0, 0:D], ACT.Copy).then_inc(xgte, 1)
                if gu:
                    act.wait_ge(gu_done, j + 1)
                    nc.scalar.activation(gact[:, u % 2], ps[:, 1 + u % 2], ACT.Silu).then_inc(g_act, 1)
                if dn:
                    act.wait_ge(ht_done, j + 0)
                    nc.scalar.activation(hid_t[:, (u + 1) % 2], ps[:, 5], ACT.Copy).then_inc(hte, 1)
            act.wait_ge(xgt, 1)
            nc.scalar.activation(xg_t[:, 0], ps[:, 0, 0:D], ACT.Copy).then_inc(xgte, 1)
            m_step(0, 0, True, True, False)
            with act.Fori(0, (NT0 - 2) // 2) as i:
                m_step(i * 2 + 1, 1, True, True, True)
                m_step(i * 2 + 2, 0, True, True, True)
            m_step(NT0 - 1, 1, False, True, True)
            m_step(NT0, 0, False, False, True)

            std(2, 0, T)

            def c_step(t, u, front, back):
                if front:
                    act.wait_ge(c_xt, t + 1)
                    nc.scalar.activation(xc_t[:, u], ps[:, 0, 0:D], ACT.Copy).then_inc(c_xte, 1)
                    act.wait_ge(c_qkb, t + 1)
                    if not isinstance(t, int) or t > 1:
                        act.wait_ge(c_kvm, t - 1)
                        act.wait_ge(c_qs, t - 1)
                    nc.scalar.activation(qk[:, u].rearrange("p s n -> p (s n)"), qkb, ACT.Gelu).then_inc(c_gelu, 1)
                if back:
                    act.wait_ge(c_qrt, t + 0)
                    nc.scalar.activation(at(arena[:, 1].rearrange("p (t n) -> p t n", t=T), t - 1),
                                         ps[:, 1, 0:D], ACT.Copy).then_inc(c_qrte, 1)
            for bt in range(BATCH):
                batch_steps(act, bt, c_step)
                act.wait_ge(c_qrte, (bt + 1) * TB)
                with act.Fori(0, TB // 2) as i:
                    for u in range(2):
                        t = i * 2 + (bt * TB + u)
                        act.wait_ge(c_oz, i * 2 + bt * TB)
                        nc.scalar.activation(qr_st[:, u].rearrange("p k n -> p (k n)"),
                                             at(arena[:, 1].rearrange("p (t n) -> p t n", t=T), t), ACT.Copy).then_inc(c_qst, 1)
                std(3 + bt, bt * TB, bt * TB + TB)
            std(5, 0, T)
            with act.Fori(0, T) as t:
                act.wait_ge(d_xt, t + 1)
                nc.scalar.activation(xn_t, ps[:, 0, 0:D], ACT.Copy).then_inc(d_xte, 1)
                act.wait_ge(d_lg, t + 1)
            act.wait_ge(d_p, 1)
            nc.scalar.activation(rt[:, 1], rt[:, 0], ACT.Exp).then_inc(d_p, 1)
            with act.Fori(0, E // 2) as i:
                for u in range(2):
                    e = i * 2 + u
                    act.wait_ge(d_xt2, e + 1)
                    nc.scalar.activation(xe_t[:, u], ps[:, 0, 0:KD * CAP].rearrange("p (k n) -> p k n", k=KD),
                                         ACT.Copy).then_inc(d_xt2e, 1)
                    for m in range(K1):
                        act.wait_ge(d_h, e * K1 + (m + 1))
                        nc.scalar.activation(he_t[:, u, m], ps[:, 1 + m % 2, 0:CAP], ACT.Gelu_apprx_tanh,
                                             bias=b1s[:, bass.ds(e, 1), m]).then_inc(d_g, 1)
                    act.wait_ge(d_y, e + 1)
                    for m in range(KD):
                        nc.scalar.activation(ye_t[:, m], ps[:, 3 + m, 0:CAP], ACT.Identity,
                                             bias=b2s[:, bass.ds(e, 1), m]).then_inc(d_ye, 1)

        @block.tensor
        def _(pe):
            pe.wait_ge(cst_in, 16)
            pe.wait_ge(aw_in, 64)
            pe.wait_ge(zpad_set, 2)

            def transposes(dst, src, dsem):
                for k in range(KD):
                    m_ = nc.tensor.transpose(dst[:, k * P:(k + 1) * P], src[:, k * P:(k + 1) * P], ident)
                m_.then_inc(dsem, 1)

            def mm(out_, w, m, start=True, stop=True, **kw):
                return nc.tensor.matmul(out_, w, m, start=start, stop=stop, **kw)

            def a_xt(t, v):
                pe.wait_ge(xn_rdy, t + 1)
                if not isinstance(t, int) or t > 0:
                    pe.wait_ge(xnt_rdy, t)
                if not isinstance(t, int) or t > 3:
                    pe.wait_ge(dt_evac, t - 3)
                transposes(ps[:, 0], xnb[:, v], xt_done)

            def a_qkv(t):
                pe.wait_ge(xnt_rdy, t + 1)
                if not isinstance(t, int) or t > 0:
                    pe.wait_ge(k_evac, t)
                    pe.wait_ge(vpad_rdy, t)
                if not isinstance(t, int) or t > 3:
                    pe.wait_ge(x1_rdy, t - 3)
                for w in range(2):
                    for g in range(KD):
                        for k in range(KD):
                            mm(ps[:, 1, (2 * w + g) * P:(2 * w + g + 1) * P],
                               wqkvo[:, w, k, g * P:(g + 1) * P], xn_t[:, k], k == 0, k == KD - 1)
                for k in range(KD):
                    m_ = mm(ps[:, 6, 0:D], xn_t[:, k], wqkvo[:, 2, k], k == 0, k == KD - 1)
                m_.then_inc(qkv_done, 1)

            def a_scores(s, u, p):
                if p == 0:
                    pe.wait_ge(qpad_rdy, s + 1)
                    pe.wait_ge(k_evac, s + 1)
                if not isinstance(s, int) or s > 0 or p > 1:
                    pe.wait_ge(ttr_done, s * 8 + (p - 1))
                lo, hi = key_slots(u)
                for h in (2 * p, 2 * p + 1):
                    m_ = mm(ps[:, 2 + p % 2, (h % 2) * 2 * P:(h % 2 + 1) * 2 * P], q_pad[:, u % 2, h],
                            k_t[:, h // HB, lo:hi + 1:hi - lo, :])
                m_.then_inc(s_done, 1)

            def a_ptrans(s, u, p):
                pe.wait_ge(p_rdy, (s - 1) * 8 + (p + 1))
                n = (s - 1) * 4 + p // 2
                if not isinstance(s, int) or s > 1 or p > 1:
                    pe.wait_ge(ptev_d if p % 2 else ptev_a, n)
                for h in (2 * p, 2 * p + 1):
                    for k in range(2):
                        m_ = nc.tensor.transpose(ps[:, 4 + p % 2, ((h % 2) * 2 + k) * P:((h % 2) * 2 + k + 1) * P],
                                                 prob[:, (u + 1) % 2, h, k * P:(k + 1) * P], ident)
                m_.then_inc(pt_done, 1)

            def a_pv(s, u, p):
                n = (s - 1) * 4 + (p // 2 + 1)
                pe.wait_ge(ptev_d if p % 2 else ptev_a, n)
                if p == 0:
                    pe.wait_ge(vpad_rdy, s)
                    if not isinstance(s, int) or s > 1:
                        pe.wait_ge(ot_rdy, s - 1)
                g, r = p // 4, p % 4
                lo, hi = key_slots((u - 1) % U)
                n = 0
                for h in (2 * p, 2 * p + 1):
                    for k, slot in enumerate((lo, hi)):
                        m_ = mm(ps[32 * r:32 * r + 32, 7, g * P:(g + 1) * P], v_pad[:, slot, h],
                                p_t[:, p % 2, ((h % 2) * 2 + k) * P:((h % 2) * 2 + k + 1) * P], n == 0, n == 3)
                        n += 1
                m_.then_inc(pv_done, 1)

            def a_wo(s):
                pe.wait_ge(ot_rdy, s + 0)
                for k in range(KD):
                    m_ = mm(ps[:, 6, D:2 * D], o_t[:, k], wqkvo[:, 3, k], k == 0, k == KD - 1)
                m_.then_inc(wo_done, 1)

            def a_step(s, u, front, scores, back):
                if front:
                    a_xt(s + 2, u % 2)
                for p in range(HEADS // 2):
                    if scores:
                        a_scores(s, u, p)
                    if back:
                        a_ptrans(s, u, p)
                        if p:
                            a_pv(s, u, p - 1)
                if back:
                    a_pv(s, u, HEADS // 2 - 1)
                    pe.wait_ge(rden_rdy, s + 0)
                    if front:
                        pe.wait_ge(xnt_rdy, s + 3)
                    elif not isinstance(s, int) or s > 1:
                        pe.wait_ge(dt_evac, s - 1)
                    transposes(ps[:, 0], rden_x.rearrange("p h c -> p (h c)"), dt_done)
                if front:
                    a_qkv(s + 2)
                if back:
                    if not front:
                        pe.wait_ge(x1_rdy, s - 1)
                        pe.wait_ge(vpad_rdy, T)
                    else:
                        pe.wait_ge(vpad_rdy, s + 3)
                    a_wo(s)
            for t in range(2):
                a_xt(t, t)
                a_qkv(t)
            a_step(0, 0, True, True, False)
            with pe.Fori(0, LOOP // U) as i:
                for u in range(U):
                    a_step(i * U + (u + 1), (u + 1) % U, True, True, True)
            for s in range(LOOP + 1, T + 1):
                a_step(s, s % U, s + 2 < T, s < T, True)

            pe.wait_ge(rw_in, 96)
            pe.wait_ge(dt_evac, T)

            def logits(xnr, xt, xte, lg, l, r):
                with pe.Fori(0, T // 2) as i:
                    for u in range(2):
                        t = i * 2 + u
                        pe.wait_ge(xnr, t + 1)
                        transposes(ps[:, 0], xnb[:, u], xt)
                        pe.wait_ge(xte, t + 1)
                        pe.wait_ge(l, t)
                        for k in range(KD):
                            m_ = mm(ps[:, 1, 0:P], xn_t[:, k], wrs[:, r, k], k == 0, k == KD - 1)
                        m_.then_inc(lg, 1)
            logits(b_xn, b_xt, b_xte, b_lg, b_l, 0)

            def ranks(ohs, rank):
                pe.wait_ge(ohs, 1)
                m2 = rt[:, 2].rearrange("p e t -> p (e t)")
                mm(ps[:, 2, 0:E * T], tri, m2)
                mm(ps[:, 3, 0:E * T], ones, m2).then_inc(rank, 1)
            ranks(r_oh, r_rank)

            pe.wait_ge(w13_in, 16 * 2 * E)
            pe.wait_ge(w2_in, 16 * E)
            pe.wait_ge(e_rdy, 1)

            def m_xt(j, q, r):
                pe.wait_ge(xg_in[r], q)
                if not isinstance(j, int) or j > 0:
                    pe.wait_ge(xgte, j)
                transposes(ps[:, 0], xg[:, r], xgt)

            def m_gu(j, u):
                e = pe.value_load(etile_i[0:1, bass.ds(j, 1)], min_val=0, max_val=E - 1)
                pe.wait_ge(xgte, j + 1)
                if not isinstance(j, int) or j > 1:
                    pe.wait_ge(h_rdy, j - 1)
                for w, bank in ((arena[:, 0, :], 1 + u % 2), (arena[:, 1, :], 3 + u % 2)):
                    for k in range(KD):
                        m_ = mm(ps[:, bank], xg_t[:, u % 2, k], w[:, bass.ds(e * (KD * F0) + k * F0, F0)], k == 0, k == KD - 1)
                m_.then_inc(gu_done, 1)

            def m_ht(j, u):
                pe.wait_ge(h_rdy, j + 0)
                if not isinstance(j, int) or j > 1:
                    pe.wait_ge(hte, j - 1)
                for k in range(K0):
                    m_ = nc.tensor.transpose(ps[:, 5, k * P:(k + 1) * P], hid[:, (u + 1) % 2, k * P:(k + 1) * P], ident)
                m_.then_inc(ht_done, 1)

            def m_dn(j, u):
                e = pe.value_load(etile_i[0:1, bass.ds(j - 1, 1)], min_val=0, max_val=E - 1)
                pe.wait_ge(hte, j + 0)
                if not isinstance(j, int) or j > 1:
                    pe.wait_ge(y_rdy, j - 1)
                for k in range(K0):
                    m_ = mm(ps[:, 6, 0:D], hid_t[:, (u + 1) % 2, k],
                            arena[:, 2, bass.ds(e * (K0 * D) + k * D, D)], k == 0, k == K0 - 1)
                m_.then_inc(dn_done, 1)

            def m_step(j, u, count, front, last):
                if front:
                    m_xt(j + 1, count, (u + 1) % 4)
                if not isinstance(j, int) or j > 0:
                    m_ht(j, u)
                if not last:
                    m_gu(j, u)
                if not isinstance(j, int) or j > 0:
                    m_dn(j, u)
            m_xt(0, 16, 0)
            m_step(0, 0, 16, True, False)
            with pe.Fori(0, (NT0 - 4) // 4) as i:
                for u in range(4):
                    m_step(i * 4 + (u + 1), u + 1, i * 16 + 16 * ((u + 2) // 4 + 1), True, False)
            for j in range(NT0 - 3, NT0 + 1):
                m_step(j, j, ((j + 1) // 4 + 1) * 16, j < NT0 - 1, j == NT0)

            pe.wait_ge(c_in, 96)
            pe.wait_ge(y_rdy, NT0)

            def c_step(t, u, front, back):
                if front:
                    pe.wait_ge(c_xn, t + 1)
                    if not isinstance(t, int) or t > 0:
                        pe.wait_ge(c_xte, t)
                    transposes(ps[:, 0], xnb[:, u], c_xt)
                    pe.wait_ge(c_xte, t + 1)
                    if not isinstance(t, int) or t > 0:
                        pe.wait_ge(c_qkb, t)
                        pe.wait_ge(c_vb, t)
                    for k in range(KD):
                        m_ = mm(ps[:, 2], xc_t[:, u, k], wqk2[:, k], k == 0, k == KD - 1)
                    m_.then_inc(c_qk, 1)
                    for k in range(KD):
                        m_ = mm(ps[:, 3, 0:D], xc_t[:, u, k], wv2[:, k], k == 0, k == KD - 1)
                    m_.then_inc(c_v, 1)
                if back:
                    v = (u + 1) % 2
                    pe.wait_ge(c_rope, t + 0)
                    pe.wait_ge(c_vb, t + 0)
                    if not isinstance(t, int) or t > 1:
                        pe.wait_ge(c_qrte, t - 1)
                    transposes(ps[:, 1], qkr[:, v, 0], c_qrt)
                    for g in range(KD):
                        mm(ps[:, 4 + g, 0:P], qkr[:, v, 1, g * P:(g + 1) * P], vb[:, v, g * P:(g + 1) * P],
                           False, False, skip_group_check=True)
                    mm(ps[:, 6, 0:D], meanm, qk[:, v, 1], False, False, skip_group_check=True).then_inc(c_kvm, 1)
            for bt in range(BATCH):
                pe.wait_ge(c_zero, bt + 1)
                batch_steps(pe, bt, c_step)
                pe.wait_ge(c_kve, 3 * (bt + 1))
                with pe.Fori(0, TB // 2) as i:
                    for u in range(2):
                        t = i * 2 + (bt * TB + u)
                        pe.wait_ge(c_qst, t + 1)
                        pe.wait_ge(c_oz, t)
                        for g in range(KD):
                            m_ = mm(ps[:, 7, g * P:(g + 1) * P], qr_st[:, u, g], kv_bd[:, g])
                        m_.then_inc(c_o, 1)

            logits(d_xn, d_xt, d_xte, d_lg, d_l, 1)
            ranks(q_oh, q_rank)
            with pe.Fori(0, E // 2) as i:
                for u in range(2):
                    e = i * 2 + u
                    pe.wait_ge(xe_in[u], i * 16 + 16)
                    pe.wait_ge(d_xt2e, e)
                    for k in range(KD):
                        for r in range(2):
                            m_ = nc.tensor.transpose(ps[:, 0, k * CAP + r * CR:k * CAP + (r + 1) * CR],
                                                     xe[:, u, r, k * P:(k + 1) * P], ident[0:CR, 0:CR])
                    m_.then_inc(d_xt2, 1)
                    pe.wait_ge(dw_in[u], i * 32 + 32)
                    pe.wait_ge(d_xt2e, e + 1)
                    for m in range(K1):
                        if m < 2:
                            pe.wait_ge(d_g, e * K1)
                        else:
                            pe.wait_ge(d_g, e * K1 + (m - 1))
                        for k in range(KD):
                            m_ = mm(ps[:, 1 + m % 2, 0:CAP], v1s[:, u, k, m * P:(m + 1) * P], xe_t[:, u, k], k == 0, k == KD - 1)
                        m_.then_inc(d_h, 1)
                    pe.wait_ge(d_g, e * K1 + K1)
                    pe.wait_ge(d_ye, e * KD)
                    for m in range(KD):
                        for k in range(K1):
                            m_ = mm(ps[:, 3 + m, 0:CAP], v2s[:, u, k, m * P:(m + 1) * P], he_t[:, u, k], k == 0, k == K1 - 1)
                    m_.then_inc(d_y, 1)
                    pe.wait_ge(d_ye, e * KD + KD)
                    pe.wait_ge(d_yte, e)
                    for r in range(2):
                        for m in range(KD):
                            m_ = nc.tensor.transpose(ps[0:CR, 5, r * D + m * P:r * D + (m + 1) * P],
                                                     ye_t[:, m, r * CR:(r + 1) * CR], ident)
                    m_.then_inc(d_yt, 1)

        @block.vector
        def _(dve):
            V = nc.vector

            def stats(t, done):
                V.bn_stats(at(st, t), at(X, t)).then_inc(done, 1)

            def finish_stats(n, lo, hi, eps, done, count):
                dve.wait_ge(done, count)
                f = ln_fin
                me, qe, mo, qo = (st[:, lo:hi, k] for k in (1, 2, 4, 5))
                w = [lnw[:, k, lo:hi] for k in range(4)]
                V.tensor_tensor(w[0], me, mo, ALU.add).then_inc(f, 1)
                V.tensor_tensor(w[1], me, mo, ALU.subtract).then_inc(f, 1)
                V.tensor_tensor(w[2], qe, qo, ALU.add).then_inc(f, 1)
                dve.wait_ge(f, 7 * n + 3)
                V.tensor_scalar(mean[:, lo:hi], w[0], 0.5, None, ALU.mult).then_inc(f, 1)
                V.tensor_tensor(w[1], w[1], w[1], ALU.mult).then_inc(f, 1)
                dve.wait_ge(f, 7 * n + 5)
                V.tensor_scalar(w[1], w[1], 0.25, eps, ALU.mult, ALU.add).then_inc(f, 1)
                dve.wait_ge(f, 7 * n + 6)
                V.scalar_tensor_tensor(out=w[2], in0=w[2], scalar=1.0 / D, in1=w[1],
                                       op0=ALU.mult, op1=ALU.add).then_inc(f, 1)
                dve.wait_ge(ln_std, n + 1)
                V.reciprocal(rstd[:, lo:hi], w[3]).then_inc(ln_rstd, 1)
                dve.wait_ge(ln_rstd, n + 1)

            def col(buf, t):
                return buf[:, t:t + 1] if isinstance(t, int) else buf[:, bass.ds(t, 1)]

            def norm(t, dst):
                return V.tensor_scalar(dst, at(X, t), col(mean, t), col(rstd, t), ALU.subtract, ALU.mult)

            dve.wait_ge(x_in, 16)
            with dve.Fori(0, T) as t:
                stats(t, ln_st[0])
            finish_stats(0, 0, T, 1e-5, ln_st[0], T)
            dve.wait_ge(cst_in, 16)
            dve.wait_ge(zpad_set, 2)

            def a_norm(t, u):
                if not isinstance(t, int) or t > 1:
                    dve.wait_ge(xt_done, t - 1)
                norm(t, xnb[:, u % 2]).then_inc(xn_rdy, 1)

            def v_evac(t, u):
                dve.wait_ge(qkv_done, t + 1)
                dst = v_pad[:, u].rearrange("p (a b) (c d) -> p a (b c) d", b=2, c=2)[:, :, 0:4:3, :]
                V.tensor_copy(dst, ps[:, 6, 0:D].rearrange("p (a b d) -> p a b d", b=2, d=HD)).then_inc(vpad_rdy, 1)

            def a_step(s, u, front, scores, back, nxt):
                if nxt:
                    a_norm(s + 3, u + 3)
                if back:
                    dve.wait_ge(p_rdy, s * 8)
                    V.reciprocal(rden, den[:, (u + 1) % 2]).then_inc(rden_a, 1)
                    dve.wait_ge(rden_a, s + 0)
                    dve.wait_ge(dt_done, s - 1)
                    V.tensor_copy(rden_x, rden.unsqueeze(2).broadcast_to((P, HEADS, HD))).then_inc(rden_rdy, 1)
                for p in range(HEADS // 2):
                    if scores:
                        dve.wait_ge(s_done, s * 8 + (p + 1))
                        if u % U == 0 and p == 0:
                            dve.wait_ge(mask_rdy, s // U + 1)
                        dve.sem_inc(s_seen, 1)
                        for h in (2 * p, 2 * p + 1):
                            r_ = V.tensor_tensor_reduce(
                                out=prob[:, u % 2, h], in0=ps[:, 2 + p % 2, (h % 2) * 2 * P:(h % 2 + 1) * 2 * P],
                                in1=mask_of(u), scale=-1.0 / HD ** 0.5, scalar=3e38, op0=ALU.add, op1=ALU.min,
                                accum_out=nmax[:, u % 2, h:h + 1])
                        r_.then_inc(ttr_done, 1)
                    if back and p % 2:
                        dve.wait_ge(pt_done, (s - 1) * 8 + (p + 1))
                        V.tensor_copy(p_t[:, 1], ps[:, 5]).then_inc(ptev_d, 1)
                if back:
                    dve.wait_ge(pv_done, s * 8)
                    dve.wait_ge(dt_evac, s + 0)
                    dve.wait_ge(wo_done, s - 1)
                    V.tensor_tensor(o_t.rearrange("p k n -> p (k n)"), ps[:, 7, 0:D], rden_t, ALU.mult).then_inc(ot_rdy, 1)
                if front:
                    v_evac(s + 2, (u + 2) % U)
                if back:
                    dve.wait_ge(wo_done, s + 0)
                    V.tensor_tensor(at(X, s - 1), at(X, s - 1), ps[:, 6, D:2 * D], ALU.add).then_inc(x1_rdy, 1)
                    dve.wait_ge(x1_rdy, s + 0)
                    stats(s - 1, ln_st[1])
            a_norm(0, 0)
            a_norm(1, 1)
            v_evac(0, 0)
            a_norm(2, 0)
            v_evac(1, 1)
            a_step(0, 0, True, True, False, True)
            with dve.Fori(0, LOOP // U) as i:
                for u in range(U):
                    a_step(i * U + (u + 1), (u + 1) % U, True, True, True, True)
            for s in range(LOOP + 1, T + 1):
                a_step(s, s % U, s + 2 < T, s < T, True, s + 3 < T)

            def router(r, xnr, xt, lg, l, eps_n, done, count):
                finish_stats(eps_n, 0, T, 1e-5, done, count)

                def norm2(t, u):
                    if not isinstance(t, int) or t > 1:
                        dve.wait_ge(xt, t - 1)
                    norm(t, xnb[:, u]).then_inc(xnr, 1)
                    norm(t, at(XN, t)).then_inc(l_xn[r], 1)

                def logit_of(t):
                    dve.wait_ge(lg, t + 1)
                    dst = logit[:, :, t] if isinstance(t, int) else logit[:, :, bass.ds(t, 1)].rearrange("p e a -> p (e a)")
                    V.tensor_tensor(dst, ps[:, 1, 0:E], rbias[:, r], ALU.add).then_inc(l, 1)
                norm2(0, 0)
                with dve.Fori(0, T // 2 - 1) as i:
                    norm2(i * 2 + 1, 1)
                    logit_of(i * 2)
                    norm2(i * 2 + 2, 0)
                    logit_of(i * 2 + 1)
                norm2(T - 1, 1)
                logit_of(T - 2)
                logit_of(T - 1)
                dve.wait_ge(l, T)
            dve.wait_ge(rw_in, 96)
            dve.wait_ge(dt_done, T)
            router(0, b_xn, b_xt, b_lg, b_l, 1, ln_st[1], T)

            class Chain:
                def __init__(self, s_):
                    self.s, self.n = s_, 0

                def __call__(self, ins):
                    self.n += 1
                    ins.then_inc(self.s, 1)
                    dve.wait_ge(self.s, self.n)

            def te(ap):
                return ap.rearrange("p e t -> p t e")

            def over_e(ap):
                return ap.unsqueeze(1).broadcast_to((P, E, T))

            def first_max(do, src, mx, onehot):
                do(V.tensor_reduce(mx, te(src), AX_X, ALU.max))
                do(V.tensor_tensor(rt[:, 0], src, over_e(mx), ALU.is_equal))
                do(V.tensor_tensor(rt[:, 0], rt[:, 0], w8, ALU.mult))
                do(V.tensor_reduce(small[:, 15], te(rt[:, 0]), AX_X, ALU.max))
                do(V.tensor_tensor(onehot, w8, over_e(small[:, 15]), ALU.is_equal))

            def earlier_tiles(do, rank):
                dve.wait_ge(rank, 1)
                do(V.tensor_copy(rt[:, 0].rearrange("p e t -> p (e t)"), ps[:, 3, 0:E * T]))
                for e in range(E):
                    V.tensor_tensor_scan(rt[:, 1, e], ones[:, 0:T], rt[:, 0, e], 0.0, ALU.mult, ALU.add).then_inc(do.s, 1)
                do.n += E
                dve.wait_ge(do.s, do.n)
                do(V.tensor_tensor(rt[:, 3], rt[:, 1], rt[:, 0], ALU.subtract))
                do(V.tensor_tensor(rt[:, 3].rearrange("p e t -> p (e t)"), rt[:, 3].rearrange("p e t -> p (e t)"),
                                   ps[:, 2, 0:E * T], ALU.add))

            do = Chain(r_dve)
            first_max(do, logit, small[:, 0], oh[:, 0])
            do(V.scalar_tensor_tensor(out=rt[:, 1], in0=oh[:, 0], scalar=-3e38, in1=logit[:, :, :], op0=ALU.mult, op1=ALU.add))
            first_max(do, rt[:, 1], small[:, 1], oh[:, 1])
            V.tensor_tensor(rt[:, 2], oh[:, 0], oh[:, 1], ALU.add).then_inc(r_oh, 1)
            V.tensor_tensor(small[:, 4], small[:, 1], small[:, 0], ALU.subtract).then_inc(cw_e, 1)
            earlier_tiles(do, r_rank)
            cnt, cp, ends, base = (ecol[:, k] for k in range(4))
            do(V.tensor_scalar(cnt, rt[:, 1, :, T - 1], float(P - 1), None, ALU.add))
            do(V.tensor_copy(ecol_i[:, 0], cnt))
            do(V.tensor_scalar(ecol_i[:, 1], ecol_i[:, 0], 7, 7, ALU.arith_shift_right, ALU.arith_shift_left))
            do(V.tensor_copy(cp, ecol_i[:, 1]))
            do(V.tensor_tensor_scan(ends, ones[:, 0:E], cp, 0.0, ALU.mult, ALU.add))
            do(V.tensor_tensor(base, ends, cp, ALU.subtract))
            do(V.tensor_tensor(rt[:, 3], rt[:, 3], base.unsqueeze(2).broadcast_to((P, E, T)), ALU.add))
            for k in range(2):
                do(V.tensor_tensor(rt[:, 0], rt[:, 3], oh[:, k], ALU.mult))
                do(V.tensor_reduce(small[:, 6 + k], te(rt[:, 0]), AX_X, ALU.add))
                V.tensor_copy(slot_i[:, k], small[:, 6 + k]).then_inc(slot_rdy, 1)
            do(V.tensor_tensor(etile, ends.unsqueeze(1).broadcast_to((P, NT0, E)),
                               jfirst.unsqueeze(2).broadcast_to((P, NT0, E)), ALU.is_le))
            do(V.tensor_reduce(etile_s, etile, AX_X, ALU.add))
            do(V.tensor_scalar(etile_s, etile_s, float(E - 1), None, ALU.min))
            V.tensor_copy(etile_i, etile_s).then_inc(e_rdy, 1)
            dve.wait_ge(cw_e, 2)
            do(V.tensor_scalar(small[:, 6], small[:, 5], 1.0, None, ALU.add))
            do(V.reciprocal(cw[:, 0], small[:, 6]))
            do(V.tensor_tensor(cw[:, 1], cw[:, 0], small[:, 5], ALU.mult))
            dve.wait_ge(e_rdy, 1)

            def m_step(j, u, count, gu, dn):
                if gu:
                    dve.wait_ge(g_act, j + 1)
                    if not isinstance(j, int) or j > 1:
                        dve.wait_ge(ht_done, j - 1)
                    V.tensor_tensor(hid[:, u % 2], gact[:, u % 2], ps[:, 3 + u % 2], ALU.mult).then_inc(h_rdy, 1)
                if dn:
                    dve.wait_ge(dn_done, j + 0)
                    if not isinstance(j, int) or count > 0:
                        dve.wait_ge(y_out[(u + 1) % 2], count)
                    V.tensor_copy(yo[:, (u + 1) % 2], ps[:, 6, 0:D]).then_inc(y_rdy, 1)
            m_step(0, 0, 0, True, False)
            with dve.Fori(0, (NT0 - 2) // 2) as i:
                m_step(i * 2 + 1, 1, i * 16, True, True)
                m_step(i * 2 + 2, 0, i * 16, True, True)
            m_step(NT0 - 1, 1, (NT0 - 2) // 2 * 16, True, True)
            m_step(NT0, 0, (NT0 - 2) // 2 * 16, False, True)

            dve.wait_ge(r_dve, do.n)
            with dve.Fori(0, T // 4) as i:
                for r in range(4):
                    t = i * 4 + r
                    dve.wait_ge(yg_in[r], i * 32 + 32)
                    for k in range(2):
                        V.scalar_tensor_tensor(out=at(X, t), in0=yg[:, 2 * r + k], scalar=col(cw[:, k], t), in1=at(X, t),
                                               op0=ALU.mult, op1=ALU.add).then_inc(yg_acc, 1)
                        dve.wait_ge(yg_acc, t * 2 + (k + 1))
                    stats(t, ln_st[2])

            finish_stats(2, 0, T, 1e-5, ln_st[2], T)
            dve.wait_ge(c_in, 96)

            def c_norm(t, u):
                if not isinstance(t, int) or t > 1:
                    dve.wait_ge(c_xt, t - 1)
                norm(t, xnb[:, u]).then_inc(c_xn, 1)
                norm(t, at(XN, t)).then_inc(c_xn2, 1)

            def c_step(bt):
                def pairs(ap):
                    return ap.rearrange("p s (n two) -> p s n two", two=2)

                def step(t, u, front, back):
                    if front:
                        if not isinstance(t, int) or t % TB != TB - 1:
                            c_norm(t + 1, (u + 1) % 2)
                        dve.wait_ge(c_qk, t + 1)
                        if not isinstance(t, int) or t > 0:
                            dve.wait_ge(c_gelu, t)
                        V.tensor_tensor(qkb, ps[:, 2], bqkv[:, 0:2 * D], ALU.add).then_inc(c_qkb, 1)
                        dve.wait_ge(c_v, t + 1)
                        if not isinstance(t, int) or t > 1:
                            dve.wait_ge(c_kvm, t - 1)
                        V.tensor_tensor(vb[:, u], ps[:, 3, 0:D], bqkv[:, 2 * D:3 * D], ALU.add).then_inc(c_vb, 1)
                    if back:
                        v = (u + 1) % 2
                        n = t - (bt * TB + 1)
                        q = qk[:, v]
                        dve.wait_ge(c_gelu, t + 0)
                        V.tensor_scalar(q, q, 0.21, None, ALU.add).then_inc(c_qk21, 1)
                        dve.wait_ge(c_qk21, t + 0)
                        cosb = at(rope_c, n).unsqueeze(1).broadcast_to((P, 2, P))
                        sinb = at(rope_s, n).unsqueeze(1).broadcast_to((P, 2, P))
                        qp, rp = pairs(q), pairs(qkr[:, v])
                        ra4 = ra.rearrange("p (h s n) -> p h s n", h=2, s=2)
                        rb4 = rb.rearrange("p (h s n) -> p h s n", h=2, s=2)
                        for h in range(2):
                            V.tensor_tensor(ra4[:, h], qp[:, :, :, h], cosb, ALU.mult).then_inc(c_ra, 1)
                            V.tensor_tensor(rb4[:, h], qp[:, :, :, 1 - h], sinb, ALU.mult).then_inc(c_ra, 1)
                        dve.wait_ge(c_ra, t * 4)
                        V.tensor_tensor(rp[:, :, :, 0], ra4[:, 0], rb4[:, 0], ALU.subtract).then_inc(c_rb, 1)
                        V.tensor_tensor(rp[:, :, :, 1], ra4[:, 1], rb4[:, 1], ALU.add).then_inc(c_rope, 1)
                return step

            for bt in range(BATCH):
                for g in range(3):
                    m_ = V.memset(ps[:, 4 + g, 0:D], 0.0)
                m_.then_inc(c_zero, 1)
                c_norm(bt * TB, 0)
                batch_steps(dve, bt, c_step(bt))
                dve.wait_ge(c_kvm, (bt + 1) * TB)
                for g in range(KD):
                    V.tensor_tensor(kv_bd[:, g], ps[:, 4 + g, 0:P], bdm, ALU.mult).then_inc(c_kve, 1)
                V.tensor_copy(kmean, ps[:, 6, 0:D]).then_inc(c_kve, 1)
                dve.wait_ge(c_kve, 3 * (bt + 1))
                with dve.Fori(0, TB) as i:
                    t = i + bt * TB
                    dve.wait_ge(c_zt, t + 1)
                    V.tensor_reduce(zd[:, 0], zt.rearrange("p (h c) -> p h c", h=HEADS), AX_X, ALU.add).then_inc(c_zd, 1)
                    dve.wait_ge(c_zd, t * 2 + 1)
                    V.tensor_scalar(zd[:, 1], zd[:, 0], 1e-6, None, ALU.add).then_inc(c_zd, 1)
                    dve.wait_ge(c_zd, t * 2 + 2)
                    V.reciprocal(zd[:, 0], zd[:, 1]).then_inc(c_z, 1)
                    dve.wait_ge(c_z, t + 1)
                    dve.wait_ge(c_o, t + 1)
                    V.tensor_tensor(at(qs, t).rearrange("p (h c) -> p h c", h=HEADS),
                                    ps[:, 7, 0:D].rearrange("p (h c) -> p h c", h=HEADS),
                                    zd[:, 0].unsqueeze(2).broadcast_to((P, HEADS, HD)), ALU.mult).then_inc(c_oz, 1)
                    dve.wait_ge(c_oz, t + 1)
                    V.tensor_tensor(at(qs, t), at(qs, t), at(XN, t), ALU.add).then_inc(c_res, 1)
                    dve.wait_ge(c_res, t + 1)
                    V.bn_stats(at(st, t), at(qs, t)).then_inc(ln_st[3], 1)
                finish_stats(3 + bt, bt * TB, (bt + 1) * TB, 1e-12, ln_st[3], (bt + 1) * TB)
                with dve.Fori(0, TB) as i:
                    t = i + bt * TB
                    V.tensor_scalar(at(qs, t), at(qs, t), col(mean, t), col(rstd, t), ALU.subtract, ALU.mult).then_inc(c_n1, 1)
                    dve.wait_ge(c_n1, t + 1)
                    V.tensor_tensor(at(qs, t), at(qs, t), gab[:, 0:D], ALU.mult).then_inc(c_n2, 1)
                    dve.wait_ge(c_n2, t + 1)
                    dve.wait_ge(c_pzt, t + 1)
                    V.tensor_tensor(at(X, t), at(X, t), at(qs, t), ALU.add).then_inc(c_x3, 1)
            dve.wait_ge(c_x3, T)
            with dve.Fori(0, T) as t:
                stats(t, ln_st[4])

            router(1, d_xn, d_xt, d_lg, d_l, 5, ln_st[4], T)
            do = Chain(q_dve)
            first_max(do, logit, small[:, 0], oh[:, 0])
            V.tensor_copy(rt[:, 2], oh[:, 0]).then_inc(q_oh, 1)
            V.tensor_tensor(rt[:, 0], logit[:, :, :], over_e(small[:, 0]), ALU.subtract).then_inc(d_p, 1)
            dve.wait_ge(d_p, 2)
            do(V.tensor_reduce(small[:, 2], te(rt[:, 1]), AX_X, ALU.add))
            do(V.reciprocal(small[:, 3], small[:, 2]))
            earlier_tiles(do, q_rank)
            do(V.tensor_tensor(rt[:, 0], rt[:, 3], oh[:, 0], ALU.mult))
            do(V.tensor_reduce(small[:, 6], te(rt[:, 0]), AX_X, ALU.add))
            do(V.tensor_tensor(rt[:, 0], ecap, oh[:, 0], ALU.mult))
            do(V.tensor_reduce(small[:, 7], te(rt[:, 0]), AX_X, ALU.add))
            do(V.tensor_scalar(small[:, 8], small[:, 6], float(CAP), None, ALU.is_lt))
            do(V.tensor_tensor(small[:, 9], small[:, 6], small[:, 7], ALU.add))
            do(V.tensor_tensor(small[:, 10], small[:, 9], small[:, 8], ALU.mult))
            do(V.tensor_tensor(small[:, 11], small[:, 9], trash, ALU.subtract))
            do(V.tensor_tensor(small[:, 11], small[:, 11], small[:, 8], ALU.mult))
            do(V.tensor_tensor(small[:, 11], small[:, 11], trash, ALU.add))
            do(V.tensor_tensor(cw[:, 0], small[:, 3], small[:, 8], ALU.mult))
            V.tensor_copy(slot2_i[:, 0], small[:, 11]).then_inc(d_slot, 1)
            V.tensor_copy(slot2_i[:, 1], small[:, 10]).then_inc(d_slot, 1)
            with dve.Fori(0, E // 2) as i:
                for u in range(2):
                    dve.wait_ge(d_yt, i * 2 + (u + 1))
                    dve.wait_ge(ye_out[u], i * 16)
                    V.tensor_copy(ye[:, u].rearrange("p r n -> p (r n)"), ps[0:CR, 5]).then_inc(d_yte, 1)
            with dve.Fori(0, T // 8) as i:
                for r in range(8):
                    t = i * 8 + r
                    dve.wait_ge(dg_in[r], i * 16 + 16)
                    V.scalar_tensor_tensor(out=at(X, t), in0=XN[:, 8 + r], scalar=col(cw[:, 0], t), in1=at(X, t),
                                           op0=ALU.mult, op1=ALU.add).then_inc(d_fin, 1)

        @block.gpsimd
        def _(pool):
            G = nc.gpsimd
            G.memset(zrow, 0.0).then_inc(zr_set, 1)
            G.memset(k_t[:, :, U - 1], 0.0).then_inc(zpad_set, 1)
            G.memset(v_pad, 0.0).then_inc(zpad_set, 1)
            pool.wait_ge(cst_in, 16)
            G.tensor_copy(mask0, cst[:, C_MT:C_MT + 2 * P]).then_inc(mask_rdy, 1)

            def q_spread(t, v):
                pool.wait_ge(q_evac, t + 1)
                for g in range(KD):
                    g_ = G.tensor_tensor(q_pad[:, v, g * HB:(g + 1) * HB], q_t[:, g].unsqueeze(1).broadcast_to((P, HB, P)),
                                         hmask.unsqueeze(2).broadcast_to((P, HB, P)), ALU.mult)
                g_.then_inc(qpad_rdy, 1)

            def a_step(s, u):
                q_spread(s + 2, u % 2)
                if u == U - 1:
                    pool.wait_ge(ttr_done, (s - 2) * 8)
                    n = ((s + 1) % TB // U + (U - 1)) // U
                    src = cst[:, bass.ds(n * (2 * P) + C_MT, 2 * P)] if not isinstance(n, int) else \
                        cst[:, C_MT + n * 2 * P:C_MT + (n + 1) * 2 * P]
                    G.tensor_copy(mask0, src).then_inc(mask_rdy, 1)
            q_spread(0, 0)
            q_spread(1, 1)
            a_step(0, 0)
            with pool.Fori(0, LOOP // U) as i:
                for u in range(U):
                    a_step(i * U + (u + 1), (u + 1) % U)
            for s in range(LOOP + 1, T - 2):
                a_step(s, s % U)

            pool.wait_ge(zr_out, 32)
            pool.wait_ge(slot_rdy, 2)
            for t in range(T):
                for k in range(2):
                    G.indirect_dma_start(rows1[:, :], bass.IndirectOffsetOnAxis(ap=slot_i[:, k, t:t + 1], axis=0),
                                         XN[:, t], None).then_inc(disp, 16)
            pool.wait_ge(disp, 32 * T)
            pool.wait_ge(y_out0, 16 * (NT0 // 2))
            pool.wait_ge(y_out1, 16 * (NT0 // 2))
            for t in range(T):
                if t >= 4:
                    pool.wait_ge(yg_acc, 2 * (t - 3))
                for k in range(2):
                    G.indirect_dma_start(yg[:, 2 * (t % 4) + k], None, outs1[:, :],
                                         bass.IndirectOffsetOnAxis(ap=slot_i[:, k, t:t + 1], axis=0)).then_inc(yg_in[t % 4], 16)

            for bt in range(BATCH):
                with pool.Fori(0, TB // 2) as i:
                    for u in range(2):
                        t = i * 2 + (bt * TB + u)
                        pool.wait_ge(c_qk21, t + 1)
                        G.tensor_copy(at(qs, t), qk[:, u, 0]).then_inc(c_qs, 1)
                pool.wait_ge(c_kve, 3 * (bt + 1))
                pool.wait_ge(c_qs, (bt + 1) * TB)
                with pool.Fori(0, TB) as i:
                    t = i + bt * TB
                    pool.wait_ge(c_z, t)
                    G.tensor_tensor(zt, at(qs, t), kmean, ALU.mult).then_inc(c_zt, 1)
                    G.tensor_tensor(at(X, t), at(X, t), gab[:, D:2 * D], ALU.add).then_inc(c_pzt, 1)

            pool.wait_ge(d_slot, 2)
            for t in range(T):
                G.indirect_dma_start(rows2[:, :], bass.IndirectOffsetOnAxis(ap=slot2_i[:, 0, t:t + 1], axis=0),
                                     XN[:, t], None).then_inc(d_scat, 16)
            pool.wait_ge(d_scat, 16 * T)
            for u in range(2):
                pool.wait_ge(ye_out[u], 16 * (E // 2))
            for t in range(T):
                if t >= 8:
                    pool.wait_ge(d_fin, t - 7)
                G.indirect_dma_start(XN[:, 8 + t % 8], None, outs2[:, :],
                                     bass.IndirectOffsetOnAxis(ap=slot2_i[:, 1, t:t + 1], axis=0)).then_inc(dg_in[t % 8], 16)


def shape_constants():
    import numpy as np
    c = np.zeros((P, C_END), np.float32)
    i, j = np.arange(P)[:, None], np.arange(P)[None, :]
    c[:, C_ID:C_ID + P] = i == j
    c[:, C_TRI:C_TRI + P] = i < j
    c[:, C_ONE:C_ONE + P] = 1
    c[:, C_MEAN:C_MEAN + P] = 1 / SEQ
    c[:, C_BD:C_BD + P] = (i // HD == j // HD) / SEQ
    c[:, C_HM:C_HM + HB] = i // HD == np.arange(HB)[None, :]
    e, t = np.arange(E)[:, None], np.arange(T)[None, :]
    c[:, C_W8:C_W8 + E * T] = (E - e + 0 * t).reshape(1, -1)
    c[:, C_J:C_J + NT0] = P * np.arange(NT0)
    c[:, C_ECAP:C_ECAP + E * T] = (CAP * e + 0 * t).reshape(1, -1)
    c[:, C_TRASH:C_TRASH + T] = NS1 + t * P + i
    none = np.full((P, P), -BIG, np.float32)
    own, prev = np.where(j <= i, 0, none), np.where(j > i, 0, none)
    c[:, C_MN:C_MN + 2 * P] = np.concatenate([prev, own], 1)
    c[:, C_MT:C_MT + 2 * P] = np.concatenate([own, none], 1)
    c[:, C_MT + 2 * P:C_MT + 4 * P] = np.concatenate([own, prev], 1)
    inv = (np.float32(1.0) / np.float32(10000.0) ** (np.arange(0, D, 2, dtype=np.float32) / np.float32(D))).astype(np.float32)
    ang = np.arange(SEQ, dtype=np.float32)[:, None] * inv
    return c, np.cos(ang).astype(np.float32), np.sin(ang).astype(np.float32)


def kernel(**inputs):
    import numpy as np
    import concourse.bacc as bacc
    from concourse.bass_utils import run_bass_kernel_spmd

    def arr(name):
        return np.asarray(inputs[name])

    def padded(w):
        return np.concatenate([w, np.zeros((w.shape[0], P - w.shape[1]), w.dtype)], 1)
    c, cos, sin = shape_constants()
    ins = {
        "x": arr("L0_attn_x").reshape(BATCH * SEQ, D),
        "wq": arr("L0_attn_Wq").T, "wk": arr("L0_attn_Wk").T, "wv": arr("L0_attn_Wv").T, "wo": arr("L0_attn_Wo").T,
        "wr": padded(arr("L0_ffn_Wr")), "br": arr("L0_ffn_br"),
        "w1": arr("L0_ffn_W1"), "w3": arr("L0_ffn_W3"), "w2": arr("L0_ffn_W2"),
        "aq": np.concatenate([arr("L1_attn_Wq").T, arr("L1_attn_Wk").T], 1), "av": arr("L1_attn_Wv").T,
        "ab": np.concatenate([arr("L1_attn_bq"), arr("L1_attn_bk"), arr("L1_attn_bv")]),
        "gamma_beta": np.concatenate([arr("L1_attn_gamma"), arr("L1_attn_beta")]),
        "gate_w": padded(arr("L1_ffn_gate_w")), "gate_b": arr("L1_ffn_gate_b"),
        "v1": arr("L1_ffn_w1").reshape(E * D, F1), "b1": arr("L1_ffn_b1").reshape(E, K1, P).transpose(2, 0, 1),
        "v2": arr("L1_ffn_w2").reshape(E * F1, D), "b2": arr("L1_ffn_b2").reshape(E, KD, P).transpose(2, 0, 1),
        "consts": c, "cos": cos, "sin": sin,
    }
    ins = {k: np.ascontiguousarray(v) for k, v in ins.items()}
    nc = bacc.Bacc("TRN2", target_bir_lowering=False, num_devices=1)
    aps = [nc.dram_tensor(f"in_{k}", v.shape, mybir.dt.from_np(v.dtype), kind="ExternalInput").ap() for k, v in ins.items()]
    out = nc.dram_tensor("out_0", (BATCH * SEQ, D), F32, kind="ExternalOutput").ap()
    mixed_model_kernel(nc, *aps, out)
    r = run_bass_kernel_spmd(nc, [{f"in_{k}": v for k, v in ins.items()}], core_ids=[0])
    return r.results[0]["out_0"].reshape(BATCH, SEQ, D)
```

```python
from contextlib import ExitStack

import concourse.bass as bass
from concourse import mybir

F32 = mybir.dt.float32
I32 = mybir.dt.int32
ALU = mybir.AluOpType
ACT = mybir.ActivationFunctionType
AX_X = mybir.AxisListType.X

P = 128
BATCH, SEQ, D = 2, 2048, 256
T = BATCH * SEQ // P
TB = SEQ // P
KD = D // P
HEADS, HD = 16, 16
HB = P // HD
WINDOW = 128
E = 8
F0 = 512
K0 = F0 // P
NT0 = 2 * T + E
F1 = 1024
K1 = F1 // P
CAP = 160
CR = CAP // 2
NS1 = E * CAP
U = 4
BIG = 1e30
QK_SHIFT = 0.21

C_ID = 0
C_TRI = C_ID + P
C_ONE = C_TRI + P
C_MEAN = C_ONE + P
C_BD = C_MEAN + P
C_HM = C_BD + P
C_W8 = C_HM + HB
C_J = C_W8 + E * T
C_ECAP = C_J + NT0
C_TRASH = C_ECAP + E * T
C_MN = C_TRASH + T
C_MT = C_MN + 2 * P
C_END = C_MT + 2 * 2 * P


def mixed_model_kernel(nc, x, wq, wk, wv, wo, wr, br, w1, w3, w2, aq, av, ab, gamma_beta,
                       gate_w, gate_b, v1, b1, v2, b2, consts, cos, sin, out):
    ctx = ExitStack()
    with ctx:
        def sb(name, shape, dt=F32):
            return ctx.enter_context(nc.sbuf_tensor(name, shape, dt))

        def sem(name):
            return ctx.enter_context(nc.semaphore(name))

        X = sb("X", [P, T, D])
        XN = sb("XN", [P, T, D])
        arena = sb("arena", [P, 3, 2 * T * P])
        cst = sb("cst", [P, C_END])
        prob = arena[:, 2, :].rearrange("p (b h k) -> p b h k", b=2, h=HEADS)
        WORK = 6912
        work = sb("work", [P, WORK])
        xn_flat = XN[:, :, :].rearrange("p t n -> p (t n)")

        def cut(at, n, of=work, size=WORK):
            assert at[0] + n <= size
            at[0] += n
            return of[:, at[0] - n:at[0]]
        a = [0]
        q_pad = cut(a, 2 * HEADS * P, xn_flat, T * D).rearrange("p (b h q) -> p b h q", b=2, h=HEADS)
        v_pad = cut(a, U * HEADS * 32, xn_flat, T * D).rearrange("p (s h c) -> p s h c", s=U, h=HEADS)
        k_t = cut(a, KD * U * P, xn_flat, T * D).rearrange("p (g s n) -> p g s n", g=KD, s=U)
        p_t = cut(a, 2 * 4 * P, xn_flat, T * D).rearrange("p (b n) -> p b n", b=2)
        a = [0]
        xnb = cut(a, 2 * D).rearrange("p (b n) -> p b n", b=2)
        xn_t = cut(a, KD * P).rearrange("p (k n) -> p k n", k=KD)
        b = [a[0]]
        c = [a[0]]
        wqkvo = cut(a, 4 * KD * D).rearrange("p (w k n) -> p w k n", w=4, k=KD)
        q_t = cut(a, KD * P).rearrange("p (k n) -> p k n", k=KD)
        rden_x = cut(a, D).rearrange("p (h c) -> p h c", h=HEADS)
        rden_t = cut(a, D)
        o_t = cut(a, D).rearrange("p (k n) -> p k n", k=KD)
        mask0 = cut(a, 2 * P)
        den = sb("den", [P, 2, HEADS])
        nmax = sb("nmax", [P, 2, HEADS])
        rden = sb("rden", [P, HEADS])[:, :]
        w1s = arena[:, 0, :].rearrange("p (e k n) -> p e k n", e=E, k=KD)
        w3s = arena[:, 1, :].rearrange("p (e k n) -> p e k n", e=E, k=KD)
        w2s = arena[:, 2, :].rearrange("p (e k n) -> p e k n", e=E, k=K0)
        xg = cut(b, 4 * D).rearrange("p (b n) -> p b n", b=4)
        xg_t = cut(b, 2 * D).rearrange("p (b k n) -> p b k n", b=2, k=KD)
        gact = cut(b, 2 * F0).rearrange("p (b n) -> p b n", b=2)
        hid = cut(b, 2 * F0).rearrange("p (b n) -> p b n", b=2)
        hid_t = cut(b, 2 * F0).rearrange("p (b k n) -> p b k n", b=2, k=K0)
        yo = cut(b, 2 * D).rearrange("p (b n) -> p b n", b=2)
        yg = XN[:, 0:8, :]
        zrow = sb("zrow", [P, D])[:, :]
        logit = sb("logit", [P, E, T])[:, :, :]
        oh = sb("oh", [P, 2, E, T])
        b = [2 * D + KD * P]
        rt = cut(b, 4 * E * T).rearrange("p (b e t) -> p b e t", b=4, e=E)
        small = sb("small", [P, 16, T])
        ecol = sb("ecol", [P, 4, E])
        ecol_i = sb("ecol_i", [P, 2, E], I32)
        slot_i = sb("slot_i", [P, 2, T], I32)
        slot2_i = sb("slot2_i", [P, 2, T], I32)
        etile = cut(b, NT0 * E).rearrange("p (j e) -> p j e", j=NT0)
        etile_s = sb("etile_s", [P, NT0])[:, :]
        etile_i = sb("etile_i", [P, NT0], I32)[:, :]
        cw = sb("cw", [P, 2, T])
        st = sb("st", [P, T, 6])
        mean = sb("mean", [P, T])[:, :]
        rstd = sb("rstd", [P, T])[:, :]
        lnw = sb("lnw", [P, 4, T])
        qs = arena[:, 0, :].rearrange("p (t n) -> p t n", t=T)
        qr_t = arena[:, 1, :].rearrange("p (t k n) -> p t k n", t=T, k=KD)
        rope_c = arena[:, 2, 0:TB * P].rearrange("p (t n) -> p t n", t=TB)
        rope_s = arena[:, 2, TB * P:2 * TB * P].rearrange("p (t n) -> p t n", t=TB)
        wqk2 = arena[:, 2, 4096:5120].rearrange("p (k n) -> p k n", k=KD)
        wv2 = arena[:, 2, 5120:5632].rearrange("p (k n) -> p k n", k=KD)
        bqkv = arena[:, 2, 5632:6400]
        gab = arena[:, 2, 6400:6912]
        xc_t = cut(c, 2 * D).rearrange("p (b k n) -> p b k n", b=2, k=KD)
        qkb = cut(c, 2 * D)
        qk = cut(c, 4 * D).rearrange("p (b s n) -> p b s n", b=2, s=2)
        vb = cut(c, 2 * D).rearrange("p (b n) -> p b n", b=2)
        ra = cut(c, 2 * D)
        rb = cut(c, 2 * D)
        qkr = cut(c, 4 * D).rearrange("p (b s n) -> p b s n", b=2, s=2)
        kv_bd = cut(c, KD * P).rearrange("p (k n) -> p k n", k=KD)
        kmean = cut(c, D)
        zt = ra.rearrange("p (t n) -> p t n", t=2)
        zd = sb("zd", [P, 2, 2 * HEADS])
        qr_st = [q_.rearrange("p (t k n) -> p t k n", t=2, k=KD) for q_ in (cut(c, 2 * D), rb)]
        v1s = arena[:, 2, 0:4096].rearrange("p (b k n) -> p b k n", b=2, k=KD)
        v2s = arena[:, 2, 4096:8192].rearrange("p (b k n) -> p b k n", b=2, k=K1)
        d = [2 * D + KD * P + 2 * D + 4 * E * T]
        xe = XN[0:CR, 0:4, :].rearrange("p (b r) n -> p b r n", b=2)
        xe_t = cut(d, 2 * KD * CAP).rearrange("p (b k n) -> p b k n", b=2, k=KD)
        he_t = arena[:, 1, 0:2 * K1 * CAP].rearrange("p (b k n) -> p b k n", b=2, k=K1)
        ye_t = arena[:, 1, 4096:4096 + KD * CAP].rearrange("p (k n) -> p k n", k=KD)
        ye = arena[0:CR, 1, 5120:5120 + 4 * D].rearrange("p (b r n) -> p b r n", b=2, r=2)
        b1s = sb("b1s", [P, E, K1])
        b2s = sb("b2s", [P, E, KD])
        wrs = sb("wrs", [P, 2, KD, P])
        rbias = sb("rbias", [P, 2, E])

        ps = ctx.enter_context(nc.psum_tensor("ps", [P, 8, 512], F32))
        rows1 = nc.dram_tensor("slots1", [NT0 * P, D], F32)
        outs1 = nc.dram_tensor("outs1", [NT0 * P, D], F32)
        rows2 = nc.dram_tensor("slots2", [NS1 + T * P, D], F32)
        outs2 = nc.dram_tensor("outs2", [NS1, D], F32)

        ident = cst[:, C_ID:C_ID + P]
        tri = cst[:, C_TRI:C_TRI + P]
        ones = cst[:, C_ONE:C_ONE + P]
        meanm = cst[:, C_MEAN:C_MEAN + P]
        bdm = cst[:, C_BD:C_BD + P]
        hmask = cst[:, C_HM:C_HM + HB]
        w8 = cst[:, C_W8:C_W8 + E * T].rearrange("p (e t) -> p e t", e=E)
        jfirst = cst[:, C_J:C_J + NT0]
        ecap = cst[:, C_ECAP:C_ECAP + E * T].rearrange("p (e t) -> p e t", e=E)
        trash = cst[:, C_TRASH:C_TRASH + T]
        mask_n = cst[:, C_MN:C_MN + 2 * P]
        
        def sems(*names):
            return [sem(n) for n in names]
        (cst_in, x_in, aw_in, rw_in, w13_in, w2_in, zr_set, zr_out, zpad_set) = sems(
            "cst_in", "x_in", "aw_in", "rw_in", "w13_in", "w2_in", "zr_set", "zr_out", "zpad_set")
        ln_st = [sem(f"ln{i}_stats") for i in range(5)]
        ln_fin, ln_std, ln_rstd = sems("ln_fin", "ln_std", "ln_rstd")
        (xn_rdy, xt_done, xnt_rdy, v_done, qk_done, q_evac, k_evac, vpad_rdy, qpad_rdy, s_done, ttr_done,
         p_rdy, pt_done, ptev_a, ptev_d, pv_done, rden_rdy, dt_done, dt_evac, ot_rdy, wo_done,
         x1_rdy, mask_rdy, rden_a) = sems(
            "a_xn_rdy", "a_xt_done", "a_xnt_rdy", "a_v_done", "a_qk_done", "a_q_evac", "a_k_evac",
            "a_vpad_rdy", "a_qpad_rdy", "a_s_done", "a_ttr_done", "a_p_rdy", "a_pt_done",
            "a_ptev_a", "a_ptev_d", "a_pv_done", "a_rden_rdy", "a_dt_done", "a_dt_evac",
            "a_ot_rdy", "a_wo_done", "x1_rdy", "a_mask_rdy", "a_rden")
        (b_xn, b_xt, b_xte, b_lg, b_l, r_oh, r_rank, r_dve, slot_rdy, disp, e_rdy, cw_e,
         xg_in0, xg_in1, xg_in2, xg_in3, xgt, xgte, gu_done, g_act, h_rdy, ht_done, hte, dn_done,
         y_rdy, y_out0, y_out1) = sems(
            "b_xn", "b_xt", "b_xte", "b_lg", "b_l", "r_oh", "r_rank", "r_dve", "slot_rdy", "disp",
            "e_rdy", "cw_e", "xg_in0", "xg_in1", "xg_in2", "xg_in3", "xgt", "xgte",
            "gu_done", "g_act", "h_rdy", "ht_done", "hte", "dn_done", "y_rdy", "y_out0", "y_out1")

        xg_in = [xg_in0, xg_in1, xg_in2, xg_in3]
        y_out = [y_out0, y_out1]
        yg_in = [sem(f"yg_in{i}") for i in range(4)]
        yg_acc = sem("yg_acc")
        (c_in, c_xn, c_xt, c_xte, c_qk, c_v, c_qkb, c_gelu, c_ra, c_rb, c_rope, c_vb,
         c_qrt, c_qrte, c_kvm, c_kve, c_zt, c_zd, c_z, c_o, c_oz, c_res, c_n1, c_x3) = sems(
            "c_in", "c_xn", "c_xt", "c_xte", "c_qk", "c_v", "c_qkb", "c_gelu", "c_ra",
            "c_rb", "c_rope", "c_vb", "c_qrt", "c_qrte", "c_kvm", "c_kve", "c_zt", "c_zd", "c_z",
            "c_o", "c_oz", "c_res", "c_n1", "c_x3")
        (d_xn, d_xt, d_xte, d_lg, d_l, q_oh, q_rank, q_dve, d_slot, d_scat, d_p, d_xt2,
         d_xt2e, d_h, d_g, d_y, d_ye, d_yt, d_yte, d_fin) = sems(
            "d_xn", "d_xt", "d_xte", "d_lg", "d_l", "q_oh", "q_rank", "q_dve", "d_slot", "d_scat",
            "d_p", "d_xt2", "d_xt2e", "d_h", "d_g", "d_y", "d_ye", "d_yt", "d_yte",
            "d_fin")
        (c_qs, c_qst, c_beta, c_zero, c_xn2) = sems("c_qs", "c_qst", "c_beta", "c_zero", "c_xn2")
        s_seen = sem("a_s_seen")
        l_xn = sems("b_xn_kept", "d_xn_kept")
        dw_in = [sem("dw_in0"), sem("dw_in1")]
        xe_in = [sem("xe_in0"), sem("xe_in1")]
        ye_out = [sem("ye_out0"), sem("ye_out1")]
        dg_in = [sem(f"dg_in{i}") for i in range(8)]
        o_out = sem("o_out")

        block = ctx.enter_context(nc.Block())

        def at(buf, t):
            if isinstance(t, int):
                return buf[:, t]
            return buf[:, bass.ds(t, 1)].rearrange("p a n -> p (a n)")

        def batch_steps(eng, bt, step):
            t0 = bt * TB

            def parts(n):
                return n + 2 < TB, n + 1 < TB, n < TB, n > 0
            step(t0, 0, *parts(0))
            with eng.Fori(0, TB // 2 - 2) as i:
                step(i * 2 + (t0 + 1), 1, *parts(1))
                step(i * 2 + (t0 + 2), 0, *parts(2))
            for n in range(TB - 3, TB + 1):
                step(t0 + n, n % 2, *parts(n))

        def key_slots(u):
            lo, hi = (u - 1, u) if u else (0, U - 1)
            return lo, hi

        def mask_of(u):
            return mask_n if u else mask0

        FIRST = 2
        LOOP = (T - 1 - FIRST) // U * U

        def attention_steps(eng, step):
            def parts(s):
                return s + 2 < T, s + 1 < T, s < T, 1 <= s <= T, 2 <= s <= T + 1
            for s in range(FIRST):
                step(s, s % U, *parts(s))
            with eng.Fori(0, LOOP // U) as i:
                for r in range(U):
                    step(i * U + (FIRST + r), (FIRST + r) % U, *parts(FIRST + r))
            for s in range(FIRST + LOOP, T + 2):
                step(s, s % U, *parts(s))

        @block.sync
        def _(sp):
            sp.dma_start(X[:, :, :], x.rearrange("(t p) n -> p t n", p=P)).then_inc(x_in, 16)
            for e in range(E):
                sp.dma_start(w1s[:, e], w1[e].rearrange("(k p) n -> p k n", p=P)).then_inc(w13_in, 16)
                sp.dma_start(w3s[:, e], w3[e].rearrange("(k p) n -> p k n", p=P)).then_inc(w13_in, 16)
            sp.wait_ge(zr_set, 1)
            sp.dma_start(rows1.rearrange("(j p) n -> p j n", p=P),
                         zrow.unsqueeze(1).broadcast_to((P, NT0, D))).then_inc(zr_out, 16)
            sp.dma_start(rows2[0:NS1].rearrange("(j p) n -> p j n", p=P),
                         zrow.unsqueeze(1).broadcast_to((P, NS1 // P, D))).then_inc(zr_out, 16)
            sp.wait_ge(x1_rdy, T)
            for e in range(E):
                sp.dma_start(w2s[:, e], w2[e].rearrange("(k p) n -> p k n", p=P)).then_inc(w2_in, 16)
            sp.wait_ge(disp, 16 * 2 * T)

            def slot_in(j, n, b_):
                sp.dma_start(xg[:, b_], rows1[bass.ds(j * P, P), :]).then_inc(xg_in[b_], 16)

            def out_store(j, done, b_):
                sp.wait_ge(y_rdy, done)
                sp.dma_start(outs1[bass.ds(j * P, P), :], yo[:, b_]).then_inc(y_out[b_], 16)
            for j in range(4):
                slot_in(j, 0, j)
            with sp.Fori(0, NT0 // 4 - 1) as i:
                for u in range(4):
                    sp.wait_ge(xgt, i * 4 + (u + 1))
                    slot_in(i * 4 + (u + 4), 0, u)
                    out_store(i * 4 + u, i * 4 + (u + 1), u % 2)
            for j in range(NT0 - 4, NT0):
                out_store(j, j + 1, j % 2)
            sp.wait_ge(dn_done, NT0)
            sp.dma_start(rope_c, cos.rearrange("(t p) n -> p t n", p=P)).then_inc(c_in, 16)
            sp.dma_start(rope_s, sin.rearrange("(t p) n -> p t n", p=P)).then_inc(c_in, 16)
            sp.dma_start(wqk2, aq.rearrange("(k p) n -> p k n", p=P)).then_inc(c_in, 16)
            sp.dma_start(wv2, av.rearrange("(k p) n -> p k n", p=P)).then_inc(c_in, 16)
            sp.dma_start(bqkv, ab.partition_broadcast(P)).then_inc(c_in, 16)
            sp.dma_start(gab, gamma_beta.partition_broadcast(P)).then_inc(c_in, 16)
            sp.wait_ge(c_x3, T)

            def expert_in(e, b_):
                sp.dma_start(v1s[:, b_], v1[bass.ds(e * D, D), :].rearrange("(k p) n -> p k n", p=P)).then_inc(dw_in[b_], 16)
                sp.dma_start(v2s[:, b_], v2[bass.ds(e * F1, F1), :].rearrange("(k p) n -> p k n", p=P)).then_inc(dw_in[b_], 16)

            def rows_in(e, b_):
                sp.dma_start(xe[:, b_], rows2[bass.ds(e * CAP, CAP), :].rearrange("(r p) n -> p r n", p=CR)).then_inc(xe_in[b_], 16)
            expert_in(0, 0)
            expert_in(1, 1)
            sp.wait_ge(d_scat, 16 * T)
            rows_in(0, 0)
            rows_in(1, 1)
            with sp.Fori(0, E // 2) as i:
                for u in range(2):
                    sp.wait_ge(d_yte, i * 2 + (u + 1))
                    sp.dma_start(outs2[bass.ds(i * (2 * CAP) + u * CAP, CAP), :].rearrange("(r p) n -> p r n", p=CR),
                                 ye[:, u]).then_inc(ye_out[u], 16)
                    nxt = (i * 2 + (u + 2)) % E
                    expert_in(nxt, u)
                    rows_in(nxt, u)
            for u in range(2):
                sp.wait_ge(ye_out[u], 16 * (E // 2))
                sp.wait_ge(dw_in[u], 32 * (E // 2 + 1))
                sp.wait_ge(xe_in[u], 16 * (E // 2 + 1))
            sp.wait_ge(zr_out, 32)
            with sp.Fori(0, T) as t:
                sp.wait_ge(d_fin, t + 1)
                sp.dma_start(out[bass.ds(t * P, P), :], X[:, bass.ds(t, 1), :].rearrange("p a n -> p (a n)")).then_inc(o_out, 16)
            sp.wait_ge(o_out, 16 * T)

        @block.scalar
        def _(act):
            act.dma_start(cst[:, :], consts[:, :]).then_inc(cst_in, 16)
            for n, w in enumerate((wq, wk, wv, wo)):
                act.dma_start(wqkvo[:, n], w.rearrange("(k p) n -> p k n", p=P)).then_inc(aw_in, 16)
            act.dma_start(wrs[:, 0], wr.rearrange("(k p) n -> p k n", p=P)).then_inc(rw_in, 16)
            act.dma_start(wrs[:, 1], gate_w.rearrange("(k p) n -> p k n", p=P)).then_inc(rw_in, 16)
            act.dma_start(rbias[:, 0], br.partition_broadcast(P)).then_inc(rw_in, 16)
            act.dma_start(rbias[:, 1], gate_b.partition_broadcast(P)).then_inc(rw_in, 16)
            act.dma_start(b1s[:, :, :], b1).then_inc(rw_in, 16)
            act.dma_start(b2s[:, :, :], b2).then_inc(rw_in, 16)

            def std(n, lo, hi):
                act.wait_ge(ln_fin, 7 * (n + 1))
                nc.scalar.activation(lnw[:, 3, lo:hi], lnw[:, 2, lo:hi], ACT.Sqrt).then_inc(ln_std, 1)
            std(0, 0, T)
            act.wait_ge(zpad_set, 2)

            def project_evac(t, u):
                act.wait_ge(qk_done, t + 1)
                if not isinstance(t, int) or t > 0:
                    act.wait_ge(qpad_rdy, t)
                nc.scalar.activation(q_t, ps[:, 1, 0:2 * P], ACT.Copy).then_inc(q_evac, 1)
                nc.scalar.activation(k_t[:, :, u, :], ps[:, 1, 2 * P:4 * P].rearrange("p (g n) -> p g n", g=KD),
                                     ACT.Copy).then_inc(k_evac, 1)

            def xnt_evac(t):
                act.wait_ge(xt_done, t + 1)
                if not isinstance(t, int) or t > 0:
                    act.wait_ge(qk_done, t)
                nc.scalar.activation(xn_t, ps[:, 0, 0:D], ACT.Copy).then_inc(xnt_rdy, 1)

            def a_step(s, u, norm_next, project, scores, sums, finish):
                for p in range(HEADS // 2):
                    if project and p == 1:
                        xnt_evac(s + 1)
                    if sums and p % 2 == 0:
                        act.wait_ge(pt_done, (s - 1) * 8 + (p + 1))
                        nc.scalar.activation(p_t[:, 0], ps[:, 4], ACT.Copy).then_inc(ptev_a, 1)
                    if scores:
                        act.wait_ge(ttr_done, s * 8 + (p + 1))
                        if p == 0 and finish:
                            act.wait_ge(rden_a, s - 1)
                        for h in (2 * p, 2 * p + 1):
                            e_ = nc.scalar.activation(prob[:, u % 2, h], prob[:, u % 2, h], ACT.Exp,
                                                      bias=nmax[:, u % 2, h:h + 1], scale=-1.0,
                                                      accum_out=den[:, u % 2, h:h + 1])
                        e_.then_inc(p_rdy, 1)
                    if project and p == 4:
                        project_evac(s + 1, (u + 1) % U)
                    if sums and p == 6:
                        act.wait_ge(dt_done, s + 0)
                        if finish:
                            act.wait_ge(ot_rdy, s - 1)
                        nc.scalar.activation(rden_t, ps[:, 0, 0:D], ACT.Copy).then_inc(dt_evac, 1)
            xnt_evac(0)
            project_evac(0, 0)
            attention_steps(act, a_step)

            std(1, 0, T)
            with act.Fori(0, T) as t:
                act.wait_ge(b_xt, t + 1)
                nc.scalar.activation(xn_t, ps[:, 0, 0:D], ACT.Copy).then_inc(b_xte, 1)
                act.wait_ge(b_lg, t + 1)
            act.wait_ge(cw_e, 1)
            nc.scalar.activation(small[:, 5], small[:, 4], ACT.Exp).then_inc(cw_e, 1)

            def m_step(j, u, load, gu, dn):
                if load:
                    act.wait_ge(xgt, j + 2)
                    nc.scalar.activation(xg_t[:, (u + 1) % 2], ps[:, 0, 0:D], ACT.Copy).then_inc(xgte, 1)
                if dn:
                    act.wait_ge(ht_done, j + 0)
                    nc.scalar.activation(hid_t[:, (u + 1) % 2], ps[:, 5], ACT.Copy).then_inc(hte, 1)
                if gu:
                    act.wait_ge(gu_done, j + 1)
                    nc.scalar.activation(gact[:, u % 2], ps[:, 1 + u % 2], ACT.Silu).then_inc(g_act, 1)
            act.wait_ge(xgt, 1)
            nc.scalar.activation(xg_t[:, 0], ps[:, 0, 0:D], ACT.Copy).then_inc(xgte, 1)
            m_step(0, 0, True, True, False)
            with act.Fori(0, (NT0 - 2) // 2) as i:
                m_step(i * 2 + 1, 1, True, True, True)
                m_step(i * 2 + 2, 0, True, True, True)
            m_step(NT0 - 1, 1, False, True, True)
            m_step(NT0, 0, False, False, True)

            std(2, 0, T)

            def c_xt_evac(t, u):
                act.wait_ge(c_xt, t + 1)
                nc.scalar.activation(xc_t[:, u], ps[:, 0, 0:D], ACT.Copy).then_inc(c_xte, 1)

            def c_step(t, u, transpose, project, activate, add):
                if activate:
                    act.wait_ge(c_qkb, t + 1)
                    if not isinstance(t, int) or t > 1:
                        act.wait_ge(c_kvm, t - 1)
                    nc.scalar.activation(qk[:, u].rearrange("p s n -> p (s n)"), qkb, ACT.Gelu).then_inc(c_gelu, 1)
                    act.wait_ge(c_gelu, t + 1)
                    nc.scalar.activation(at(qs, t), qk[:, u, 0], ACT.Copy, bias=QK_SHIFT).then_inc(c_qs, 1)
                if transpose:
                    c_xt_evac(t + 2, u)
                if add:
                    act.wait_ge(c_qrt, t + 0)
                    nc.scalar.activation(at(arena[:, 1].rearrange("p (t n) -> p t n", t=T), t - 1),
                                         ps[:, 1, 0:D], ACT.Copy).then_inc(c_qrte, 1)
            for bt in range(BATCH):
                c_xt_evac(bt * TB, 0)
                c_xt_evac(bt * TB + 1, 1)
                batch_steps(act, bt, c_step)
                act.wait_ge(c_qrte, (bt + 1) * TB)
                with act.Fori(0, TB // 4) as i:
                    for v in range(2):
                        n = i * 2 + (bt * TB // 2 + v)
                        if v or bt:
                            act.wait_ge(c_o, n - 1)
                        else:
                            act.wait_ge(c_o, i * 2)
                        nc.scalar.activation(qr_st[v].rearrange("p t k n -> p t (k n)"),
                                             arena[:, 1].rearrange("p (t n) -> p t n", t=T)[:, bass.ds(n * 2, 2)],
                                             ACT.Copy).then_inc(c_qst, 1)
                std(3 + bt, bt * TB, bt * TB + TB)
            std(5, 0, T)
            with act.Fori(0, T) as t:
                act.wait_ge(d_xt, t + 1)
                nc.scalar.activation(xn_t, ps[:, 0, 0:D], ACT.Copy).then_inc(d_xte, 1)
                act.wait_ge(d_lg, t + 1)
            act.wait_ge(d_p, 1)
            nc.scalar.activation(rt[:, 1], rt[:, 0], ACT.Exp).then_inc(d_p, 1)
            with act.Fori(0, E // 2) as i:
                for u in range(2):
                    e = i * 2 + u
                    act.wait_ge(d_xt2, e + 1)
                    nc.scalar.activation(xe_t[:, u], ps[:, 0, 0:KD * CAP].rearrange("p (k n) -> p k n", k=KD),
                                         ACT.Copy).then_inc(d_xt2e, 1)
                    for m in range(K1):
                        act.wait_ge(d_h, e * K1 + (m + 1))
                        nc.scalar.activation(he_t[:, u, m], ps[:, 1 + m % 2, 0:CAP], ACT.Gelu_apprx_tanh,
                                             bias=b1s[:, bass.ds(e, 1), m]).then_inc(d_g, 1)
                    act.wait_ge(d_y, e + 1)
                    for m in range(KD):
                        nc.scalar.activation(ye_t[:, m], ps[:, 3 + m, 0:CAP], ACT.Identity,
                                             bias=b2s[:, bass.ds(e, 1), m]).then_inc(d_ye, 1)

        @block.tensor
        def _(pe):
            pe.wait_ge(cst_in, 16)
            pe.wait_ge(aw_in, 64)
            pe.wait_ge(zpad_set, 2)

            def transposes(dst, src, dsem):
                for k in range(KD):
                    m_ = nc.tensor.transpose(dst[:, k * P:(k + 1) * P], src[:, k * P:(k + 1) * P], ident)
                m_.then_inc(dsem, 1)

            def mm(out_, w, m, start=True, stop=True, **kw):
                return nc.tensor.matmul(out_, w, m, start=start, stop=stop, **kw)

            def a_xt(t, v):
                pe.wait_ge(xn_rdy, t + 1)
                if not isinstance(t, int) or t > 0:
                    pe.wait_ge(vpad_rdy, t)
                if not isinstance(t, int) or t > 2:
                    pe.wait_ge(dt_evac, t - 2)
                transposes(ps[:, 0], xnb[:, v], xt_done)

            def a_v(t):
                pe.wait_ge(xnt_rdy, t + 1)
                for k in range(KD):
                    m_ = mm(ps[:, 0, 0:D], xn_t[:, k], wqkvo[:, 2, k], k == 0, k == KD - 1)
                m_.then_inc(v_done, 1)

            def a_qk(t):
                if not isinstance(t, int) or t > 0:
                    pe.wait_ge(k_evac, t)
                for w in range(2):
                    for g in range(KD):
                        for k in range(KD):
                            m_ = mm(ps[:, 1, (2 * w + g) * P:(2 * w + g + 1) * P],
                                    wqkvo[:, w, k, g * P:(g + 1) * P], xn_t[:, k], k == 0, k == KD - 1)
                m_.then_inc(qk_done, 1)

            def a_scores(s, u, p):
                if p == 0:
                    pe.wait_ge(qpad_rdy, s + 1)
                    pe.wait_ge(k_evac, s + 1)
                if not isinstance(s, int) or s > 0 or p > 1:
                    pe.wait_ge(ttr_done, s * 8 + (p - 1))
                lo, hi = key_slots(u)
                for h in (2 * p, 2 * p + 1):
                    m_ = mm(ps[:, 2 + p % 2, (h % 2) * 2 * P:(h % 2 + 1) * 2 * P], q_pad[:, u % 2, h],
                            k_t[:, h // HB, lo:hi + 1:hi - lo, :])
                m_.then_inc(s_done, 1)

            def a_ptrans(t, u, p):
                pe.wait_ge(p_rdy, t * 8 + (p + 1))
                if not isinstance(t, int) or t > 0 or p > 1:
                    pe.wait_ge(ptev_d if p % 2 else ptev_a, t * 4 + p // 2)
                for h in (2 * p, 2 * p + 1):
                    for k in range(2):
                        m_ = nc.tensor.transpose(ps[:, 4 + p % 2, ((h % 2) * 2 + k) * P:((h % 2) * 2 + k + 1) * P],
                                                 prob[:, u % 2, h, k * P:(k + 1) * P], ident)
                m_.then_inc(pt_done, 1)

            def a_pv(t, u, p):
                pe.wait_ge(ptev_d if p % 2 else ptev_a, t * 4 + (p // 2 + 1))
                if p == 0:
                    pe.wait_ge(vpad_rdy, t + 1)
                    if not isinstance(t, int) or t > 1:
                        pe.wait_ge(x1_rdy, t - 1)
                g, r = p // 4, p % 4
                n = 0
                for h in (2 * p, 2 * p + 1):
                    for k, slot in enumerate(key_slots(u)):
                        m_ = mm(ps[32 * r:32 * r + 32, 6 + u % 2, g * P:(g + 1) * P], v_pad[:, slot, h],
                                p_t[:, p % 2, ((h % 2) * 2 + k) * P:((h % 2) * 2 + k + 1) * P], n == 0, n == 3)
                        n += 1
                m_.then_inc(pv_done, 1)

            def a_dt(t):
                pe.wait_ge(rden_rdy, t + 1)
                pe.wait_ge(vpad_rdy, t + 3 if not isinstance(t, int) else min(t + 3, T))
                if isinstance(t, int) and t + 3 > T:
                    pe.wait_ge(dt_evac, t)
                transposes(ps[:, 0], rden_x.rearrange("p h c -> p (h c)"), dt_done)

            def a_wo(t, u):
                pe.wait_ge(ot_rdy, t + 1)
                for k in range(KD):
                    m_ = mm(ps[:, 6 + u % 2, D:2 * D], o_t[:, k], wqkvo[:, 3, k], k == 0, k == KD - 1)
                m_.then_inc(wo_done, 1)

            def a_step(s, u, norm_next, project, scores, sums, finish):
                before, last = (u + U - 1) % U, HEADS // 2 - 1
                for p in range(HEADS // 2):
                    if scores:
                        a_scores(s, u, p)
                    if project and p == 0:
                        a_xt(s + 1, (u + 1) % 2)
                    if sums:
                        a_ptrans(s - 1, before, p)
                        if p:
                            a_pv(s - 1, before, p - 1)
                    if finish and p == 0:
                        a_pv(s - 2, (u + 2) % U, last)
                    if project and p == 2:
                        a_v(s + 1)
                    if project and p == 3:
                        a_qk(s + 1)
                    if finish and p == 4:
                        a_wo(s - 2, u)
                    if sums and p == 5:
                        a_dt(s - 1)
            a_xt(0, 0)
            a_v(0)
            a_qk(0)
            attention_steps(pe, a_step)

            pe.wait_ge(rw_in, 96)
            pe.wait_ge(dt_evac, T)

            def logits(xnr, xt, xte, lg, l, r):
                with pe.Fori(0, T // 2) as i:
                    for u in range(2):
                        t = i * 2 + u
                        pe.wait_ge(xnr, t + 1)
                        transposes(ps[:, 0], xnb[:, u], xt)
                        pe.wait_ge(xte, t + 1)
                        pe.wait_ge(l, t)
                        for k in range(KD):
                            m_ = mm(ps[:, 1, 0:P], xn_t[:, k], wrs[:, r, k], k == 0, k == KD - 1)
                        m_.then_inc(lg, 1)
            logits(b_xn, b_xt, b_xte, b_lg, b_l, 0)

            def ranks(ohs, rank):
                pe.wait_ge(ohs, 1)
                m2 = rt[:, 2].rearrange("p e t -> p (e t)")
                mm(ps[:, 2, 0:E * T], tri, m2)
                mm(ps[:, 3, 0:E * T], ones, m2).then_inc(rank, 1)
            ranks(r_oh, r_rank)

            pe.wait_ge(w13_in, 16 * 2 * E)
            pe.wait_ge(w2_in, 16 * E)
            pe.wait_ge(e_rdy, 1)

            def m_xt(j, q, r):
                pe.wait_ge(xg_in[r], q)
                if not isinstance(j, int) or j > 0:
                    pe.wait_ge(xgte, j)
                transposes(ps[:, 0], xg[:, r], xgt)

            def m_gu(j, u):
                e = pe.value_load(etile_i[0:1, bass.ds(j, 1)], min_val=0, max_val=E - 1)
                pe.wait_ge(xgte, j + 1)
                if not isinstance(j, int) or j > 1:
                    pe.wait_ge(h_rdy, j - 1)
                for w, bank in ((arena[:, 0, :], 1 + u % 2), (arena[:, 1, :], 3 + u % 2)):
                    for k in range(KD):
                        m_ = mm(ps[:, bank], xg_t[:, u % 2, k], w[:, bass.ds(e * (KD * F0) + k * F0, F0)], k == 0, k == KD - 1)
                m_.then_inc(gu_done, 1)

            def m_ht(j, u):
                pe.wait_ge(h_rdy, j + 0)
                if not isinstance(j, int) or j > 1:
                    pe.wait_ge(hte, j - 1)
                for k in range(K0):
                    m_ = nc.tensor.transpose(ps[:, 5, k * P:(k + 1) * P], hid[:, (u + 1) % 2, k * P:(k + 1) * P], ident)
                m_.then_inc(ht_done, 1)

            def m_dn(j, u):
                e = pe.value_load(etile_i[0:1, bass.ds(j - 1, 1)], min_val=0, max_val=E - 1)
                pe.wait_ge(hte, j + 0)
                if not isinstance(j, int) or j > 1:
                    pe.wait_ge(y_rdy, j - 1)
                for k in range(K0):
                    m_ = mm(ps[:, 6, 0:D], hid_t[:, (u + 1) % 2, k],
                            arena[:, 2, bass.ds(e * (K0 * D) + k * D, D)], k == 0, k == K0 - 1)
                m_.then_inc(dn_done, 1)

            def m_step(j, u, count, front, last):
                if front:
                    m_xt(j + 1, count, (u + 1) % 4)
                if not isinstance(j, int) or j > 0:
                    m_ht(j, u)
                if not last:
                    m_gu(j, u)
                if not isinstance(j, int) or j > 0:
                    m_dn(j, u)
            m_xt(0, 16, 0)
            m_step(0, 0, 16, True, False)
            with pe.Fori(0, (NT0 - 4) // 4) as i:
                for u in range(4):
                    m_step(i * 4 + (u + 1), u + 1, i * 16 + 16 * ((u + 2) // 4 + 1), True, False)
            for j in range(NT0 - 3, NT0 + 1):
                m_step(j, j, ((j + 1) // 4 + 1) * 16, j < NT0 - 1, j == NT0)

            pe.wait_ge(c_in, 96)
            pe.wait_ge(y_rdy, NT0)

            def c_transpose(t, u):
                pe.wait_ge(c_xn, t + 1)
                if not isinstance(t, int) or t > 0:
                    pe.wait_ge(c_xte, t)
                transposes(ps[:, 0], xnb[:, u], c_xt)

            def c_project(t, u):
                pe.wait_ge(c_xte, t + 1)
                if not isinstance(t, int) or t > 1:
                    pe.wait_ge(c_qkb, t - 1)
                for k in range(KD):
                    m_ = mm(ps[:, 7 if u else 2], xc_t[:, u, k], wqk2[:, k], k == 0, k == KD - 1)
                m_.then_inc(c_qk, 1)
                if not isinstance(t, int) or t > 0:
                    pe.wait_ge(c_vb, t)
                for k in range(KD):
                    m_ = mm(ps[:, 3, 0:D], xc_t[:, u, k], wv2[:, k], k == 0, k == KD - 1)
                m_.then_inc(c_v, 1)

            def c_step(t, u, transpose, project, activate, add):
                v = (u + 1) % 2
                if project:
                    c_project(t + 1, v)
                if transpose:
                    c_transpose(t + 2, u)
                if add:
                    pe.wait_ge(c_rope, t + 0)
                    pe.wait_ge(c_vb, t + 0)
                    if not isinstance(t, int) or t > 1:
                        pe.wait_ge(c_qrte, t - 1)
                    transposes(ps[:, 1], qkr[:, v, 0], c_qrt)
                    for g in range(KD):
                        mm(ps[:, 4 + g, 0:P], qkr[:, v, 1, g * P:(g + 1) * P], vb[:, v, g * P:(g + 1) * P],
                           False, False, skip_group_check=True)
                    mm(ps[:, 6, 0:D], meanm, qk[:, v, 1], False, False, skip_group_check=True).then_inc(c_kvm, 1)
            for bt in range(BATCH):
                pe.wait_ge(c_zero, bt + 1)
                if bt:
                    pe.wait_ge(c_oz, TB // 2)
                c_transpose(bt * TB, 0)
                c_transpose(bt * TB + 1, 1)
                c_project(bt * TB, 0)
                batch_steps(pe, bt, c_step)
                pe.wait_ge(c_kve, 3 * (bt + 1))
                with pe.Fori(0, TB // 4) as i:
                    for v in range(2):
                        n = i * 2 + (bt * TB // 2 + v)
                        pe.wait_ge(c_qst, n + 1)
                        if v or bt:
                            pe.wait_ge(c_oz, n - 1)
                        else:
                            pe.wait_ge(c_oz, i * 2)
                        for r in range(2):
                            for g in range(KD):
                                m_ = mm(ps[:, 2 if v else 7, r * D + g * P:r * D + (g + 1) * P], qr_st[v][:, r, g], kv_bd[:, g])
                        m_.then_inc(c_o, 1)

            logits(d_xn, d_xt, d_xte, d_lg, d_l, 1)
            ranks(q_oh, q_rank)
            with pe.Fori(0, E // 2) as i:
                for u in range(2):
                    e = i * 2 + u
                    pe.wait_ge(xe_in[u], i * 16 + 16)
                    pe.wait_ge(d_xt2e, e)
                    for k in range(KD):
                        for r in range(2):
                            m_ = nc.tensor.transpose(ps[:, 0, k * CAP + r * CR:k * CAP + (r + 1) * CR],
                                                     xe[:, u, r, k * P:(k + 1) * P], ident[0:CR, 0:CR])
                    m_.then_inc(d_xt2, 1)
                    pe.wait_ge(dw_in[u], i * 32 + 32)
                    pe.wait_ge(d_xt2e, e + 1)
                    for m in range(K1):
                        if m < 2:
                            pe.wait_ge(d_g, e * K1)
                        else:
                            pe.wait_ge(d_g, e * K1 + (m - 1))
                        for k in range(KD):
                            m_ = mm(ps[:, 1 + m % 2, 0:CAP], v1s[:, u, k, m * P:(m + 1) * P], xe_t[:, u, k], k == 0, k == KD - 1)
                        m_.then_inc(d_h, 1)
                    pe.wait_ge(d_g, e * K1 + K1)
                    pe.wait_ge(d_ye, e * KD)
                    for m in range(KD):
                        for k in range(K1):
                            m_ = mm(ps[:, 3 + m, 0:CAP], v2s[:, u, k, m * P:(m + 1) * P], he_t[:, u, k], k == 0, k == K1 - 1)
                    m_.then_inc(d_y, 1)
                    pe.wait_ge(d_ye, e * KD + KD)
                    pe.wait_ge(d_yte, e)
                    for r in range(2):
                        for m in range(KD):
                            m_ = nc.tensor.transpose(ps[0:CR, 5, r * D + m * P:r * D + (m + 1) * P],
                                                     ye_t[:, m, r * CR:(r + 1) * CR], ident)
                    m_.then_inc(d_yt, 1)

        @block.vector
        def _(dve):
            V = nc.vector

            def stats(t, done):
                V.bn_stats(at(st, t), at(X, t)).then_inc(done, 1)

            def finish_stats(n, lo, hi, eps, done, count):
                dve.wait_ge(done, count)
                f = ln_fin
                me, qe, mo, qo = (st[:, lo:hi, k] for k in (1, 2, 4, 5))
                w = [lnw[:, k, lo:hi] for k in range(4)]
                V.tensor_tensor(w[0], me, mo, ALU.add).then_inc(f, 1)
                V.tensor_tensor(w[1], me, mo, ALU.subtract).then_inc(f, 1)
                V.tensor_tensor(w[2], qe, qo, ALU.add).then_inc(f, 1)
                dve.wait_ge(f, 7 * n + 3)
                V.tensor_scalar(mean[:, lo:hi], w[0], 0.5, None, ALU.mult).then_inc(f, 1)
                V.tensor_tensor(w[1], w[1], w[1], ALU.mult).then_inc(f, 1)
                dve.wait_ge(f, 7 * n + 5)
                V.tensor_scalar(w[1], w[1], 0.25, eps, ALU.mult, ALU.add).then_inc(f, 1)
                dve.wait_ge(f, 7 * n + 6)
                V.scalar_tensor_tensor(out=w[2], in0=w[2], scalar=1.0 / D, in1=w[1],
                                       op0=ALU.mult, op1=ALU.add).then_inc(f, 1)
                dve.wait_ge(ln_std, n + 1)
                V.reciprocal(rstd[:, lo:hi], w[3]).then_inc(ln_rstd, 1)
                dve.wait_ge(ln_rstd, n + 1)

            def col(buf, t):
                return buf[:, t:t + 1] if isinstance(t, int) else buf[:, bass.ds(t, 1)]

            def norm(t, dst):
                return V.tensor_scalar(dst, at(X, t), col(mean, t), col(rstd, t), ALU.subtract, ALU.mult)

            dve.wait_ge(x_in, 16)
            with dve.Fori(0, T) as t:
                stats(t, ln_st[0])
            finish_stats(0, 0, T, 1e-5, ln_st[0], T)
            dve.wait_ge(cst_in, 16)
            dve.wait_ge(zpad_set, 2)

            def a_norm(t, u):
                if not isinstance(t, int) or t > 1:
                    dve.wait_ge(xt_done, t - 1)
                norm(t, xnb[:, u % 2]).then_inc(xn_rdy, 1)

            def v_evac(t, u):
                dve.wait_ge(v_done, t + 1)
                dst = v_pad[:, u].rearrange("p (a b) (c d) -> p a (b c) d", b=2, c=2)[:, :, 0:4:3, :]
                V.tensor_copy(dst, ps[:, 0, 0:D].rearrange("p (a b d) -> p a b d", b=2, d=HD)).then_inc(vpad_rdy, 1)

            def a_rden(t, u):
                dve.wait_ge(p_rdy, t * 8 + 8)
                V.reciprocal(rden, den[:, u % 2]).then_inc(rden_a, 1)
                dve.wait_ge(rden_a, t + 1)
                if not isinstance(t, int) or t > 0:
                    dve.wait_ge(dt_done, t)
                V.tensor_copy(rden_x, rden.unsqueeze(2).broadcast_to((P, HEADS, HD))).then_inc(rden_rdy, 1)

            def a_ot(t, u):
                dve.wait_ge(pv_done, t * 8 + 8)
                dve.wait_ge(dt_evac, t + 1)
                if not isinstance(t, int) or t > 0:
                    dve.wait_ge(wo_done, t)
                V.tensor_tensor(o_t.rearrange("p k n -> p (k n)"), ps[:, 6 + u % 2, 0:D], rden_t, ALU.mult).then_inc(ot_rdy, 1)

            def a_x1(t, u):
                dve.wait_ge(wo_done, t + 1)
                V.tensor_tensor(at(X, t), at(X, t), ps[:, 6 + u % 2, D:2 * D], ALU.add).then_inc(x1_rdy, 1)
                dve.wait_ge(x1_rdy, t + 1)
                stats(t, ln_st[1])

            def a_step(s, u, norm_next, project, scores, sums, finish):
                for p in range(HEADS // 2):
                    if scores:
                        dve.wait_ge(s_done, s * 8 + (p + 1))
                        if u == 0 and p == 0:
                            dve.wait_ge(mask_rdy, s // U + 1)
                        dve.sem_inc(s_seen, 1)
                        for h in (2 * p, 2 * p + 1):
                            r_ = V.tensor_tensor_reduce(
                                out=prob[:, u % 2, h], in0=ps[:, 2 + p % 2, (h % 2) * 2 * P:(h % 2 + 1) * 2 * P],
                                in1=mask_of(u), scale=-1.0 / HD ** 0.5, scalar=3e38, op0=ALU.add, op1=ALU.min,
                                accum_out=nmax[:, u % 2, h:h + 1])
                        r_.then_inc(ttr_done, 1)
                    if sums and p % 2:
                        dve.wait_ge(pt_done, (s - 1) * 8 + (p + 1))
                        V.tensor_copy(p_t[:, 1], ps[:, 5]).then_inc(ptev_d, 1)
                    if finish and p == 1:
                        a_ot(s - 2, u)
                    if norm_next and p == 1:
                        a_norm(s + 2, u)
                    if sums and p == 2:
                        a_rden(s - 1, u + 1)
                    if project and p == 3:
                        v_evac(s + 1, (u + 1) % U)
                    if finish and p == 5:
                        a_x1(s - 2, u)
            a_norm(0, 0)
            a_norm(1, 1)
            v_evac(0, 0)
            attention_steps(dve, a_step)

            def router(r, xnr, xt, lg, l, eps_n, done, count):
                finish_stats(eps_n, 0, T, 1e-5, done, count)

                def norm2(t, u):
                    if not isinstance(t, int) or t > 1:
                        dve.wait_ge(xt, t - 1)
                    norm(t, xnb[:, u]).then_inc(xnr, 1)
                    norm(t, at(XN, t)).then_inc(l_xn[r], 1)

                def logit_of(t):
                    dve.wait_ge(lg, t + 1)
                    dst = logit[:, :, t] if isinstance(t, int) else logit[:, :, bass.ds(t, 1)].rearrange("p e a -> p (e a)")
                    V.tensor_tensor(dst, ps[:, 1, 0:E], rbias[:, r], ALU.add).then_inc(l, 1)
                norm2(0, 0)
                with dve.Fori(0, T // 2 - 1) as i:
                    norm2(i * 2 + 1, 1)
                    logit_of(i * 2)
                    norm2(i * 2 + 2, 0)
                    logit_of(i * 2 + 1)
                norm2(T - 1, 1)
                logit_of(T - 2)
                logit_of(T - 1)
                dve.wait_ge(l, T)
            dve.wait_ge(rw_in, 96)
            dve.wait_ge(dt_done, T)
            router(0, b_xn, b_xt, b_lg, b_l, 1, ln_st[1], T)

            class Chain:
                def __init__(self, s_):
                    self.s, self.n = s_, 0

                def __call__(self, ins):
                    self.n += 1
                    ins.then_inc(self.s, 1)
                    dve.wait_ge(self.s, self.n)

            def te(ap):
                return ap.rearrange("p e t -> p t e")

            def over_e(ap):
                return ap.unsqueeze(1).broadcast_to((P, E, T))

            def first_max(do, src, mx, onehot):
                do(V.tensor_reduce(mx, te(src), AX_X, ALU.max))
                do(V.tensor_tensor(rt[:, 0], src, over_e(mx), ALU.is_equal))
                do(V.tensor_tensor(rt[:, 0], rt[:, 0], w8, ALU.mult))
                do(V.tensor_reduce(small[:, 15], te(rt[:, 0]), AX_X, ALU.max))
                do(V.tensor_tensor(onehot, w8, over_e(small[:, 15]), ALU.is_equal))

            def earlier_tiles(do, rank):
                dve.wait_ge(rank, 1)
                do(V.tensor_copy(rt[:, 0].rearrange("p e t -> p (e t)"), ps[:, 3, 0:E * T]))
                for e in range(E):
                    V.tensor_tensor_scan(rt[:, 1, e], ones[:, 0:T], rt[:, 0, e], 0.0, ALU.mult, ALU.add).then_inc(do.s, 1)
                do.n += E
                dve.wait_ge(do.s, do.n)
                do(V.tensor_tensor(rt[:, 3], rt[:, 1], rt[:, 0], ALU.subtract))
                do(V.tensor_tensor(rt[:, 3].rearrange("p e t -> p (e t)"), rt[:, 3].rearrange("p e t -> p (e t)"),
                                   ps[:, 2, 0:E * T], ALU.add))

            do = Chain(r_dve)
            first_max(do, logit, small[:, 0], oh[:, 0])
            do(V.scalar_tensor_tensor(out=rt[:, 1], in0=oh[:, 0], scalar=-3e38, in1=logit[:, :, :], op0=ALU.mult, op1=ALU.add))
            first_max(do, rt[:, 1], small[:, 1], oh[:, 1])
            V.tensor_tensor(rt[:, 2], oh[:, 0], oh[:, 1], ALU.add).then_inc(r_oh, 1)
            V.tensor_tensor(small[:, 4], small[:, 1], small[:, 0], ALU.subtract).then_inc(cw_e, 1)
            earlier_tiles(do, r_rank)
            cnt, cp, ends, base = (ecol[:, k] for k in range(4))
            do(V.tensor_scalar(cnt, rt[:, 1, :, T - 1], float(P - 1), None, ALU.add))
            do(V.tensor_copy(ecol_i[:, 0], cnt))
            do(V.tensor_scalar(ecol_i[:, 1], ecol_i[:, 0], 7, 7, ALU.arith_shift_right, ALU.arith_shift_left))
            do(V.tensor_copy(cp, ecol_i[:, 1]))
            do(V.tensor_tensor_scan(ends, ones[:, 0:E], cp, 0.0, ALU.mult, ALU.add))
            do(V.tensor_tensor(base, ends, cp, ALU.subtract))
            do(V.tensor_tensor(rt[:, 3], rt[:, 3], base.unsqueeze(2).broadcast_to((P, E, T)), ALU.add))
            for k in range(2):
                do(V.tensor_tensor(rt[:, 0], rt[:, 3], oh[:, k], ALU.mult))
                do(V.tensor_reduce(small[:, 6 + k], te(rt[:, 0]), AX_X, ALU.add))
                V.tensor_copy(slot_i[:, k], small[:, 6 + k]).then_inc(slot_rdy, 1)
            do(V.tensor_tensor(etile, ends.unsqueeze(1).broadcast_to((P, NT0, E)),
                               jfirst.unsqueeze(2).broadcast_to((P, NT0, E)), ALU.is_le))
            do(V.tensor_reduce(etile_s, etile, AX_X, ALU.add))
            do(V.tensor_scalar(etile_s, etile_s, float(E - 1), None, ALU.min))
            V.tensor_copy(etile_i, etile_s).then_inc(e_rdy, 1)
            dve.wait_ge(cw_e, 2)
            do(V.tensor_scalar(small[:, 6], small[:, 5], 1.0, None, ALU.add))
            do(V.reciprocal(cw[:, 0], small[:, 6]))
            do(V.tensor_tensor(cw[:, 1], cw[:, 0], small[:, 5], ALU.mult))
            dve.wait_ge(e_rdy, 1)

            def m_step(j, u, count, gu, dn):
                if gu:
                    dve.wait_ge(g_act, j + 1)
                    if not isinstance(j, int) or j > 1:
                        dve.wait_ge(ht_done, j - 1)
                    V.tensor_tensor(hid[:, u % 2], gact[:, u % 2], ps[:, 3 + u % 2], ALU.mult).then_inc(h_rdy, 1)
                if dn:
                    dve.wait_ge(dn_done, j + 0)
                    if not isinstance(j, int) or count > 0:
                        dve.wait_ge(y_out[(u + 1) % 2], count)
                    V.tensor_copy(yo[:, (u + 1) % 2], ps[:, 6, 0:D]).then_inc(y_rdy, 1)
            m_step(0, 0, 0, True, False)
            with dve.Fori(0, (NT0 - 2) // 2) as i:
                m_step(i * 2 + 1, 1, i * 16, True, True)
                m_step(i * 2 + 2, 0, i * 16, True, True)
            m_step(NT0 - 1, 1, (NT0 - 2) // 2 * 16, True, True)
            m_step(NT0, 0, (NT0 - 2) // 2 * 16, False, True)

            dve.wait_ge(r_dve, do.n)
            with dve.Fori(0, T // 4) as i:
                for r in range(4):
                    t = i * 4 + r
                    dve.wait_ge(yg_in[r], i * 32 + 32)
                    for k in range(2):
                        V.scalar_tensor_tensor(out=at(X, t), in0=yg[:, 2 * r + k], scalar=col(cw[:, k], t), in1=at(X, t),
                                               op0=ALU.mult, op1=ALU.add).then_inc(yg_acc, 1)
                        dve.wait_ge(yg_acc, t * 2 + (k + 1))
                    stats(t, ln_st[2])

            finish_stats(2, 0, T, 1e-5, ln_st[2], T)
            dve.wait_ge(c_in, 96)

            def c_norm(t, u):
                if not isinstance(t, int) or t > 1:
                    dve.wait_ge(c_xt, t - 1)
                    dve.wait_ge(c_xn2, t - 1)
                norm(t, xnb[:, u]).then_inc(c_xn, 1)

            def c_step(bt):
                def pairs(ap):
                    return ap.rearrange("p s (n two) -> p s n two", two=2)

                def step(t, u, transpose, project, activate, add):
                    if transpose:
                        c_norm(t + 2, u)
                    if activate:
                        dve.wait_ge(c_qk, t + 1)
                        if not isinstance(t, int) or t > 0:
                            dve.wait_ge(c_gelu, t)
                        V.tensor_tensor(qkb, ps[:, 7 if u else 2], bqkv[:, 0:2 * D], ALU.add).then_inc(c_qkb, 1)
                        dve.wait_ge(c_v, t + 1)
                        if not isinstance(t, int) or t > 1:
                            dve.wait_ge(c_kvm, t - 1)
                        V.tensor_tensor(vb[:, u], ps[:, 3, 0:D], bqkv[:, 2 * D:3 * D], ALU.add).then_inc(c_vb, 1)
                    if add:
                        v = (u + 1) % 2
                        n = t - (bt * TB + 1)
                        dve.wait_ge(c_gelu, t + 0)
                        cosb = at(rope_c, n).unsqueeze(1).broadcast_to((P, 2, P))
                        sinb = at(rope_s, n).unsqueeze(1).broadcast_to((P, 2, P))
                        qp, rp = pairs(qk[:, v]), pairs(qkr[:, v])
                        ra4 = ra.rearrange("p (h s n) -> p h s n", h=2, s=2)
                        rb4 = rb.rearrange("p (h s n) -> p h s n", h=2, s=2)
                        if not isinstance(t, int) or t > 1:
                            dve.wait_ge(c_rope, t - 1)
                        for h in range(2):
                            V.scalar_tensor_tensor(out=ra4[:, h], in0=qp[:, :, :, h], scalar=QK_SHIFT, in1=cosb,
                                                   op0=ALU.add, op1=ALU.mult).then_inc(c_ra, 1)
                            V.scalar_tensor_tensor(out=rb4[:, h], in0=qp[:, :, :, 1 - h], scalar=QK_SHIFT, in1=sinb,
                                                   op0=ALU.add, op1=ALU.mult).then_inc(c_ra, 1)
                        dve.wait_ge(c_ra, t * 4)
                        V.tensor_tensor(rp[:, :, :, 0], ra4[:, 0], rb4[:, 0], ALU.subtract).then_inc(c_rb, 1)
                        V.tensor_tensor(rp[:, :, :, 1], ra4[:, 1], rb4[:, 1], ALU.add).then_inc(c_rope, 1)
                return step

            for bt in range(BATCH):
                for g in range(3):
                    m_ = V.memset(ps[:, 4 + g, 0:D], 0.0)
                m_.then_inc(c_zero, 1)
                c_norm(bt * TB, 0)
                c_norm(bt * TB + 1, 1)
                batch_steps(dve, bt, c_step(bt))
                dve.wait_ge(c_kvm, (bt + 1) * TB)
                for g in range(KD):
                    V.tensor_tensor(kv_bd[:, g], ps[:, 4 + g, 0:P], bdm, ALU.mult).then_inc(c_kve, 1)
                V.tensor_scalar(kmean, ps[:, 6, 0:D], QK_SHIFT, None, ALU.add).then_inc(c_kve, 1)
                dve.wait_ge(c_kve, 3 * (bt + 1))
                dve.wait_ge(c_xn2, (bt + 1) * TB)
                with dve.Fori(0, TB // 4) as i:
                    for v in range(2):
                        n = i * 2 + (bt * TB // 2 + v)
                        dve.wait_ge(c_zt, n + 1)
                        V.tensor_reduce(zd[:, 0], zt.rearrange("p t (h c) -> p (t h) c", h=HEADS), AX_X, ALU.add).then_inc(c_zd, 1)
                        dve.wait_ge(c_zd, n * 2 + 1)
                        V.tensor_scalar(zd[:, 1], zd[:, 0], 1e-6, None, ALU.add).then_inc(c_zd, 1)
                        dve.wait_ge(c_zd, n * 2 + 2)
                        V.reciprocal(zd[:, 0], zd[:, 1]).then_inc(c_z, 1)
                        dve.wait_ge(c_z, n + 1)
                        dve.wait_ge(c_o, n + 1)
                        res = qs[:, bass.ds(n * 2, 2)]
                        V.tensor_tensor(res.rearrange("p t (h c) -> p (t h) c", h=HEADS),
                                        ps[:, 2 if v else 7].rearrange("p (h c) -> p h c", h=2 * HEADS),
                                        zd[:, 0].unsqueeze(2).broadcast_to((P, 2 * HEADS, HD)), ALU.mult).then_inc(c_oz, 1)
                        dve.wait_ge(c_oz, n + 1)
                        V.tensor_tensor(res, res, XN[:, bass.ds(n * 2, 2)], ALU.add).then_inc(c_res, 1)
                        dve.wait_ge(c_res, n + 1)
                        for r in range(2):
                            t = n * 2 + r
                            V.bn_stats(at(st, t), at(qs, t)).then_inc(ln_st[3], 1)
                finish_stats(3 + bt, bt * TB, (bt + 1) * TB, 1e-12, ln_st[3], (bt + 1) * TB)
                dve.wait_ge(c_beta, (bt + 1) * TB)
                with dve.Fori(0, TB // 2) as i:
                    t0 = i * 2 + bt * TB
                    for r in range(2):
                        t = t0 + r
                        V.scalar_tensor_tensor(out=at(qs, t), in0=at(qs, t), scalar=col(mean, t), in1=gab[:, 0:D],
                                               op0=ALU.subtract, op1=ALU.mult).then_inc(c_n1, 1)
                    for r in range(2):
                        t = t0 + r
                        dve.wait_ge(c_n1, t + 1)
                        V.scalar_tensor_tensor(out=at(X, t), in0=at(qs, t), scalar=col(rstd, t), in1=at(X, t),
                                               op0=ALU.mult, op1=ALU.add).then_inc(c_x3, 1)
                    for r in range(2):
                        t = t0 + r
                        dve.wait_ge(c_x3, t + 1)
                        stats(t, ln_st[4])

            router(1, d_xn, d_xt, d_lg, d_l, 5, ln_st[4], T)
            do = Chain(q_dve)
            first_max(do, logit, small[:, 0], oh[:, 0])
            V.tensor_copy(rt[:, 2], oh[:, 0]).then_inc(q_oh, 1)
            V.tensor_tensor(rt[:, 0], logit[:, :, :], over_e(small[:, 0]), ALU.subtract).then_inc(d_p, 1)
            dve.wait_ge(d_p, 2)
            do(V.tensor_reduce(small[:, 2], te(rt[:, 1]), AX_X, ALU.add))
            do(V.reciprocal(small[:, 3], small[:, 2]))
            earlier_tiles(do, q_rank)
            do(V.tensor_tensor(rt[:, 0], rt[:, 3], oh[:, 0], ALU.mult))
            do(V.tensor_reduce(small[:, 6], te(rt[:, 0]), AX_X, ALU.add))
            do(V.tensor_tensor(rt[:, 0], ecap, oh[:, 0], ALU.mult))
            do(V.tensor_reduce(small[:, 7], te(rt[:, 0]), AX_X, ALU.add))
            do(V.tensor_scalar(small[:, 8], small[:, 6], float(CAP), None, ALU.is_lt))
            do(V.tensor_tensor(small[:, 9], small[:, 6], small[:, 7], ALU.add))
            do(V.tensor_tensor(small[:, 10], small[:, 9], small[:, 8], ALU.mult))
            do(V.tensor_tensor(small[:, 11], small[:, 9], trash, ALU.subtract))
            do(V.tensor_tensor(small[:, 11], small[:, 11], small[:, 8], ALU.mult))
            do(V.tensor_tensor(small[:, 11], small[:, 11], trash, ALU.add))
            do(V.tensor_tensor(cw[:, 0], small[:, 3], small[:, 8], ALU.mult))
            V.tensor_copy(slot2_i[:, 0], small[:, 11]).then_inc(d_slot, 1)
            V.tensor_copy(slot2_i[:, 1], small[:, 10]).then_inc(d_slot, 1)
            with dve.Fori(0, E // 2) as i:
                for u in range(2):
                    dve.wait_ge(d_yt, i * 2 + (u + 1))
                    dve.wait_ge(ye_out[u], i * 16)
                    V.tensor_copy(ye[:, u].rearrange("p r n -> p (r n)"), ps[0:CR, 5]).then_inc(d_yte, 1)
            with dve.Fori(0, T // 8) as i:
                for r in range(8):
                    t = i * 8 + r
                    dve.wait_ge(dg_in[r], i * 16 + 16)
                    V.scalar_tensor_tensor(out=at(X, t), in0=XN[:, 8 + r], scalar=col(cw[:, 0], t), in1=at(X, t),
                                           op0=ALU.mult, op1=ALU.add).then_inc(d_fin, 1)

        @block.gpsimd
        def _(pool):
            G = nc.gpsimd
            G.memset(zrow, 0.0).then_inc(zr_set, 1)
            G.memset(k_t[:, :, U - 1], 0.0).then_inc(zpad_set, 1)
            G.memset(v_pad, 0.0).then_inc(zpad_set, 1)
            pool.wait_ge(cst_in, 16)
            G.tensor_copy(mask0, cst[:, C_MT:C_MT + 2 * P]).then_inc(mask_rdy, 1)

            def q_spread(t, v):
                pool.wait_ge(q_evac, t + 1)
                for g in range(KD):
                    g_ = G.tensor_tensor(q_pad[:, v, g * HB:(g + 1) * HB], q_t[:, g].unsqueeze(1).broadcast_to((P, HB, P)),
                                         hmask.unsqueeze(2).broadcast_to((P, HB, P)), ALU.mult)
                g_.then_inc(qpad_rdy, 1)

            def a_step(s, u, norm_next, project, scores, sums, finish):
                if u == 2 and norm_next:
                    pool.wait_ge(ttr_done, (s - 1) * 8)
                    n = ((s + 2) % TB // U + (U - 1)) // U
                    src = cst[:, bass.ds(n * (2 * P) + C_MT, 2 * P)] if not isinstance(n, int) else \
                        cst[:, C_MT + n * 2 * P:C_MT + (n + 1) * 2 * P]
                    G.tensor_copy(mask0, src).then_inc(mask_rdy, 1)
                if project:
                    q_spread(s + 1, (u + 1) % 2)
            q_spread(0, 0)
            attention_steps(pool, a_step)

            pool.wait_ge(zr_out, 32)
            pool.wait_ge(slot_rdy, 2)
            for t in range(T):
                for k in range(2):
                    G.indirect_dma_start(rows1[:, :], bass.IndirectOffsetOnAxis(ap=slot_i[:, k, t:t + 1], axis=0),
                                         XN[:, t], None).then_inc(disp, 16)
            pool.wait_ge(disp, 32 * T)
            pool.wait_ge(y_out0, 16 * (NT0 // 2))
            pool.wait_ge(y_out1, 16 * (NT0 // 2))
            for t in range(T):
                if t >= 4:
                    pool.wait_ge(yg_acc, 2 * (t - 3))
                for k in range(2):
                    G.indirect_dma_start(yg[:, 2 * (t % 4) + k], None, outs1[:, :],
                                         bass.IndirectOffsetOnAxis(ap=slot_i[:, k, t:t + 1], axis=0)).then_inc(yg_in[t % 4], 16)

            pool.wait_ge(c_in, 96)
            for bt in range(BATCH):
                with pool.Fori(0, TB // 2) as i:
                    for u in range(2):
                        t = i * 2 + (bt * TB + u)
                        pool.wait_ge(c_xn, t + 1)
                        G.tensor_copy(at(XN, t), xnb[:, u]).then_inc(c_xn2, 1)
                        G.tensor_tensor(at(X, t), at(X, t), gab[:, D:2 * D], ALU.add).then_inc(c_beta, 1)
                pool.wait_ge(c_kve, 3 * (bt + 1))
                pool.wait_ge(c_qs, (bt + 1) * TB)
                with pool.Fori(0, TB // 2) as i:
                    n = i + bt * TB // 2
                    pool.wait_ge(c_zd, n * 2)
                    G.tensor_tensor(zt, qs[:, bass.ds(n * 2, 2)], kmean.unsqueeze(1).broadcast_to((P, 2, D)),
                                    ALU.mult).then_inc(c_zt, 1)

            pool.wait_ge(d_slot, 2)
            for t in range(T):
                G.indirect_dma_start(rows2[:, :], bass.IndirectOffsetOnAxis(ap=slot2_i[:, 0, t:t + 1], axis=0),
                                     XN[:, t], None).then_inc(d_scat, 16)
            pool.wait_ge(d_scat, 16 * T)
            for u in range(2):
                pool.wait_ge(ye_out[u], 16 * (E // 2))
            for t in range(T):
                if t >= 8:
                    pool.wait_ge(d_fin, t - 7)
                G.indirect_dma_start(XN[:, 8 + t % 8], None, outs2[:, :],
                                     bass.IndirectOffsetOnAxis(ap=slot2_i[:, 1, t:t + 1], axis=0)).then_inc(dg_in[t % 8], 16)


def shape_constants():
    import numpy as np
    c = np.zeros((P, C_END), np.float32)
    i, j = np.arange(P)[:, None], np.arange(P)[None, :]
    c[:, C_ID:C_ID + P] = i == j
    c[:, C_TRI:C_TRI + P] = i < j
    c[:, C_ONE:C_ONE + P] = 1
    c[:, C_MEAN:C_MEAN + P] = 1 / SEQ
    c[:, C_BD:C_BD + P] = (i // HD == j // HD) / SEQ
    c[:, C_HM:C_HM + HB] = i // HD == np.arange(HB)[None, :]
    e, t = np.arange(E)[:, None], np.arange(T)[None, :]
    c[:, C_W8:C_W8 + E * T] = (E - e + 0 * t).reshape(1, -1)
    c[:, C_J:C_J + NT0] = P * np.arange(NT0)
    c[:, C_ECAP:C_ECAP + E * T] = (CAP * e + 0 * t).reshape(1, -1)
    c[:, C_TRASH:C_TRASH + T] = NS1 + t * P + i
    none = np.full((P, P), -BIG, np.float32)
    own, prev = np.where(j <= i, 0, none), np.where(j > i, 0, none)
    c[:, C_MN:C_MN + 2 * P] = np.concatenate([prev, own], 1)
    c[:, C_MT:C_MT + 2 * P] = np.concatenate([own, none], 1)
    c[:, C_MT + 2 * P:C_MT + 4 * P] = np.concatenate([own, prev], 1)
    inv = (np.float32(1.0) / np.float32(10000.0) ** (np.arange(0, D, 2, dtype=np.float32) / np.float32(D))).astype(np.float32)
    ang = np.arange(SEQ, dtype=np.float32)[:, None] * inv
    return c, np.cos(ang).astype(np.float32), np.sin(ang).astype(np.float32)


def kernel(**inputs):
    import numpy as np
    import concourse.bacc as bacc
    from concourse.bass_utils import run_bass_kernel_spmd

    def arr(name):
        return np.asarray(inputs[name])

    def padded(w):
        return np.concatenate([w, np.zeros((w.shape[0], P - w.shape[1]), w.dtype)], 1)
    c, cos, sin = shape_constants()
    ins = {
        "x": arr("L0_attn_x").reshape(BATCH * SEQ, D),
        "wq": arr("L0_attn_Wq").T, "wk": arr("L0_attn_Wk").T, "wv": arr("L0_attn_Wv").T, "wo": arr("L0_attn_Wo").T,
        "wr": padded(arr("L0_ffn_Wr")), "br": arr("L0_ffn_br"),
        "w1": arr("L0_ffn_W1"), "w3": arr("L0_ffn_W3"), "w2": arr("L0_ffn_W2"),
        "aq": np.concatenate([arr("L1_attn_Wq").T, arr("L1_attn_Wk").T], 1), "av": arr("L1_attn_Wv").T,
        "ab": np.concatenate([arr("L1_attn_bq"), arr("L1_attn_bk"), arr("L1_attn_bv")]),
        "gamma_beta": np.concatenate([arr("L1_attn_gamma"), arr("L1_attn_beta")]),
        "gate_w": padded(arr("L1_ffn_gate_w")), "gate_b": arr("L1_ffn_gate_b"),
        "v1": arr("L1_ffn_w1").reshape(E * D, F1), "b1": arr("L1_ffn_b1").reshape(E, K1, P).transpose(2, 0, 1),
        "v2": arr("L1_ffn_w2").reshape(E * F1, D), "b2": arr("L1_ffn_b2").reshape(E, KD, P).transpose(2, 0, 1),
        "consts": c, "cos": cos, "sin": sin,
    }
    ins = {k: np.ascontiguousarray(v) for k, v in ins.items()}
    nc = bacc.Bacc("TRN2", target_bir_lowering=False, num_devices=1)
    aps = [nc.dram_tensor(f"in_{k}", v.shape, mybir.dt.from_np(v.dtype), kind="ExternalInput").ap() for k, v in ins.items()]
    out = nc.dram_tensor("out_0", (BATCH * SEQ, D), F32, kind="ExternalOutput").ap()
    mixed_model_kernel(nc, *aps, out)
    r = run_bass_kernel_spmd(nc, [{f"in_{k}": v for k, v in ins.items()}], core_ids=[0])
    return r.results[0]["out_0"].reshape(BATCH, SEQ, D)
```

```python
from contextlib import ExitStack

import concourse.bass as bass
from concourse import mybir

F32 = mybir.dt.float32
I32 = mybir.dt.int32
ALU = mybir.AluOpType
ACT = mybir.ActivationFunctionType
AX_X = mybir.AxisListType.X

P = 128
BATCH, SEQ, D = 2, 2048, 256
T = BATCH * SEQ // P
TB = SEQ // P
KD = D // P
HEADS, HD = 16, 16
HB = P // HD
WINDOW = 128
assert WINDOW == P
E = 8
F0 = 512
K0 = F0 // P
NT0 = 2 * T + E - 1
REG = T * P + P
NSPARE = NT0 - 2 * T
NROW1 = E * REG + NSPARE * P
GT, NG = 8, T // 8
F1 = 1024
K1 = F1 // P
CAP = 160
CR = CAP // 2
NS1 = E * CAP
FIRST = 2
X_HEAD = FIRST + 2
X_PART = (T - X_HEAD) // FIRST
X_REST = tuple((X_HEAD + n * X_PART, X_HEAD + (n + 1) * X_PART) for n in range(FIRST))
U = 4
BIG = 1e30
QK_SHIFT = 0.21

C_ID = 0
C_TRI = C_ID + P
C_ONE = C_TRI + P
C_MEAN = C_ONE + P
C_BD = C_MEAN + P
C_HM = C_BD + P
C_W8 = C_HM + HB
C_J = C_W8 + E * T
C_ECAP = C_J + NT0
C_TRASH = C_ECAP + E * T
C_LE = C_TRASH + T
C_EROW = C_LE + P
C_MN = C_EROW + E
C_MT = C_MN + 2 * P
C_END = C_MT + 2 * 2 * P


def mixed_model_kernel(nc, x, wq, wk, wv, wo, wr, br, w1, w3, w2, aq, av, ab, gamma_beta,
                       gate_w, gate_b, v1, b1, v2, b2, consts, cos, sin, out):
    ctx = ExitStack()
    with ctx:
        def sb(name, shape, dt=F32):
            return ctx.enter_context(nc.sbuf_tensor(name, shape, dt))

        def sem(name):
            return ctx.enter_context(nc.semaphore(name))

        X = sb("X", [P, T, D])
        XN = sb("XN", [P, T, D])
        arena = sb("arena", [P, 3, 2 * T * P])
        cst = sb("cst", [P, C_END])
        prob = arena[:, 2, :].rearrange("p (b h k) -> p b h k", b=2, h=HEADS)
        WORK = 6912
        work = sb("work", [P, WORK])
        xn_flat = XN[:, :, :].rearrange("p t n -> p (t n)")

        def cut(at, n, of=work, size=WORK):
            assert at[0] + n <= size
            at[0] += n
            return of[:, at[0] - n:at[0]]
        a = [0]
        q_pad = cut(a, 2 * HEADS * P, xn_flat, T * D).rearrange("p (b h q) -> p b h q", b=2, h=HEADS)
        v_pad = cut(a, U * HEADS * 32, xn_flat, T * D).rearrange("p (s h c) -> p s h c", s=U, h=HEADS)
        k_t = cut(a, KD * U * P, xn_flat, T * D).rearrange("p (g s n) -> p g s n", g=KD, s=U)
        p_t = cut(a, 2 * 4 * P, xn_flat, T * D).rearrange("p (b w n) -> p b w n", b=2, w=2)
        a = [0]
        xnb = cut(a, 2 * D).rearrange("p (b n) -> p b n", b=2)
        xn_t = cut(a, KD * P).rearrange("p (k n) -> p k n", k=KD)
        xr_t = [k_.rearrange("p (k n) -> p k n", k=KD) for k_ in (work[:, a[0] - KD * P:a[0]], work[:, WORK - KD * P:])]
        b = [a[0]]
        c = [a[0]]
        wqkvo = cut(a, 4 * KD * D).rearrange("p (w k n) -> p w k n", w=4, k=KD)
        q_t = cut(a, KD * P).rearrange("p (k n) -> p k n", k=KD)
        rden_x = cut(a, D).rearrange("p (h c) -> p h c", h=HEADS)
        rden_t = cut(a, D)
        o_t = cut(a, D).rearrange("p (k n) -> p k n", k=KD)
        mask0 = cut(a, 2 * P)
        vd_pad = cut(a, U * HEADS * 32).rearrange("p (s h c) -> p s h c", s=U, h=HEADS)
        den = sb("den", [P, 2, HEADS])
        nmax = sb("nmax", [P, 2, HEADS])
        rden = sb("rden", [P, HEADS])[:, :]
        w1s = arena[:, 0, :].rearrange("p (e k n) -> p e k n", e=E, k=KD)
        w3s = arena[:, 1, :].rearrange("p (e k n) -> p e k n", e=E, k=KD)
        w2s = arena[:, 2, :].rearrange("p (e k n) -> p e k n", e=E, k=K0)
        xg = cut(b, 4 * D).rearrange("p (b n) -> p b n", b=4)
        xg_t = cut(b, 2 * D).rearrange("p (b k n) -> p b k n", b=2, k=KD)
        gact = cut(b, 2 * F0).rearrange("p (b n) -> p b n", b=2)
        hid = cut(b, 2 * F0).rearrange("p (b n) -> p b n", b=2)
        hid_t = cut(b, 2 * F0).rearrange("p (b k n) -> p b k n", b=2, k=K0)
        yo = cut(b, 2 * D).rearrange("p (b n) -> p b n", b=2)
        yg = XN[:, T - 8:, :]
        zrow = sb("zrow", [P, D])[:, :]
        logit = sb("logit", [P, E, T])[:, :, :]
        oh = sb("oh", [P, 2, E, T])
        b = [2 * D + KD * P]
        rt = cut(b, 4 * E * T).rearrange("p (b e t) -> p b e t", b=4, e=E)
        small = sb("small", [P, 16, T])
        ecol = sb("ecol", [P, 4, E])
        ecol_i = sb("ecol_i", [P, 2, E], I32)
        slot_i = sb("slot_i", [P, 2, T], I32)
        out_i = sb("out_i", [P, 2, T], I32)
        slot2_i = slot_i
        etile = cut(b, NT0 * E).rearrange("p (j e) -> p j e", j=NT0)
        etile_s = sb("etile_s", [P, NT0])[:, :]
        etile_i = sb("etile_i", [P, NT0], I32)[:, :]
        row_i = sb("row_i", [P, NT0], I32)[:, :]
        pad_i = sb("pad_i", [P, E], I32)[:, :]
        cw = sb("cw", [P, 2, T])
        st = sb("st", [P, T, 6])
        mean = sb("mean", [P, T])[:, :]
        rstd = sb("rstd", [P, T])[:, :]
        lnw = sb("lnw", [P, 4, T])
        qs = arena[:, 0, :].rearrange("p (t n) -> p t n", t=T)
        qr_t = arena[:, 1, :].rearrange("p (t n) -> p t n", t=T)
        rope_c = arena[:, 2, 0:TB * P].rearrange("p (t n) -> p t n", t=TB)
        rope_s = arena[:, 2, TB * P:2 * TB * P].rearrange("p (t n) -> p t n", t=TB)
        wqk2 = arena[:, 2, 4096:5120].rearrange("p (k n) -> p k n", k=KD)
        wv2 = arena[:, 2, 5120:5632].rearrange("p (k n) -> p k n", k=KD)
        bqkv = arena[:, 2, 5632:6400]
        gab = arena[:, 2, 6400:6912]
        xc_t = cut(c, 2 * D).rearrange("p (b k n) -> p b k n", b=2, k=KD)
        qkb = cut(c, 2 * D)
        qk = cut(c, 4 * D).rearrange("p (b s n) -> p b s n", b=2, s=2)
        vb = cut(c, 2 * D).rearrange("p (b n) -> p b n", b=2)
        ra = cut(c, 2 * D)
        rb = cut(c, 2 * D)
        qkr = cut(c, 4 * D).rearrange("p (b s n) -> p b s n", b=2, s=2)
        kv_bd = cut(c, KD * P).rearrange("p (k n) -> p k n", k=KD)
        kmean = cut(c, D)
        ksum = cut(c, D)
        zt = ra.rearrange("p (t n) -> p t n", t=2)
        zd = sb("zd", [P, 2, 2 * HEADS])
        qr_st = [q_.rearrange("p (t k n) -> p t k n", t=2, k=KD) for q_ in (cut(c, 2 * D), rb)]
        v1s = arena[:, 2, 0:4096].rearrange("p (b k n) -> p b k n", b=2, k=KD)
        v2s = arena[:, 2, 4096:8192].rearrange("p (b k n) -> p b k n", b=2, k=K1)
        d = [2 * D + KD * P + 2 * D + 4 * E * T]
        xe = XN[0:CR, 0:4, :].rearrange("p (b r) n -> p b r n", b=2)
        xe_t = cut(d, 2 * KD * CAP).rearrange("p (b k n) -> p b k n", b=2, k=KD)
        he_t = arena[:, 1, 0:2 * K1 * CAP].rearrange("p (b k n) -> p b k n", b=2, k=K1)
        ye_t = arena[:, 1, 4096:4096 + KD * CAP].rearrange("p (k n) -> p k n", k=KD)
        ye = arena[0:CR, 1, 5120:5120 + 4 * D].rearrange("p (b r n) -> p b r n", b=2, r=2)
        b1s = sb("b1s", [P, E, K1])
        b2s = sb("b2s", [P, E, KD])
        wrs = sb("wrs", [P, 2, KD, P])
        rbias = sb("rbias", [P, 2, E])

        ps = ctx.enter_context(nc.psum_tensor("ps", [P, 8, 512], F32))
        rows1 = nc.dram_tensor("slots1", [NROW1, D], F32)
        outs1 = nc.dram_tensor("outs1", [NT0 * P, D], F32)
        rows2 = nc.dram_tensor("slots2", [NS1 + T * P, D], F32)
        outs2 = nc.dram_tensor("outs2", [NS1, D], F32)

        ident = cst[:, C_ID:C_ID + P]
        tri = cst[:, C_TRI:C_TRI + P]
        ones = cst[:, C_ONE:C_ONE + P]
        meanm = cst[:, C_MEAN:C_MEAN + P]
        bdm = cst[:, C_BD:C_BD + P]
        hmask = cst[:, C_HM:C_HM + HB]
        w8 = cst[:, C_W8:C_W8 + E * T].rearrange("p (e t) -> p e t", e=E)
        jfirst = cst[:, C_J:C_J + NT0]
        ecap = cst[:, C_ECAP:C_ECAP + E * T].rearrange("p (e t) -> p e t", e=E)
        trash = cst[:, C_TRASH:C_TRASH + T]
        erow = cst[:, C_EROW:C_EROW + E]
        own_keys = cst[:, C_LE:C_LE + P]
        mask_n = cst[:, C_MN:C_MN + 2 * P]

        def sems(*names):
            return [sem(n) for n in names]
        (cst_in, x_head_in, aw_in, rw_in, w13_in, w2_in, zr_set, zr_out, zpad_set) = sems(
            "cst_in", "x_head_in", "aw_in", "rw_in", "w13_in", "w2_in", "zr_set", "zr_out", "zpad_set")
        ln_st = [sem(f"ln{i}_stats") for i in range(5)]
        ln_fin, ln_std, ln_rstd = sems("ln_fin", "ln_std", "ln_rstd")
        (xn_rdy, xt_done, xnt_rdy, v_done, qk_done, q_evac, k_evac, vpad_rdy, qpad_rdy, s_done, ttr_done,
         p_rdy, pt_done, ptev_a, ptev_d, pv_done, rden_rdy, dt_done, dt_evac, ot_rdy, wo_done,
         x1_rdy, mask_rdy, rden_a) = sems(
            "a_xn_rdy", "a_xt_done", "a_xnt_rdy", "a_v_done", "a_qk_done", "a_q_evac", "a_k_evac",
            "a_vpad_rdy", "a_qpad_rdy", "a_s_done", "a_ttr_done", "a_p_rdy", "a_pt_done",
            "a_ptev_a", "a_ptev_d", "a_pv_done", "a_rden_rdy", "a_dt_done", "a_dt_evac",
            "a_ot_rdy", "a_wo_done", "x1_rdy", "a_mask_rdy", "a_rden")
        (b_xn, b_xt, b_xte, b_lg, b_l, r_oh, r_rank, r_dve, slot_rdy, disp, e_rdy, cw_e,
         xg_in0, xg_in1, xg_in2, xg_in3, xgt, xgte, gu_done, g_act, h_rdy, ht_done, hte, dn_done,
         y_rdy, y_out0, y_out1) = sems(
            "b_xn", "b_xt", "b_xte", "b_lg", "b_l", "r_oh", "r_rank", "r_dve", "slot_rdy", "disp",
            "e_rdy", "cw_e", "xg_in0", "xg_in1", "xg_in2", "xg_in3", "xgt", "xgte",
            "gu_done", "g_act", "h_rdy", "ht_done", "hte", "dn_done", "y_rdy", "y_out0", "y_out1")

        xg_in = [xg_in0, xg_in1, xg_in2, xg_in3]
        y_out = [y_out0, y_out1]
        yg_in = [sem(f"yg_in{i}") for i in range(4)]
        yg2_in = sems("yg2_in0", "yg2_in1")
        yg_acc = sem("yg_acc")
        (c_in, c_xn, c_xt, c_xte, c_qk, c_v, c_qkb, c_gelu, c_ra, c_rope, c_vb,
         c_qrt, c_qrte, c_kvm, c_kve, c_zt, c_zd, c_z, c_o, c_oz, c_res, c_n1, c_x3) = sems(
            "c_in", "c_xn", "c_xt", "c_xte", "c_qk", "c_v", "c_qkb", "c_gelu", "c_ra",
            "c_rope", "c_vb", "c_qrt", "c_qrte", "c_kvm", "c_kve", "c_zt", "c_zd", "c_z",
            "c_o", "c_oz", "c_res", "c_n1", "c_x3")
        (d_xn, d_xt, d_xte, d_lg, d_l, q_oh, q_rank, q_dve, d_slot, d_scat, d_p, d_xt2,
         d_xt2e, d_h, d_g, d_y, d_ye, d_yt, d_yte, d_fin) = sems(
            "d_xn", "d_xt", "d_xte", "d_lg", "d_l", "q_oh", "q_rank", "q_dve", "d_slot", "d_scat",
            "d_p", "d_xt2", "d_xt2e", "d_h", "d_g", "d_y", "d_ye", "d_yt", "d_yte",
            "d_fin")
        (c_qs, c_qst, c_beta, c_zero, c_xn2) = sems("c_qs", "c_qst", "c_beta", "c_zero", "c_xn2")
        x_rest_in = [sem(f"x_rest{n}_in") for n in range(FIRST)]
        pad_rdy, pad_out, out_rdy = sems("pad_rdy", "pad_out", "out_rdy")
        p_seen = sem("c_p_seen")
        c_qkm, c_rbm, c_ksum, c_km = sems("c_qkm", "c_rb_products", "c_ksum", "c_km")
        merged = sem("a_merged")
        s_seen = sem("a_s_seen")
        dw_in = [sem("dw_in0"), sem("dw_in1")]
        xe_in = [sem("xe_in0"), sem("xe_in1")]
        ye_out = [sem("ye_out0"), sem("ye_out1")]
        dg_in = [sem(f"dg_in{i}") for i in range(8)]
        o_out = sem("o_out")

        block = ctx.enter_context(nc.Block())

        def at(buf, t):
            if isinstance(t, int):
                return buf[:, t]
            return buf[:, bass.ds(t, 1)].rearrange("p a n -> p (a n)")

        def batch_steps(eng, bt, step):
            t0 = bt * TB

            def parts(n):
                return n + 2 < TB, n + 1 < TB, n < TB, n > 0
            step(t0, 0, *parts(0))
            step(t0 + 1, 1, *parts(1))
            with eng.Fori(0, TB // 4 - 1) as i:
                for r in range(2, 6):
                    step(i * 4 + (t0 + r), r % 2, *parts(2))
            for n in range(TB - 2, TB + 1):
                step(t0 + n, n % 2, *parts(n))

        def pairs(ap):
            return ap.rearrange("p s (n two) -> p s n two", two=2)
        ra4 = ra.rearrange("p (h s n) -> p h s n", h=2, s=2)
        rb4 = rb.rearrange("p (h s n) -> p h s n", h=2, s=2)

        def pair_steps(eng, bt, step):
            n0 = bt * TB // 2
            step(n0, 0)
            step(n0 + 1, 1)
            with eng.Fori(0, TB // 4 - 1) as i:
                for v in range(2):
                    step(i * 2 + (n0 + 2 + v), v)

        D_H = (1, 2, 6, 7)

        def expert_steps(eng, step):
            for e in range(3):
                step(e, e % 2, e == 0, False)
            with eng.Fori(0, E // 2 - 2) as i:
                step(i * 2 + 3, 1, False, False)
                step(i * 2 + 4, 0, False, False)
            step(E - 1, 1, False, True)

        def slot_parts(j):
            return (j + 1 < NT0, j < NT0, j > 0) if isinstance(j, int) else (True, True, True)

        def slot_steps(eng, step, unroll):
            for j in range(3):
                step(j, j % unroll)
            rounds = (NT0 - 1 - 3) // unroll
            with eng.Fori(0, rounds) as i:
                for r in range(3, 3 + unroll):
                    step(i * unroll + r, r % unroll)
            for j in range(3 + rounds * unroll, NT0 + 1):
                step(j, j % unroll)

        def key_slots(u):
            lo, hi = (u - 1, u) if u else (0, U - 1)
            return lo, hi

        def mask_of(u):
            return mask_n if u else mask0

        LOOP = (T - 1 - FIRST) // U * U

        def attention_steps(eng, step, between=(lambda s: None)):
            def parts(s):
                return s + 2 < T, s + 1 < T, s < T, 1 <= s <= T, 2 <= s <= T + 1
            for s in range(FIRST):
                step(s, s % U, *parts(s))
                between(s)
            with eng.Fori(0, LOOP // U) as i:
                for r in range(U):
                    step(i * U + (FIRST + r), (FIRST + r) % U, *parts(FIRST + r))
            for s in range(FIRST + LOOP, T + 2):
                step(s, s % U, *parts(s))

        @block.sync
        def _(sp):
            x_tiles = x.rearrange("(t p) n -> p t n", p=P)
            sp.dma_start(X[:, 0:X_HEAD], x_tiles[:, 0:X_HEAD]).then_inc(x_head_in, 16)
            sp.wait_ge(aw_in, 64)
            for n, (lo, hi) in enumerate(X_REST):
                sp.dma_start(X[:, lo:hi], x_tiles[:, lo:hi]).then_inc(x_rest_in[n], 16)
            sp.wait_ge(x_rest_in[-1], 16)
            for e in range(E):
                sp.dma_start(w1s[:, e], w1[e].rearrange("(k p) n -> p k n", p=P)).then_inc(w13_in, 16)
                sp.dma_start(w3s[:, e], w3[e].rearrange("(k p) n -> p k n", p=P)).then_inc(w13_in, 16)
            sp.wait_ge(zr_set, 1)
            sp.dma_start(rows1[E * REG:NROW1].rearrange("(j p) n -> p j n", p=P),
                         zrow.unsqueeze(1).broadcast_to((P, NSPARE, D))).then_inc(zr_out, 16)
            sp.dma_start(rows2[0:NS1].rearrange("(j p) n -> p j n", p=P),
                         zrow.unsqueeze(1).broadcast_to((P, NS1 // P, D))).then_inc(zr_out, 16)
            sp.wait_ge(x1_rdy, T)
            for e in range(E):
                sp.dma_start(w2s[:, e], w2[e].rearrange("(k p) n -> p k n", p=P)).then_inc(w2_in, 16)
            sp.wait_ge(pad_rdy, 1)
            for e in range(E):
                r = sp.value_load(pad_i[0:1, e:e + 1], min_val=0, max_val=E * REG - P)
                sp.dma_start(rows1[bass.ds(r, P), :], zrow).then_inc(pad_out, 16)
            sp.wait_ge(pad_out, 16 * E)
            sp.wait_ge(e_rdy, 2)
            sp.wait_ge(disp, 16 * 2 * T)

            def slot_in(j, b_):
                r = sp.value_load(row_i[0:1, bass.ds(j, 1)], min_val=0, max_val=NROW1 - P)
                sp.dma_start(xg[:, b_], rows1[bass.ds(r, P), :]).then_inc(xg_in[b_], 16)

            def out_store(j, done, b_):
                sp.wait_ge(y_rdy, done)
                sp.dma_start(outs1[bass.ds(j * P, P), :], yo[:, b_]).then_inc(y_out[b_], 16)
            for j in range(4):
                slot_in(j, j)
            with sp.Fori(0, (NT0 - 4) // 4) as i:
                for u in range(4):
                    sp.wait_ge(xgt, i * 4 + (u + 1))
                    slot_in(i * 4 + (u + 4), u)
                    out_store(i * 4 + u, i * 4 + (u + 1), u % 2)
            for j in range((NT0 - 4) // 4 * 4, NT0):
                if j + 4 < NT0:
                    sp.wait_ge(xgt, j + 1)
                    slot_in(j + 4, j % 4)
                out_store(j, j + 1, j % 2)
            sp.wait_ge(dn_done, NT0)
            sp.dma_start(rope_c, cos.rearrange("(t p) n -> p t n", p=P)).then_inc(c_in, 16)
            sp.dma_start(rope_s, sin.rearrange("(t p) n -> p t n", p=P)).then_inc(c_in, 16)
            sp.dma_start(wqk2, aq.rearrange("(k p) n -> p k n", p=P)).then_inc(c_in, 16)
            sp.dma_start(wv2, av.rearrange("(k p) n -> p k n", p=P)).then_inc(c_in, 16)
            sp.dma_start(bqkv, ab.partition_broadcast(P)).then_inc(c_in, 16)
            sp.dma_start(gab, gamma_beta.partition_broadcast(P)).then_inc(c_in, 16)
            sp.wait_ge(c_x3, T)

            def expert_in(e, b_):
                sp.dma_start(v1s[:, b_], v1[bass.ds(e * D, D), :].rearrange("(k p) n -> p k n", p=P)).then_inc(dw_in[b_], 16)
                sp.dma_start(v2s[:, b_], v2[bass.ds(e * F1, F1), :].rearrange("(k p) n -> p k n", p=P)).then_inc(dw_in[b_], 16)

            def rows_in(e, b_):
                sp.dma_start(xe[:, b_], rows2[bass.ds(e * CAP, CAP), :].rearrange("(r p) n -> p r n", p=CR)).then_inc(xe_in[b_], 16)
            expert_in(0, 0)
            expert_in(1, 1)
            sp.wait_ge(d_scat, 16 * T)
            rows_in(0, 0)
            rows_in(1, 1)

            def outputs(e, u):
                sp.wait_ge(d_yte, e + 1)
                sp.dma_start(outs2[bass.ds(e * CAP, CAP), :].rearrange("(r p) n -> p r n", p=CR), ye[:, u]).then_inc(ye_out[u], 16)

            def d_step(e, u, first, last):
                if not first:
                    outputs(e - 1, 1 - u)
                sp.wait_ge(d_y, e + 1)
                nxt = (e + 2) % E
                rows_in(nxt, u)
                expert_in(nxt, u)
            expert_steps(sp, d_step)
            outputs(E - 1, 1)
            for u in range(2):
                sp.wait_ge(ye_out[u], 16 * (E // 2))
                sp.wait_ge(dw_in[u], 32 * (E // 2 + 1))
                sp.wait_ge(xe_in[u], 16 * (E // 2 + 1))
            sp.wait_ge(zr_out, 32)
            with sp.Fori(0, T) as t:
                sp.wait_ge(d_fin, t + 1)
                sp.dma_start(out[bass.ds(t * P, P), :], X[:, bass.ds(t, 1), :].rearrange("p a n -> p (a n)")).then_inc(o_out, 16)
            sp.wait_ge(o_out, 16 * T)

        @block.scalar
        def _(act):
            act.dma_start(cst[:, :], consts[:, :]).then_inc(cst_in, 16)
            for n, w in enumerate((wq, wk, wv, wo)):
                act.dma_start(wqkvo[:, n], w.rearrange("(k p) n -> p k n", p=P)).then_inc(aw_in, 16)
            act.dma_start(wrs[:, 0], wr.rearrange("(k p) n -> p k n", p=P)).then_inc(rw_in, 16)
            act.dma_start(wrs[:, 1], gate_w.rearrange("(k p) n -> p k n", p=P)).then_inc(rw_in, 16)
            act.dma_start(rbias[:, 0], br.partition_broadcast(P)).then_inc(rw_in, 16)
            act.dma_start(rbias[:, 1], gate_b.partition_broadcast(P)).then_inc(rw_in, 16)
            act.dma_start(b1s[:, :, :], b1).then_inc(rw_in, 16)
            act.dma_start(b2s[:, :, :], b2).then_inc(rw_in, 16)

            def std(n, lo, hi):
                act.wait_ge(ln_fin, 7 * (n + 1))
                nc.scalar.activation(lnw[:, 3, lo:hi], lnw[:, 2, lo:hi], ACT.Sqrt).then_inc(ln_std, 1)
            std(0, 0, X_HEAD)
            act.wait_ge(zpad_set, 3)

            def project_evac(t, u):
                act.wait_ge(qk_done, t + 1)
                if not isinstance(t, int) or t > 0:
                    act.wait_ge(qpad_rdy, t)
                nc.scalar.activation(q_t, ps[:, 1, 0:2 * P], ACT.Copy).then_inc(q_evac, 1)
                nc.scalar.activation(k_t[:, :, u, :], ps[:, 1, 2 * P:4 * P].rearrange("p (g n) -> p g n", g=KD),
                                     ACT.Copy).then_inc(k_evac, 1)

            def xnt_evac(t):
                act.wait_ge(xt_done, t + 1)
                if not isinstance(t, int) or t > 0:
                    act.wait_ge(qk_done, t)
                nc.scalar.activation(xn_t, ps[:, 0, 0:D], ACT.Copy).then_inc(xnt_rdy, 1)

            def a_step(s, u, norm_next, project, scores, sums, finish):
                for p in range(HEADS // 2):
                    if project and p == 1:
                        xnt_evac(s + 1)
                    if sums:
                        act.wait_ge(pt_done, (s - 1) * 8 + (p + 1))
                        nc.scalar.activation(p_t[:, p % 2, 0], ps[:, 4 + p % 2, 0:2 * P], ACT.Copy).then_inc(ptev_a, 1)
                    if scores:
                        act.wait_ge(ttr_done, s * 8 + (p + 1))
                        if p == 0 and finish:
                            act.wait_ge(rden_a, s - 1)
                        for h in (2 * p, 2 * p + 1):
                            e_ = nc.scalar.activation(prob[:, u % 2, h], prob[:, u % 2, h], ACT.Exp,
                                                      bias=nmax[:, u % 2, h:h + 1], scale=-1.0,
                                                      accum_out=den[:, u % 2, h:h + 1])
                        e_.then_inc(p_rdy, 1)
                    if project and p == 4:
                        project_evac(s + 1, (u + 1) % U)
                    if sums and p == 6:
                        act.wait_ge(dt_done, s)
                        if finish:
                            act.wait_ge(ot_rdy, s - 1)
                        nc.scalar.activation(rden_t, ps[:, 0, 0:D], ACT.Copy).then_inc(dt_evac, 1)
            xnt_evac(0)
            project_evac(0, 0)
            attention_steps(act, a_step, lambda s: std(1, X_HEAD, T) if s == FIRST - 1 else None)

            std(2, 0, T)
            def router_evac(xt, xte, lg):
                def evac(t, u):
                    act.wait_ge(xt, t + 1)
                    if not isinstance(t, int) or t > 1:
                        act.wait_ge(lg, t - 1)
                    nc.scalar.activation(xr_t[u], ps[:, 2 * u, 0:D].rearrange("p (k n) -> p k n", k=KD), ACT.Copy).then_inc(xte, 1)
                for t in range(2):
                    evac(t, t)
                with act.Fori(1, T // 2) as i:
                    for u in range(2):
                        evac(i * 2 + u, u)
            router_evac(b_xt, b_xte, b_lg)
            act.wait_ge(cw_e, 1)
            nc.scalar.activation(small[:, 5], small[:, 4], ACT.Exp).then_inc(cw_e, 1)

            def m_step(j, u):
                load, gu, dn = slot_parts(j)
                if load:
                    act.wait_ge(xgt, j + 2)
                    nc.scalar.activation(xg_t[:, (u + 1) % 2], ps[:, 0, 0:D], ACT.Copy).then_inc(xgte, 1)
                if dn:
                    act.wait_ge(ht_done, j)
                    nc.scalar.activation(hid_t[:, (u + 1) % 2], ps[:, 5], ACT.Copy).then_inc(hte, 1)
                if gu:
                    act.wait_ge(gu_done, j + 1)
                    nc.scalar.activation(gact[:, u % 2], ps[:, 1 + u % 2], ACT.Silu).then_inc(g_act, 1)
            act.wait_ge(xgt, 1)
            nc.scalar.activation(xg_t[:, 0], ps[:, 0, 0:D], ACT.Copy).then_inc(xgte, 1)
            slot_steps(act, m_step, 2)

            std(3, 0, TB)

            def c_xt_evac(t, u):
                act.wait_ge(c_xt, t + 1)
                nc.scalar.activation(xc_t[:, u], ps[:, 0, 0:D], ACT.Copy).then_inc(c_xte, 1)
                nc.scalar.activation(at(XN, t), xnb[:, u], ACT.Copy).then_inc(c_xn2, 1)

            def c_step(t, u, transpose, project, activate, add):
                if activate:
                    act.wait_ge(c_qkb, t + 1)
                    if not isinstance(t, int) or t > 1:
                        act.wait_ge(c_ksum, t - 1)
                        act.wait_ge(c_rope, t - 1)
                    qk_ = qk[:, u].rearrange("p s n -> p (s n)")
                    nc.scalar.activation(qk_, qkb, ACT.Gelu).then_inc(c_gelu, 1)
                    act.wait_ge(c_gelu, t + 1)
                    nc.scalar.activation(qk_, qk_, ACT.Copy, bias=QK_SHIFT).then_inc(c_qk, 1)
                    act.wait_ge(c_qk, t + 1)
                    nc.scalar.activation(at(qs, t), qk[:, u, 0], ACT.Copy).then_inc(c_qs, 1)
                if transpose:
                    c_xt_evac(t + 2, u)
                if add:
                    act.wait_ge(c_qrt, t)
                    nc.scalar.activation(at(qr_t, t - 1),
                                         ps[:, 1, 0:D], ACT.Copy).then_inc(c_qrte, 1)
            for bt in range(BATCH):
                c_xt_evac(bt * TB, 0)
                c_xt_evac(bt * TB + 1, 1)
                batch_steps(act, bt, c_step)
                act.wait_ge(c_qrte, (bt + 1) * TB)
                if bt == 0:
                    std(4, TB, T)
                def stage(n, v):
                    if not isinstance(n, int) or n > 1:
                        act.wait_ge(c_o, n - 1)
                    nc.scalar.activation(qr_st[v].rearrange("p t k n -> p t (k n)"),
                                         qr_t[:, bass.ds(n * 2, 2)],
                                         ACT.Copy).then_inc(c_qst, 1)
                pair_steps(act, bt, stage)
                std(5 + bt, bt * TB, bt * TB + TB)
            std(7, 0, T)
            router_evac(d_xt, d_xte, d_lg)
            act.wait_ge(d_p, 1)
            nc.scalar.activation(rt[:, 1], rt[:, 0], ACT.Exp).then_inc(d_p, 1)

            def d_step(e, u, first, last):
                for m in range(K1):
                    act.wait_ge(d_h, e * K1 + (m + 1))
                    nc.scalar.activation(he_t[:, u, m], ps[:, D_H[m % 4], 0:CAP], ACT.Gelu_apprx_tanh,
                                         bias=b1s[:, bass.ds(e, 1), m]).then_inc(d_g, 1)
            expert_steps(act, d_step)

        @block.tensor
        def _(pe):
            pe.wait_ge(cst_in, 16)
            pe.wait_ge(aw_in, 64)
            pe.wait_ge(zpad_set, 3)

            def transposes(dst, src, dsem):
                for k in range(KD):
                    m_ = nc.tensor.transpose(dst[:, k * P:(k + 1) * P], src[:, k * P:(k + 1) * P], ident)
                m_.then_inc(dsem, 1)

            def mm(out_, w, m, start=True, stop=True, **kw):
                return nc.tensor.matmul(out_, w, m, start=start, stop=stop, **kw)

            def a_xt(t, v):
                pe.wait_ge(xn_rdy, t + 1)
                if not isinstance(t, int) or t > 0:
                    pe.wait_ge(vpad_rdy, t)
                if not isinstance(t, int) or t > 2:
                    pe.wait_ge(dt_evac, t - 2)
                transposes(ps[:, 0], xnb[:, v], xt_done)

            def a_v(t):
                pe.wait_ge(xnt_rdy, t + 1)
                for k in range(KD):
                    m_ = mm(ps[:, 0, 0:D], xn_t[:, k], wqkvo[:, 2, k], k == 0, k == KD - 1)
                m_.then_inc(v_done, 1)

            def a_qk(t):
                if not isinstance(t, int) or t > 0:
                    pe.wait_ge(k_evac, t)
                for w in range(2):
                    for g in range(KD):
                        for k in range(KD):
                            m_ = mm(ps[:, 1, (2 * w + g) * P:(2 * w + g + 1) * P],
                                    wqkvo[:, w, k, g * P:(g + 1) * P], xn_t[:, k], k == 0, k == KD - 1)
                m_.then_inc(qk_done, 1)

            def a_scores(s, u, p):
                if p == 0:
                    pe.wait_ge(qpad_rdy, s + 1)
                    pe.wait_ge(k_evac, s + 1)
                if not isinstance(s, int) or s > 0 or p > 1:
                    pe.wait_ge(ttr_done, s * 8 + (p - 1))
                lo, hi = key_slots(u)
                for h in (2 * p, 2 * p + 1):
                    m_ = mm(ps[:, 2 + p % 2, (h % 2) * 2 * P:(h % 2 + 1) * 2 * P], q_pad[:, u % 2, h],
                            k_t[:, h // HB, lo:hi + 1:hi - lo, :])
                m_.then_inc(s_done, 1)

            def a_ptrans(t, u, p):
                pe.wait_ge(merged, t * 8 + (p + 1))
                if not isinstance(t, int) or t > 0 or p > 1:
                    pe.wait_ge(ptev_a, t * 8 + (p - 1))
                for h in (2 * p, 2 * p + 1):
                    m_ = nc.tensor.transpose(ps[:, 4 + p % 2, (h % 2) * P:(h % 2 + 1) * P], prob[:, u % 2, h, 0:P], ident)
                m_.then_inc(pt_done, 1)

            def a_pv(t, u, p):
                pe.wait_ge(ptev_a, t * 8 + (p + 1))
                pe.wait_ge(ptev_d, t * 8 + (p + 1))
                if p == 0:
                    pe.wait_ge(vpad_rdy, t + 1)
                g, r = p // 4, p % 4
                n = 0
                for h in (2 * p, 2 * p + 1):
                    for w, v_ in enumerate((v_pad[:, (u + U - 1) % U, h], vd_pad[:, u, h])):
                        m_ = mm(ps[32 * r:32 * r + 32, 6 + u % 2, g * P:(g + 1) * P], v_,
                                p_t[:, p % 2, w, (h % 2) * P:(h % 2 + 1) * P], n == 0, n == 3)
                        n += 1
                m_.then_inc(pv_done, 1)

            def a_dt(t):
                pe.wait_ge(rden_rdy, t + 1)
                pe.wait_ge(vpad_rdy, t + 3 if not isinstance(t, int) else min(t + 3, T))
                if isinstance(t, int) and t + 3 > T:
                    pe.wait_ge(dt_evac, t)
                transposes(ps[:, 0], rden_x.rearrange("p h c -> p (h c)"), dt_done)

            def a_wo(t, u):
                pe.wait_ge(ot_rdy, t + 1)
                for k in range(KD):
                    m_ = mm(ps[:, 6 + u % 2, D:2 * D], o_t[:, k], wqkvo[:, 3, k], k == 0, k == KD - 1)
                m_.then_inc(wo_done, 1)

            def a_step(s, u, norm_next, project, scores, sums, finish):
                before, last = (u + U - 1) % U, HEADS // 2 - 1
                for p in range(HEADS // 2):
                    if scores:
                        a_scores(s, u, p)
                    if project and p == 0:
                        a_xt(s + 1, (u + 1) % 2)
                    if sums:
                        a_ptrans(s - 1, before, p)
                        if p:
                            a_pv(s - 1, before, p - 1)
                    if finish and p == 0:
                        a_pv(s - 2, (u + 2) % U, last)
                    if project and p == 2:
                        a_v(s + 1)
                    if project and p == 3:
                        a_qk(s + 1)
                    if finish and p == 4:
                        a_wo(s - 2, u)
                    if sums and p == 5:
                        a_dt(s - 1)
            a_xt(0, 0)
            a_v(0)
            a_qk(0)
            attention_steps(pe, a_step)

            pe.wait_ge(rw_in, 96)
            pe.wait_ge(dt_evac, T)

            def ranks(g, ohs, rank):
                pe.wait_ge(ohs, g + 1)
                chosen = rt[:, 2, :, g * GT:(g + 1) * GT]
                mm(ps[:, 4, 0:E * GT].rearrange("p (e t) -> p e t", e=E), tri, chosen)
                mm(ps[:, 5, 0:E * GT].rearrange("p (e t) -> p e t", e=E), ones, chosen).then_inc(rank, 1)

            def logits(xnr, xt, xte, lg, l, r, ohs, rank):
                def turn(t):
                    pe.wait_ge(xnr, t + 1)
                    if t > 1:
                        pe.wait_ge(xte, t - 1)
                    transposes(ps[:, 2 * (t % 2)], XN[:, t], xt)

                turn(0)
                for t in range(T):
                    if t + 1 < T and t != GT - 1:
                        turn(t + 1)
                    pe.wait_ge(xte, t + 1)
                    if t % 4 == 0 and t >= 8:
                        pe.wait_ge(l, t // 4 - 1)
                    for k in range(KD):
                        m_ = mm(ps[:, 1 + 2 * (t // 4 % 2), t % 4 * P:(t % 4 + 1) * P], xr_t[t % 2][:, k], wrs[:, r, k],
                                k == 0, k == KD - 1)
                    m_.then_inc(lg, 1)
                    if t % GT == GT - 1:
                        ranks(t // GT, ohs, rank)
                    if t == GT - 1:
                        turn(t + 1)
            logits(b_xn, b_xt, b_xte, b_lg, b_l, 0, r_oh, r_rank)

            pe.wait_ge(w13_in, 16 * 2 * E)
            pe.wait_ge(w2_in, 16 * E)
            pe.wait_ge(e_rdy, 1)

            def m_xt(j, q, r):
                pe.wait_ge(xg_in[r], q)
                if not isinstance(j, int) or j > 0:
                    pe.wait_ge(xgte, j)
                transposes(ps[:, 0], xg[:, r], xgt)

            def m_gu(j, u):
                e = pe.value_load(etile_i[0:1, bass.ds(j, 1)], min_val=0, max_val=E - 1)
                pe.wait_ge(xgte, j + 1)
                if not isinstance(j, int) or j > 1:
                    pe.wait_ge(h_rdy, j - 1)
                for w, bank in ((arena[:, 0, :], 1 + u % 2), (arena[:, 1, :], 3 + u % 2)):
                    for k in range(KD):
                        m_ = mm(ps[:, bank], xg_t[:, u % 2, k], w[:, bass.ds(e * (KD * F0) + k * F0, F0)], k == 0, k == KD - 1)
                m_.then_inc(gu_done, 1)

            def m_ht(j, u):
                pe.wait_ge(h_rdy, j)
                if not isinstance(j, int) or j > 1:
                    pe.wait_ge(hte, j - 1)
                for k in range(K0):
                    m_ = nc.tensor.transpose(ps[:, 5, k * P:(k + 1) * P], hid[:, (u + 1) % 2, k * P:(k + 1) * P], ident)
                m_.then_inc(ht_done, 1)

            def m_dn(j, u):
                e = pe.value_load(etile_i[0:1, bass.ds(j - 1, 1)], min_val=0, max_val=E - 1)
                pe.wait_ge(hte, j)
                if not isinstance(j, int) or j > 1:
                    pe.wait_ge(y_rdy, j - 1)
                for k in range(K0):
                    m_ = mm(ps[:, 6, 0:D], hid_t[:, (u + 1) % 2, k],
                            arena[:, 2, bass.ds(e * (K0 * D) + k * D, D)], k == 0, k == K0 - 1)
                m_.then_inc(dn_done, 1)

            def m_step(j, u):
                turn, compute, finish = slot_parts(j)
                if turn:
                    m_xt(j + 1, (j + 1) // 4 * 16 + 16 if isinstance(j, int) else (j + (1 - (u + 1) % 4)) * 4 + 16, (u + 1) % 4)
                if finish:
                    m_ht(j, u)
                if compute:
                    m_gu(j, u)
                if finish:
                    m_dn(j, u)
            m_xt(0, 16, 0)
            slot_steps(pe, m_step, 4)

            pe.wait_ge(c_in, 96)
            pe.wait_ge(y_rdy, NT0)

            def c_transpose(t, u):
                pe.wait_ge(c_xn, t + 1)
                if not isinstance(t, int) or t > 0:
                    pe.wait_ge(c_xte, t)
                transposes(ps[:, 0], xnb[:, u], c_xt)

            def c_project(t, u):
                pe.wait_ge(c_xte, t + 1)
                if not isinstance(t, int) or t > 1:
                    pe.wait_ge(c_qkb, t - 1)
                for k in range(KD):
                    m_ = mm(ps[:, 7 if u else 2], xc_t[:, u, k], wqk2[:, k], k == 0, k == KD - 1)
                m_.then_inc(c_qkm, 1)
                if not isinstance(t, int) or t > 0:
                    pe.wait_ge(c_vb, t)
                for k in range(KD):
                    m_ = mm(ps[:, 3, 0:D], xc_t[:, u, k], wv2[:, k], k == 0, k == KD - 1)
                m_.then_inc(c_v, 1)

            def c_step(t, u, transpose, project, activate, add):
                v = (u + 1) % 2
                if project:
                    c_project(t + 1, v)
                if transpose:
                    c_transpose(t + 2, u)
                if add:
                    pe.wait_ge(c_rope, t)
                    pe.wait_ge(c_vb, t)
                    if not isinstance(t, int) or t > 1:
                        pe.wait_ge(c_qrte, t - 1)
                    transposes(ps[:, 1], qkr[:, v, 0], c_qrt)
                    for g in range(KD):
                        m_ = mm(ps[:, 4 + g, 0:P], qkr[:, v, 1, g * P:(g + 1) * P], vb[:, v, g * P:(g + 1) * P],
                                False, False, skip_group_check=True)
                    m_.then_inc(c_kvm, 1)
            for bt in range(BATCH):
                pe.wait_ge(c_zero, bt + 1)
                if bt:
                    pe.wait_ge(c_oz, TB // 2)
                c_transpose(bt * TB, 0)
                c_transpose(bt * TB + 1, 1)
                c_project(bt * TB, 0)
                batch_steps(pe, bt, c_step)
                pe.wait_ge(c_ksum, (bt + 1) * TB)
                mm(ps[:, 6, 0:D], meanm, ksum).then_inc(c_km, 1)
                pe.wait_ge(c_kve, 3 * (bt + 1))

                def apply(n, v):
                    pe.wait_ge(c_qst, n + 1)
                    if not isinstance(n, int) or n > 1:
                        pe.wait_ge(c_oz, n - 1)
                    for r in range(2):
                        for g in range(KD):
                            m_ = mm(ps[:, 2 if v else 7, r * D + g * P:r * D + (g + 1) * P], qr_st[v][:, r, g], kv_bd[:, g])
                    m_.then_inc(c_o, 1)
                pair_steps(pe, bt, apply)

            logits(d_xn, d_xt, d_xte, d_lg, d_l, 1, q_oh, q_rank)

            def d_turn_in(e, u, count):
                pe.wait_ge(xe_in[u], count)
                if not isinstance(e, int) or e > 0:
                    pe.wait_ge(d_xt2e, e)
                for k in range(KD):
                    for r in range(2):
                        m_ = nc.tensor.transpose(ps[:, 0, k * CAP + r * CR:k * CAP + (r + 1) * CR],
                                                 xe[:, u, r, k * P:(k + 1) * P], ident[0:CR, 0:CR])
                m_.then_inc(d_xt2, 1)

            def d_turn_out(e):
                pe.wait_ge(d_ye, e * KD + KD)
                if not isinstance(e, int) or e > 0:
                    pe.wait_ge(d_yte, e)
                for r in range(2):
                    for m in range(KD):
                        m_ = nc.tensor.transpose(ps[0:CR, 5, r * D + m * P:r * D + (m + 1) * P],
                                                 ye_t[:, m, r * CR:(r + 1) * CR], ident)
                m_.then_inc(d_yt, 1)

            def d_step(e, u, first, last):
                pe.wait_ge(dw_in[u], (e - u) * 16 + 32)
                pe.wait_ge(d_xt2e, e + 1)
                for m in range(K1):
                    if not first or m >= 4:
                        pe.wait_ge(d_g, e * K1 + (m - 3))
                    for k in range(KD):
                        m_ = mm(ps[:, D_H[m % 4], 0:CAP], v1s[:, u, k, m * P:(m + 1) * P], xe_t[:, u, k], k == 0, k == KD - 1)
                    m_.then_inc(d_h, 1)
                if not first:
                    d_turn_out(e - 1)
                if not last:
                    d_turn_in(e + 1, 1 - u, (e + u) * 8 + 16)
                pe.wait_ge(d_g, e * K1 + K1)
                if not first:
                    pe.wait_ge(d_ye, e * KD)
                for m in range(KD):
                    for k in range(K1):
                        m_ = mm(ps[:, 3 + m, 0:CAP], v2s[:, u, k, m * P:(m + 1) * P], he_t[:, u, k], k == 0, k == K1 - 1)
                m_.then_inc(d_y, 1)
            d_turn_in(0, 0, 16)
            expert_steps(pe, d_step)
            d_turn_out(E - 1)

        @block.vector
        def _(dve):
            V = nc.vector

            def stats(t, done):
                V.bn_stats(at(st, t), at(X, t)).then_inc(done, 1)

            def finish_stats(n, lo, hi, eps, done, count):
                dve.wait_ge(done, count)
                f = ln_fin
                me, qe, mo, qo = (st[:, lo:hi, k] for k in (1, 2, 4, 5))
                w = [lnw[:, k, lo:hi] for k in range(4)]
                V.tensor_tensor(w[0], me, mo, ALU.add).then_inc(f, 1)
                V.tensor_tensor(w[1], me, mo, ALU.subtract).then_inc(f, 1)
                V.tensor_tensor(w[2], qe, qo, ALU.add).then_inc(f, 1)
                dve.wait_ge(f, 7 * n + 3)
                V.tensor_scalar(mean[:, lo:hi], w[0], 0.5, None, ALU.mult).then_inc(f, 1)
                V.tensor_tensor(w[1], w[1], w[1], ALU.mult).then_inc(f, 1)
                dve.wait_ge(f, 7 * n + 5)
                V.tensor_scalar(w[1], w[1], 0.25, eps, ALU.mult, ALU.add).then_inc(f, 1)
                dve.wait_ge(f, 7 * n + 6)
                V.scalar_tensor_tensor(out=w[2], in0=w[2], scalar=1.0 / D, in1=w[1],
                                       op0=ALU.mult, op1=ALU.add).then_inc(f, 1)
                dve.wait_ge(ln_std, n + 1)
                V.reciprocal(rstd[:, lo:hi], w[3]).then_inc(ln_rstd, 1)
                dve.wait_ge(ln_rstd, n + 1)

            def col(buf, t):
                return buf[:, t:t + 1] if isinstance(t, int) else buf[:, bass.ds(t, 1)]

            def norm(t, dst):
                return V.tensor_scalar(dst, at(X, t), col(mean, t), col(rstd, t), ALU.subtract, ALU.mult)

            dve.wait_ge(x_head_in, 16)
            for t in range(X_HEAD):
                stats(t, ln_st[0])
            finish_stats(0, 0, X_HEAD, 1e-5, ln_st[0], X_HEAD)
            dve.wait_ge(cst_in, 16)
            dve.wait_ge(zpad_set, 3)

            def a_norm(t, u):
                if not isinstance(t, int) or t > 1:
                    dve.wait_ge(xt_done, t - 1)
                norm(t, xnb[:, u % 2]).then_inc(xn_rdy, 1)

            def v_evac(t, u):
                dve.wait_ge(v_done, t + 1)
                def heads(buf):
                    return buf.rearrange("p (a b) (c d) -> p a (b c) d", b=2, c=2)[:, :, 0:4:3, :]
                src = ps[:, 0, 0:D].rearrange("p (a b d) -> p a b d", b=2, d=HD)
                V.tensor_copy(heads(v_pad[:, u]), src)
                V.tensor_tensor(heads(vd_pad[:, u]), src, heads(v_pad[:, (u + U - 1) % U]), ALU.subtract).then_inc(vpad_rdy, 1)

            def a_rden(t, u):
                dve.wait_ge(p_rdy, t * 8 + 8)
                V.reciprocal(rden, den[:, u % 2]).then_inc(rden_a, 1)
                dve.wait_ge(rden_a, t + 1)
                if not isinstance(t, int) or t > 0:
                    dve.wait_ge(dt_done, t)
                V.tensor_copy(rden_x, rden.unsqueeze(2).broadcast_to((P, HEADS, HD))).then_inc(rden_rdy, 1)

            def a_ot(t, u):
                dve.wait_ge(pv_done, t * 8 + 8)
                dve.wait_ge(dt_evac, t + 1)
                V.tensor_tensor(o_t.rearrange("p k n -> p (k n)"), ps[:, 6 + u % 2, 0:D], rden_t, ALU.mult).then_inc(ot_rdy, 1)

            def a_x1(t, u):
                dve.wait_ge(wo_done, t + 1)
                V.tensor_tensor(at(X, t), at(X, t), ps[:, 6 + u % 2, D:2 * D], ALU.add).then_inc(x1_rdy, 1)
                dve.wait_ge(x1_rdy, t + 1)
                stats(t, ln_st[1])

            def a_step(s, u, norm_next, project, scores, sums, finish):
                for p in range(HEADS // 2):
                    if scores:
                        dve.wait_ge(s_done, s * 8 + (p + 1))
                        if u == 0 and p == 0:
                            dve.wait_ge(mask_rdy, s // U + 1)
                        dve.sem_inc(s_seen, 1)
                        for h in (2 * p, 2 * p + 1):
                            r_ = V.tensor_tensor_reduce(
                                out=prob[:, u % 2, h], in0=ps[:, 2 + p % 2, (h % 2) * 2 * P:(h % 2 + 1) * 2 * P],
                                in1=mask_of(u), scale=-1.0 / HD ** 0.5, scalar=3e38, op0=ALU.add, op1=ALU.min,
                                accum_out=nmax[:, u % 2, h:h + 1])
                        r_.then_inc(ttr_done, 1)
                    if sums:
                        dve.wait_ge(ptev_a, (s - 1) * 8 + (p + 1))
                        V.tensor_tensor(p_t[:, p % 2, 1].rearrange("p (h q) -> p h q", h=2),
                                        p_t[:, p % 2, 0].rearrange("p (h q) -> p h q", h=2),
                                        own_keys.unsqueeze(1).broadcast_to((P, 2, P)), ALU.mult).then_inc(ptev_d, 1)
                    if finish and p == 1:
                        a_ot(s - 2, u)
                    if norm_next and p == 1:
                        a_norm(s + 2, u)
                    if sums and p == 2:
                        a_rden(s - 1, u + 1)
                    if project and p == 3:
                        v_evac(s + 1, (u + 1) % U)
                    if finish and p == 5:
                        a_x1(s - 2, u)
            a_norm(0, 0)
            a_norm(1, 1)
            v_evac(0, 0)

            def rest_of_stats(s):
                lo, hi = X_REST[s]
                dve.wait_ge(x_rest_in[s], 16)
                with dve.Fori(0, hi - lo) as t:
                    stats(t + lo, ln_st[0])
                if hi == T:
                    finish_stats(1, X_HEAD, T, 1e-5, ln_st[0], T)
            attention_steps(dve, a_step, rest_of_stats)

            def router(r, xnr, xt, lg, l, eps_n, done, count, route):
                finish_stats(eps_n, 0, T, 1e-5, done, count)

                def norms(g):
                    with dve.Fori(0, GT // 4) as i:
                        for u in range(4):
                            t = i * 4 + (g * GT + u)
                            norm(t, at(XN, t)).then_inc(xnr, 1)
                norms(0)
                for g in range(NG):
                    if 0 < g < NG - 1:
                        norms(g + 1)
                    for q in range(GT // 4):
                        t = g * GT + 4 * q
                        dve.wait_ge(lg, t + 4)
                        V.tensor_tensor(logit[:, :, t:t + 4].rearrange("p e t -> p t e"),
                                        ps[:, 1 + 2 * q].rearrange("p (t n) -> p t n", n=P)[:, :, 0:E],
                                        rbias[:, r].unsqueeze(1).broadcast_to((P, 4, E)), ALU.add).then_inc(l, 1)
                    dve.wait_ge(l, (g + 1) * (GT // 4))
                    route(g)
                    if g == 0:
                        norms(1)
            dve.wait_ge(rw_in, 96)
            dve.wait_ge(dt_done, T)
            class Chain:
                def __init__(self, s_):
                    self.s, self.n = s_, 0

                def __call__(self, ins):
                    self.n += 1
                    ins.then_inc(self.s, 1)
                    dve.wait_ge(self.s, self.n)

            def te(ap):
                return ap.rearrange("p e t -> p t e")

            def over_e(ap):
                return ap.unsqueeze(1).broadcast_to((P, E, GT))

            def of_group(ap, g):
                return ap[..., g * GT:(g + 1) * GT]

            def first_max(do, g, src, mx, onehot):
                w8_, t_, m_ = of_group(w8, g), of_group(rt[:, 0], g), of_group(small[:, 15], g)
                do(V.tensor_reduce(mx, te(src), AX_X, ALU.max))
                do(V.tensor_tensor(t_, src, over_e(mx), ALU.is_equal))
                do(V.tensor_tensor(t_, t_, w8_, ALU.mult))
                do(V.tensor_reduce(m_, te(t_), AX_X, ALU.max))
                do(V.tensor_tensor(onehot, w8_, over_e(m_), ALU.is_equal))

            cnt, cp, ends, base = (ecol[:, k] for k in range(4))

            def places(do, g, rank):
                dve.wait_ge(rank, g + 1)
                in_tile, total, place = (of_group(rt[:, k], g) for k in (0, 1, 3))
                do(V.tensor_copy(in_tile, ps[:, 5, 0:E * GT].rearrange("p (e t) -> p e t", e=E)))
                for e in range(E):
                    V.tensor_tensor_scan(total[:, e], ones[:, 0:GT], in_tile[:, e], 0.0, ALU.mult, ALU.add).then_inc(do.s, 1)
                do.n += E
                dve.wait_ge(do.s, do.n)
                do(V.tensor_tensor(place, total, in_tile, ALU.subtract))
                do(V.tensor_tensor(place, place, ps[:, 4, 0:E * GT].rearrange("p (e t) -> p e t", e=E), ALU.add))
                do(V.tensor_tensor(place, place, base.unsqueeze(2).broadcast_to((P, E, GT)), ALU.add))
                do(V.tensor_tensor(base, base, total[:, :, GT - 1], ALU.add))

            def sum_e(do, g, a_, b_, out_):
                t_ = of_group(rt[:, 0], g)
                do(V.tensor_tensor(t_, a_, b_, ALU.mult))
                do(V.tensor_reduce(out_, te(t_), AX_X, ALU.add))

            def route1(g):
                l_, l2, o0, o1 = (of_group(ap, g) for ap in (logit, rt[:, 1], oh[:, 0], oh[:, 1]))
                first_max(do, g, l_, of_group(small[:, 0], g), o0)
                do(V.scalar_tensor_tensor(out=l2, in0=o0, scalar=-3e38, in1=l_, op0=ALU.mult, op1=ALU.add))
                first_max(do, g, l2, of_group(small[:, 1], g), o1)
                V.tensor_tensor(of_group(rt[:, 2], g), o0, o1, ALU.add).then_inc(r_oh, 1)
                places(do, g, r_rank)
                for k in range(2):
                    s_ = of_group(small[:, 6 + k], g)
                    sum_e(do, g, of_group(rt[:, 3], g), of_group(oh[:, k], g), s_)
                    V.tensor_copy(of_group(slot_i[:, k], g), s_).then_inc(slot_rdy, 1)
            do = Chain(r_dve)
            do(V.tensor_copy(base, erow))
            router(0, b_xn, b_xt, b_lg, b_l, 2, ln_st[1], T, route1)
            V.tensor_tensor(small[:, 4], small[:, 1], small[:, 0], ALU.subtract).then_inc(cw_e, 1)
            V.tensor_copy(pad_i, base).then_inc(pad_rdy, 1)
            do(V.tensor_tensor(cnt, base, erow, ALU.subtract))
            do(V.tensor_scalar(cnt, cnt, float(P - 1), None, ALU.add))
            do(V.tensor_copy(ecol_i[:, 0], cnt))
            do(V.tensor_scalar(ecol_i[:, 1], ecol_i[:, 0], 7, 7, ALU.arith_shift_right, ALU.arith_shift_left))
            do(V.tensor_copy(cp, ecol_i[:, 1]))
            do(V.tensor_tensor_scan(ends, ones[:, 0:E], cp, 0.0, ALU.mult, ALU.add))
            do(V.tensor_scalar(cnt, cp, -1.0, float(REG), ALU.mult, ALU.add))
            do(V.tensor_tensor(etile, ends.unsqueeze(1).broadcast_to((P, NT0, E)),
                               jfirst.unsqueeze(2).broadcast_to((P, NT0, E)), ALU.is_le))
            do(V.tensor_reduce(etile_s, etile, AX_X, ALU.add))
            do(V.tensor_scalar(etile_s, etile_s, float(E - 1), None, ALU.min))
            do(V.tensor_tensor(etile, etile, cnt.unsqueeze(1).broadcast_to((P, NT0, E)), ALU.mult))
            V.tensor_copy(etile_i, etile_s).then_inc(e_rdy, 1)
            dve.wait_ge(e_rdy, 1)
            do(V.tensor_reduce(etile_s, etile, AX_X, ALU.add))
            do(V.tensor_tensor(etile_s, etile_s, jfirst, ALU.add))
            V.tensor_copy(row_i, etile_s).then_inc(e_rdy, 1)
            dve.wait_ge(cw_e, 2)
            do(V.tensor_scalar(small[:, 8], small[:, 5], 1.0, None, ALU.add))
            do(V.reciprocal(cw[:, 0], small[:, 8]))
            do(V.tensor_tensor(cw[:, 1], cw[:, 0], small[:, 5], ALU.mult))
            do(V.tensor_tensor(cnt, cp, ends, ALU.subtract))
            do(V.tensor_tensor(cnt, cnt, erow, ALU.add))
            for k in range(2):
                do(V.tensor_tensor(oh[:, k], oh[:, k], cnt.unsqueeze(2).broadcast_to((P, E, T)), ALU.mult))
                do(V.tensor_reduce(small[:, 12], te(oh[:, k]), AX_X, ALU.add))
                do(V.tensor_tensor(small[:, 6 + k], small[:, 6 + k], small[:, 12], ALU.subtract))
                V.tensor_copy(out_i[:, k], small[:, 6 + k]).then_inc(out_rdy, 1)
            dve.wait_ge(e_rdy, 2)
            dve.wait_ge(out_rdy, 2)

            def m_step(j, u):
                _, gu, dn = slot_parts(j)
                if gu:
                    dve.wait_ge(g_act, j + 1)
                    if not isinstance(j, int) or j > 1:
                        dve.wait_ge(ht_done, j - 1)
                    V.tensor_tensor(hid[:, u % 2], gact[:, u % 2], ps[:, 3 + u % 2], ALU.mult).then_inc(h_rdy, 1)
                if dn:
                    v = (u + 1) % 2
                    dve.wait_ge(dn_done, j)
                    if not isinstance(j, int) or j > 2:
                        dve.wait_ge(y_out[v], (j - (1 + v)) * 8)
                    V.tensor_copy(yo[:, v], ps[:, 6, 0:D]).then_inc(y_rdy, 1)
            slot_steps(dve, m_step, 2)

            dve.wait_ge(r_dve, do.n)

            def combine(t, r, filled, count):
                dve.wait_ge(filled, count)
                for k in range(2):
                    V.scalar_tensor_tensor(out=at(X, t), in0=yg[:, 2 * r + k], scalar=col(cw[:, k], t), in1=at(X, t),
                                           op0=ALU.mult, op1=ALU.add).then_inc(yg_acc, 1)
                    dve.wait_ge(yg_acc, t * 2 + (k + 1))
                stats(t, ln_st[2])
            with dve.Fori(0, TB // 4) as i:
                for r in range(4):
                    combine(i * 4 + r, r, yg_in[r], i * 32 + 32)

            finish_stats(3, 0, TB, 1e-5, ln_st[2], TB)
            dve.wait_ge(c_in, 96)

            def c_norm(t, u):
                if not isinstance(t, int) or t > 1:
                    dve.wait_ge(c_xt, t - 1)
                    dve.wait_ge(c_xn2, t - 1)
                norm(t, xnb[:, u]).then_inc(c_xn, 1)

            def normed_result(t):
                V.scalar_tensor_tensor(out=at(qs, t), in0=at(qs, t), scalar=col(mean, t), in1=gab[:, 0:D],
                                       op0=ALU.subtract, op1=ALU.mult).then_inc(c_n1, 1)

            def add_normed(t):
                dve.wait_ge(c_n1, t + 1)
                V.scalar_tensor_tensor(out=at(X, t), in0=at(qs, t), scalar=col(rstd, t), in1=at(X, t),
                                       op0=ALU.mult, op1=ALU.add).then_inc(c_x3, 1)

            def next_stats(t):
                dve.wait_ge(c_x3, t + 1)
                stats(t, ln_st[4])

            def c_step(bt):
                def step(t, u, transpose, project, activate, add):
                    if transpose:
                        c_norm(t + 2, u)
                    if activate:
                        dve.wait_ge(c_qkm, t + 1)
                        if not isinstance(t, int) or t > 0:
                            dve.wait_ge(c_gelu, t)
                        V.tensor_tensor(qkb, ps[:, 7 if u else 2], bqkv[:, 0:2 * D], ALU.add).then_inc(c_qkb, 1)
                        dve.wait_ge(c_v, t + 1)
                        if not isinstance(t, int) or t > 1:
                            dve.wait_ge(c_kvm, t - 1)
                        V.tensor_tensor(vb[:, u], ps[:, 3, 0:D], bqkv[:, 2 * D:3 * D], ALU.add).then_inc(c_vb, 1)
                    if activate and bt == 0:
                        combine(t + TB, u, yg2_in[u], (t - u) * 16 + 32)
                    if add:
                        v = (u + 1) % 2
                        n = t - (bt * TB + 1)
                        dve.wait_ge(c_qk, t)
                        cosb = at(rope_c, n).unsqueeze(1).broadcast_to((P, 2, P))
                        qp, rp = pairs(qk[:, v]), pairs(qkr[:, v])
                        if not isinstance(t, int) or t > 1:
                            dve.wait_ge(c_rope, t - 1)
                        for h in range(2):
                            V.tensor_tensor(ra4[:, h], qp[:, :, :, h], cosb, ALU.mult).then_inc(c_ra, 1)
                        dve.wait_ge(c_ra, t * 2)
                        dve.wait_ge(c_rbm, t * 2)
                        V.tensor_tensor(rp[:, :, :, 0], ra4[:, 0], rb4[:, 0], ALU.subtract)
                        V.tensor_tensor(rp[:, :, :, 1], ra4[:, 1], rb4[:, 1], ALU.add).then_inc(c_rope, 1)
                    if activate and bt == 1:
                        for part in (normed_result, add_normed, next_stats):
                            part(t - TB)
                return step

            for bt in range(BATCH):
                for g in range(KD):
                    m_ = V.memset(ps[:, 4 + g, 0:P], 0.0)
                m_.then_inc(c_zero, 1)
                c_norm(bt * TB, 0)
                c_norm(bt * TB + 1, 1)
                batch_steps(dve, bt, c_step(bt))
                if bt == 0:
                    finish_stats(4, TB, T, 1e-5, ln_st[2], T)
                dve.wait_ge(c_kvm, (bt + 1) * TB)
                for g in range(KD):
                    V.tensor_tensor(kv_bd[:, g], ps[:, 4 + g, 0:P], bdm, ALU.mult).then_inc(c_kve, 1)
                dve.wait_ge(c_km, bt + 1)
                V.tensor_copy(kmean, ps[:, 6, 0:D]).then_inc(c_kve, 1)
                dve.wait_ge(c_kve, 3 * (bt + 1))
                dve.wait_ge(c_xn2, (bt + 1) * TB)

                def result(n, v):
                    dve.wait_ge(c_zt, n + 1)
                    V.tensor_reduce(zd[:, 0], zt.rearrange("p t (h c) -> p (t h) c", h=HEADS), AX_X, ALU.add).then_inc(c_zd, 1)
                    dve.wait_ge(c_zd, n * 2 + 1)
                    V.tensor_scalar(zd[:, 1], zd[:, 0], 1e-6, None, ALU.add).then_inc(c_zd, 1)
                    dve.wait_ge(c_zd, n * 2 + 2)
                    V.reciprocal(zd[:, 0], zd[:, 1]).then_inc(c_z, 1)
                    dve.wait_ge(c_z, n + 1)
                    dve.wait_ge(c_o, n + 1)
                    res = qs[:, bass.ds(n * 2, 2)]
                    V.tensor_tensor(res.rearrange("p t (h c) -> p (t h) c", h=HEADS),
                                    ps[:, 2 if v else 7].rearrange("p (h c) -> p h c", h=2 * HEADS),
                                    zd[:, 0].unsqueeze(2).broadcast_to((P, 2 * HEADS, HD)), ALU.mult).then_inc(c_oz, 1)
                    dve.wait_ge(c_oz, n + 1)
                    V.tensor_tensor(res, res, XN[:, bass.ds(n * 2, 2)], ALU.add).then_inc(c_res, 1)
                    dve.wait_ge(c_res, n + 1)
                    for r in range(2):
                        t = n * 2 + r
                        V.bn_stats(at(st, t), at(qs, t)).then_inc(ln_st[3], 1)
                pair_steps(dve, bt, result)
                finish_stats(5 + bt, bt * TB, (bt + 1) * TB, 1e-12, ln_st[3], (bt + 1) * TB)
                dve.wait_ge(c_beta, (bt + 1) * TB // 2)
            with dve.Fori(0, TB // 4) as i:
                for part in (normed_result, add_normed, next_stats):
                    for r in range(4):
                        part(i * 4 + (TB + r))

            do = Chain(q_dve)

            def route2(g):
                o_, place = of_group(oh[:, 0], g), of_group(rt[:, 3], g)
                n_, first, kept, slot, read, write = (of_group(small[:, k], g) for k in (6, 7, 8, 9, 10, 11))
                trash_ = of_group(trash, g)
                first_max(do, g, of_group(logit, g), of_group(small[:, 0], g), o_)
                V.tensor_copy(of_group(rt[:, 2], g), o_).then_inc(q_oh, 1)
                places(do, g, q_rank)
                sum_e(do, g, place, o_, n_)
                sum_e(do, g, of_group(ecap, g), o_, first)
                do(V.tensor_scalar(kept, n_, float(CAP), None, ALU.is_lt))
                do(V.tensor_tensor(slot, n_, first, ALU.add))
                do(V.tensor_tensor(read, slot, kept, ALU.mult))
                do(V.tensor_tensor(write, slot, trash_, ALU.subtract))
                do(V.tensor_tensor(write, write, kept, ALU.mult))
                do(V.tensor_tensor(write, write, trash_, ALU.add))
                V.tensor_copy(of_group(slot2_i[:, 0], g), write).then_inc(d_slot, 1)
                V.tensor_copy(of_group(slot2_i[:, 1], g), read).then_inc(d_slot, 1)
            do(V.memset(base, 0.0))
            router(1, d_xn, d_xt, d_lg, d_l, 7, ln_st[4], T, route2)
            V.tensor_tensor(rt[:, 0], logit[:, :, :], small[:, 0].unsqueeze(1).broadcast_to((P, E, T)), ALU.subtract).then_inc(d_p, 1)
            dve.wait_ge(d_p, 2)
            do(V.tensor_reduce(small[:, 2], te(rt[:, 1]), AX_X, ALU.add))
            do(V.reciprocal(small[:, 3], small[:, 2]))
            do(V.tensor_tensor(cw[:, 0], small[:, 3], small[:, 8], ALU.mult))

            def d_in_evac(e, u):
                dve.wait_ge(d_xt2, e + 1)
                V.tensor_copy(xe_t[:, u], ps[:, 0, 0:KD * CAP].rearrange("p (k n) -> p k n", k=KD)).then_inc(d_xt2e, 1)

            def d_out_evac(e, u):
                dve.wait_ge(d_yt, e + 1)
                if not isinstance(e, int) or e > 1:
                    dve.wait_ge(ye_out[u], (e - u) * 8)
                V.tensor_copy(ye[:, u].rearrange("p r n -> p (r n)"), ps[0:CR, 5]).then_inc(d_yte, 1)

            def d_step(e, u, first, last):
                if not first:
                    d_out_evac(e - 1, 1 - u)
                if not last:
                    d_in_evac(e + 1, 1 - u)
                dve.wait_ge(d_y, e + 1)
                for m in range(KD):
                    V.tensor_scalar(ye_t[:, m], ps[:, 3 + m, 0:CAP], b2s[:, bass.ds(e, 1), m], None, ALU.add).then_inc(d_ye, 1)
            d_in_evac(0, 0)
            expert_steps(dve, d_step)
            d_out_evac(E - 1, 1)
            with dve.Fori(0, T // 8) as i:
                for r in range(8):
                    t = i * 8 + r
                    dve.wait_ge(dg_in[r], i * 16 + 16)
                    V.scalar_tensor_tensor(out=at(X, t), in0=XN[:, 8 + r], scalar=col(cw[:, 0], t), in1=at(X, t),
                                           op0=ALU.mult, op1=ALU.add).then_inc(d_fin, 1)

        @block.gpsimd
        def _(pool):
            G = nc.gpsimd
            G.memset(zrow, 0.0).then_inc(zr_set, 1)
            G.memset(k_t[:, :, U - 1], 0.0).then_inc(zpad_set, 1)
            G.memset(v_pad, 0.0).then_inc(zpad_set, 1)
            G.memset(vd_pad, 0.0).then_inc(zpad_set, 1)
            pool.wait_ge(cst_in, 16)
            G.tensor_copy(mask0, cst[:, C_MT:C_MT + 2 * P]).then_inc(mask_rdy, 1)

            def q_spread(t, v):
                pool.wait_ge(q_evac, t + 1)
                for g in range(KD):
                    g_ = G.tensor_tensor(q_pad[:, v, g * HB:(g + 1) * HB], q_t[:, g].unsqueeze(1).broadcast_to((P, HB, P)),
                                         hmask.unsqueeze(2).broadcast_to((P, HB, P)), ALU.mult)
                g_.then_inc(qpad_rdy, 1)

            def a_step(s, u, norm_next, project, scores, sums, finish):
                if u == 2 and norm_next:
                    pool.wait_ge(ttr_done, (s - 1) * 8)
                    n = ((s + 2) % TB // U + (U - 1)) // U
                    src = cst[:, bass.ds(n * (2 * P) + C_MT, 2 * P)] if not isinstance(n, int) else \
                        cst[:, C_MT + n * 2 * P:C_MT + (n + 1) * 2 * P]
                    G.tensor_copy(mask0, src).then_inc(mask_rdy, 1)
                for p in range(HEADS // 2):
                    if project and p == 4:
                        q_spread(s + 1, (u + 1) % 2)
                    if scores:
                        pool.wait_ge(p_rdy, s * 8 + (p + 1))
                        both = prob[:, u % 2, 2 * p:2 * p + 2]
                        G.tensor_tensor(both[:, :, 0:P], both[:, :, 0:P], both[:, :, P:2 * P], ALU.add).then_inc(merged, 1)
            q_spread(0, 0)
            attention_steps(pool, a_step)

            pool.wait_ge(zr_out, 32)
            for t in range(T):
                if t % GT == 0:
                    pool.wait_ge(slot_rdy, 2 * (t // GT + 1))
                for k in range(2):
                    G.indirect_dma_start(rows1[:, :], bass.IndirectOffsetOnAxis(ap=slot_i[:, k, t:t + 1], axis=0),
                                         XN[:, t], None).then_inc(disp, 16)
            pool.wait_ge(disp, 32 * T)
            pool.wait_ge(out_rdy, 2)
            pool.wait_ge(y_out0, 16 * ((NT0 + 1) // 2))
            pool.wait_ge(y_out1, 16 * (NT0 // 2))
            def gather(t):
                ring, filled = (4, yg_in) if t < TB else (2, yg2_in)
                if t >= ring:
                    pool.wait_ge(yg_acc, 2 * (t - ring + 1))
                for k in range(2):
                    G.indirect_dma_start(yg[:, 2 * (t % ring) + k], None, outs1[:, :],
                                         bass.IndirectOffsetOnAxis(ap=out_i[:, k, t:t + 1], axis=0)).then_inc(filled[t % ring], 16)
            for t in range(TB + 2):
                gather(t)

            def c_step(t, n, u):
                pool.wait_ge(c_qk, t + 1)
                if not isinstance(t, int) or t > 0:
                    pool.wait_ge(c_rope, t)
                pool.sem_inc(p_seen, 1)
                sinb = at(rope_s, n).unsqueeze(1).broadcast_to((P, 2, P))
                qp = pairs(qk[:, u])
                for h in range(2):
                    G.tensor_tensor(rb4[:, h], qp[:, :, :, 1 - h], sinb, ALU.mult).then_inc(c_rbm, 1)
                if isinstance(n, int) and n == 0:
                    G.tensor_copy(ksum, qk[:, u, 1]).then_inc(c_ksum, 1)
                else:
                    pool.wait_ge(c_ksum, t)
                    G.tensor_tensor(ksum, ksum, qk[:, u, 1], ALU.add).then_inc(c_ksum, 1)
            pool.wait_ge(c_in, 96)
            for bt in range(BATCH):
                if bt == 0:
                    for n in range(TB):
                        c_step(n, n, n % 2)
                        if n + TB + 2 < T:
                            gather(n + TB + 2)
                else:
                    c_step(TB, 0, 0)
                    c_step(TB + 1, 1, 1)
                    with pool.Fori(0, TB // 2 - 1) as i:
                        for u in range(2):
                            c_step(i * 2 + (TB + 2 + u), i * 2 + (2 + u), u)
                pool.wait_ge(c_kve, 3 * (bt + 1))
                pool.wait_ge(c_qs, (bt + 1) * TB)

                def key_products(n, v):
                    if not isinstance(n, int) or n > 0:
                        pool.wait_ge(c_zd, n * 2)
                    G.tensor_tensor(zt, qs[:, bass.ds(n * 2, 2)], kmean.unsqueeze(1).broadcast_to((P, 2, D)),
                                    ALU.mult).then_inc(c_zt, 1)
                    x_ = X[:, bass.ds(n * 2, 2)]
                    G.tensor_tensor(x_, x_, gab[:, D:2 * D].unsqueeze(1).broadcast_to((P, 2, D)), ALU.add).then_inc(c_beta, 1)
                pair_steps(pool, bt, key_products)

            for t in range(T):
                if t % GT == 0:
                    pool.wait_ge(d_slot, 2 * (t // GT + 1))
                G.indirect_dma_start(rows2[:, :], bass.IndirectOffsetOnAxis(ap=slot2_i[:, 0, t:t + 1], axis=0),
                                     XN[:, t], None).then_inc(d_scat, 16)
            pool.wait_ge(d_scat, 16 * T)
            for u in range(2):
                pool.wait_ge(ye_out[u], 16 * (E // 2))
            for t in range(T):
                if t >= 8:
                    pool.wait_ge(d_fin, t - 7)
                G.indirect_dma_start(XN[:, 8 + t % 8], None, outs2[:, :],
                                     bass.IndirectOffsetOnAxis(ap=slot2_i[:, 1, t:t + 1], axis=0)).then_inc(dg_in[t % 8], 16)


def shape_constants():
    import numpy as np
    c = np.zeros((P, C_END), np.float32)
    i, j = np.arange(P)[:, None], np.arange(P)[None, :]
    c[:, C_ID:C_ID + P] = i == j
    c[:, C_TRI:C_TRI + P] = i < j
    c[:, C_ONE:C_ONE + P] = 1
    c[:, C_MEAN:C_MEAN + P] = 1 / SEQ
    c[:, C_BD:C_BD + P] = (i // HD == j // HD) / SEQ
    c[:, C_HM:C_HM + HB] = i // HD == np.arange(HB)[None, :]
    e, t = np.arange(E)[:, None], np.arange(T)[None, :]
    c[:, C_W8:C_W8 + E * T] = (E - e + 0 * t).reshape(1, -1)
    c[:, C_J:C_J + NT0] = P * np.arange(NT0)
    c[:, C_ECAP:C_ECAP + E * T] = (CAP * e + 0 * t).reshape(1, -1)
    c[:, C_TRASH:C_TRASH + T] = NS1 + t * P + i
    c[:, C_LE:C_LE + P] = i <= j
    c[:, C_EROW:C_EROW + E] = REG * np.arange(E)
    none = np.full((P, P), -BIG, np.float32)
    own, prev = np.where(j <= i, 0, none), np.where(j > i, 0, none)
    c[:, C_MN:C_MN + 2 * P] = np.concatenate([prev, own], 1)
    c[:, C_MT:C_MT + 2 * P] = np.concatenate([own, none], 1)
    c[:, C_MT + 2 * P:C_MT + 4 * P] = np.concatenate([own, prev], 1)
    inv = (np.float32(1.0) / np.float32(10000.0) ** (np.arange(0, D, 2, dtype=np.float32) / np.float32(D))).astype(np.float32)
    ang = np.arange(SEQ, dtype=np.float32)[:, None] * inv
    return c, np.cos(ang).astype(np.float32), np.sin(ang).astype(np.float32)


def kernel(**inputs):
    import numpy as np
    import concourse.bacc as bacc
    from concourse.bass_utils import run_bass_kernel_spmd

    def arr(name):
        return np.asarray(inputs[name])

    def padded(w):
        return np.concatenate([w, np.zeros((w.shape[0], P - w.shape[1]), w.dtype)], 1)
    c, cos, sin = shape_constants()
    ins = {
        "x": arr("L0_attn_x").reshape(BATCH * SEQ, D),
        "wq": arr("L0_attn_Wq").T, "wk": arr("L0_attn_Wk").T, "wv": arr("L0_attn_Wv").T, "wo": arr("L0_attn_Wo").T,
        "wr": padded(arr("L0_ffn_Wr")), "br": arr("L0_ffn_br"),
        "w1": arr("L0_ffn_W1"), "w3": arr("L0_ffn_W3"), "w2": arr("L0_ffn_W2"),
        "aq": np.concatenate([arr("L1_attn_Wq").T, arr("L1_attn_Wk").T], 1), "av": arr("L1_attn_Wv").T,
        "ab": np.concatenate([arr("L1_attn_bq"), arr("L1_attn_bk"), arr("L1_attn_bv")]),
        "gamma_beta": np.concatenate([arr("L1_attn_gamma"), arr("L1_attn_beta")]),
        "gate_w": padded(arr("L1_ffn_gate_w")), "gate_b": arr("L1_ffn_gate_b"),
        "v1": arr("L1_ffn_w1").reshape(E * D, F1), "b1": arr("L1_ffn_b1").reshape(E, K1, P).transpose(2, 0, 1),
        "v2": arr("L1_ffn_w2").reshape(E * F1, D), "b2": arr("L1_ffn_b2").reshape(E, KD, P).transpose(2, 0, 1),
        "consts": c, "cos": cos, "sin": sin,
    }
    ins = {k: np.ascontiguousarray(v) for k, v in ins.items()}
    nc = bacc.Bacc("TRN2", target_bir_lowering=False, num_devices=1)
    aps = [nc.dram_tensor(f"in_{k}", v.shape, mybir.dt.from_np(v.dtype), kind="ExternalInput").ap() for k, v in ins.items()]
    out = nc.dram_tensor("out_0", (BATCH * SEQ, D), F32, kind="ExternalOutput").ap()
    mixed_model_kernel(nc, *aps, out)
    r = run_bass_kernel_spmd(nc, [{f"in_{k}": v for k, v in ins.items()}], core_ids=[0])
    return r.results[0]["out_0"].reshape(BATCH, SEQ, D)
```
